# Optimizing a Trainium2 kernel written in Bass

```python
import numpy as np
import jax
import jax.numpy as jnp

def _softmax(x, axis=-1):
    return jax.nn.softmax(x, axis=axis)

def _gelu(x):
    return jax.nn.gelu(x, approximate=True)

def _silu(x):
    return jax.nn.silu(x)

def _sigmoid(x):
    return jax.nn.sigmoid(x)

def _layernorm(x, axis=-1, eps=1e-05):
    m = jnp.mean(x, axis=axis, keepdims=True)
    v = jnp.var(x, axis=axis, keepdims=True)
    return (x - m) / jnp.sqrt(v + eps)

def _scatter_add(tgt, idx, src, axis=0):
    return tgt.at[idx].add(src)

def _segment_sum(src, seg, n):
    return jax.ops.segment_sum(src, seg, n)
kernel_name = 'mk_hybrid_d1_jaxref_r8_8c681b'

def setup_inputs(seed: int=0):
    np.random.seed(seed)
    _w = jnp.asarray

    def _L0_attn_a_setup():
        import jax, jax.numpy as jnp
        import numpy as np
        HEADS = 4
        DIM_HEAD = 32
        EPS = 1e-05
        key = jax.random.key(seed)
        ks = jax.random.split(key, 6)
        b, n, dim = (8, 512, 128)
        hidden = HEADS * DIM_HEAD
        x = jax.random.normal(ks[0], (b, n, dim), dtype=jnp.float32)
        gamma = jnp.ones((1, 1, dim), dtype=jnp.float32)
        beta = jnp.zeros((1, 1, dim), dtype=jnp.float32)
        w_qkv = jax.random.normal(ks[1], (dim, hidden * 3), dtype=jnp.float32) / np.sqrt(dim)
        w_out = jax.random.normal(ks[2], (hidden, dim), dtype=jnp.float32) / np.sqrt(hidden)
        b_out = jnp.zeros((dim,), dtype=jnp.float32)
        return {'x': x, 'gamma': gamma, 'beta': beta, 'w_qkv': w_qkv, 'w_out': w_out, 'b_out': b_out}
    _L0_attn_a_in = _L0_attn_a_setup()

    def _L0_attn_b_setup():
        import jax, jax.numpy as jnp
        import numpy as np
        D_MODEL = 128
        IDX_HEADS = 4
        IDX_DIM = 64
        TOP_K = 32

        def _rope(x):
            B, S, D = x.shape
            half = D // 2
            inv_freq = 1.0 / 10000.0 ** (jnp.arange(half, dtype=jnp.float32) / half)
            ang = jnp.arange(S, dtype=jnp.float32)[:, None] * inv_freq[None, :]
            cos, sin = (jnp.cos(ang), jnp.sin(ang))
            x1, x2 = (x[..., :half], x[..., half:])
            return jnp.concatenate([x1 * cos - x2 * sin, x1 * sin + x2 * cos], axis=-1)
        key = jax.random.key(seed)
        ks = jax.random.split(key, 11)
        B, S, D = (2, 512, D_MODEL)
        s = 0.02
        return {'x': jax.random.normal(ks[0], (B, S, D), dtype=jnp.float32), 'w_qkv': jax.random.normal(ks[1], (3 * D, D), dtype=jnp.float32) * s, 'b_qkv': jnp.zeros((3 * D,), dtype=jnp.float32), 'w_o': jax.random.normal(ks[2], (D, D), dtype=jnp.float32) * s, 'b_o': jnp.zeros((D,), dtype=jnp.float32), 'w_iq': jax.random.normal(ks[3], (IDX_HEADS * IDX_DIM, D), dtype=jnp.float32) * s, 'b_iq': jnp.zeros((IDX_HEADS * IDX_DIM,), dtype=jnp.float32), 'w_ik': jax.random.normal(ks[4], (IDX_DIM, D), dtype=jnp.float32) * s, 'b_ik': jnp.zeros((IDX_DIM,), dtype=jnp.float32), 'w_iw': jax.random.normal(ks[5], (IDX_HEADS, D), dtype=jnp.float32) * s, 'b_iw': jnp.zeros((IDX_HEADS,), dtype=jnp.float32)}
    _L0_attn_b_in = _L0_attn_b_setup()

    def _L0_ffn_setup():
        import jax, jax.numpy as jnp
        import numpy as np
        H, E, DFF = (128, 8, 512)
        key = jax.random.key(seed)
        ks = jax.random.split(key, 7)
        s = lambda *shape: 1.0 / np.sqrt(shape[-2] if len(shape) > 1 else shape[-1])
        x = jax.random.normal(ks[0], (2, 256, H), dtype=jnp.float32)
        Wr = jax.random.normal(ks[1], (H, E), dtype=jnp.float32) * (1.0 / np.sqrt(H))
        br = jnp.zeros((E,), dtype=jnp.float32)
        W1 = jax.random.normal(ks[2], (E, H, DFF), dtype=jnp.float32) * (1.0 / np.sqrt(H))
        b1 = jnp.zeros((E, DFF), dtype=jnp.float32)
        W2 = jax.random.normal(ks[3], (E, DFF, H), dtype=jnp.float32) * (1.0 / np.sqrt(DFF))
        b2 = jnp.zeros((E, H), dtype=jnp.float32)
        return {'x': x, 'Wr': Wr, 'br': br, 'W1': W1, 'b1': b1, 'W2': W2, 'b2': b2}
    _L0_ffn_in = _L0_ffn_setup()
    _d = {'L0_attn_a_x': _L0_attn_a_in['x'], 'L0_attn_a_gamma': _L0_attn_a_in['gamma'], 'L0_attn_a_beta': _L0_attn_a_in['beta'], 'L0_attn_a_w_qkv': _L0_attn_a_in['w_qkv'], 'L0_attn_a_w_out': _L0_attn_a_in['w_out'], 'L0_attn_a_b_out': _L0_attn_a_in['b_out'], 'L0_attn_b_w_qkv': _L0_attn_b_in['w_qkv'], 'L0_attn_b_b_qkv': _L0_attn_b_in['b_qkv'], 'L0_attn_b_w_o': _L0_attn_b_in['w_o'], 'L0_attn_b_b_o': _L0_attn_b_in['b_o'], 'L0_attn_b_w_iq': _L0_attn_b_in['w_iq'], 'L0_attn_b_b_iq': _L0_attn_b_in['b_iq'], 'L0_attn_b_w_ik': _L0_attn_b_in['w_ik'], 'L0_attn_b_b_ik': _L0_attn_b_in['b_ik'], 'L0_attn_b_w_iw': _L0_attn_b_in['w_iw'], 'L0_attn_b_b_iw': _L0_attn_b_in['b_iw'], 'L0_ffn_Wr': _L0_ffn_in['Wr'], 'L0_ffn_br': _L0_ffn_in['br'], 'L0_ffn_W1': _L0_ffn_in['W1'], 'L0_ffn_b1': _L0_ffn_in['b1'], 'L0_ffn_W2': _L0_ffn_in['W2'], 'L0_ffn_b2': _L0_ffn_in['b2']}
    _x0 = _d['L0_attn_a_x']
    _d['L0_attn_a_x'] = jax.random.normal(jax.random.fold_in(jax.random.key(seed), 1), (16, 256, 128), dtype=_x0.dtype)
    del _x0
    return _d

def reference(L0_attn_a_x, L0_attn_a_gamma, L0_attn_a_beta, L0_attn_a_w_qkv, L0_attn_a_w_out, L0_attn_a_b_out, L0_attn_b_w_qkv, L0_attn_b_b_qkv, L0_attn_b_w_o, L0_attn_b_b_o, L0_attn_b_w_iq, L0_attn_b_b_iq, L0_attn_b_w_ik, L0_attn_b_b_ik, L0_attn_b_w_iw, L0_attn_b_b_iw, L0_ffn_Wr, L0_ffn_br, L0_ffn_W1, L0_ffn_b1, L0_ffn_W2, L0_ffn_b2):

    def _L0_attn_a_ref(x, gamma, beta, w_qkv, w_out, b_out):
        import jax, jax.numpy as jnp
        import numpy as np
        HEADS = 4
        DIM_HEAD = 32
        EPS = 1e-05
        b, n, dim = x.shape
        mean = jnp.mean(x, axis=2, keepdims=True)
        var = jnp.var(x, axis=2, keepdims=True)
        xn = (x - mean) / jnp.sqrt(var + EPS) * gamma + beta
        qkv = jnp.einsum('bnc,ck->bnk', xn, w_qkv)
        q, k, v = jnp.split(qkv, 3, axis=2)

        def to_heads(t):
            return t.reshape(b, n, HEADS, DIM_HEAD)
        q, k, v = (to_heads(q), to_heads(k), to_heads(v))
        q = q * DIM_HEAD ** (-0.5)
        k = jax.nn.softmax(k, axis=1)
        context = jnp.einsum('bnhd,bnhe->bhde', k, v)
        out = jnp.einsum('bhde,bnhd->bnhe', context, q)
        out = out.reshape(b, n, HEADS * DIM_HEAD)
        out = jnp.einsum('bnk,kc->bnc', out, w_out) + b_out
        return out + x

    def _L0_attn_b_ref(x, w_qkv, b_qkv, w_o, b_o, w_iq, b_iq, w_ik, b_ik, w_iw, b_iw):
        import jax, jax.numpy as jnp
        import numpy as np
        D_MODEL = 128
        IDX_HEADS = 4
        IDX_DIM = 64
        TOP_K = 32

        def _rope(x):
            B, S, D = x.shape
            half = D // 2
            inv_freq = 1.0 / 10000.0 ** (jnp.arange(half, dtype=jnp.float32) / half)
            ang = jnp.arange(S, dtype=jnp.float32)[:, None] * inv_freq[None, :]
            cos, sin = (jnp.cos(ang), jnp.sin(ang))
            x1, x2 = (x[..., :half], x[..., half:])
            return jnp.concatenate([x1 * cos - x2 * sin, x1 * sin + x2 * cos], axis=-1)
        B, S, D = x.shape
        qkv = x @ w_qkv.T + b_qkv
        Q, K, V = jnp.split(qkv, 3, axis=-1)
        Q, K = (_rope(Q), _rope(K))
        iq = (x @ w_iq.T + b_iq).reshape(B, S, IDX_HEADS, IDX_DIM)
        ik = x @ w_ik.T + b_ik
        iw = x @ w_iw.T + b_iw
        head_scores = jax.nn.relu(jnp.einsum('bqhd,bkd->bhqk', iq, ik))
        index_scores = jnp.einsum('bhqk,bqh->bqk', head_scores, iw)
        k = min(TOP_K, S)
        _, top_idx = jax.lax.top_k(index_scores, k)
        mask = jnp.zeros((B, S, S), dtype=bool)
        mask = mask.at[jnp.arange(B)[:, None, None], jnp.arange(S)[None, :, None], top_idx].set(True)
        attn_bias = jnp.where(mask, 0.0, -jnp.inf)
        scale = 1.0 / np.sqrt(D).astype(np.float32)
        logits = jnp.einsum('bqd,bkd->bqk', Q, K) * scale + attn_bias
        attn = jax.nn.softmax(logits, axis=-1)
        attn_out = jnp.einsum('bqk,bkd->bqd', attn, V)
        return attn_out @ w_o.T + b_o

    def _L0_ffn_ref(x, Wr, br, W1, b1, W2, b2):
        import jax, jax.numpy as jnp
        import numpy as np
        H, E, DFF = (128, 8, 512)
        B, S, Hd = x.shape
        n_exp = W1.shape[0]
        xt = x.reshape(-1, Hd)
        logits = xt @ Wr + br
        probs = jax.nn.softmax(logits, axis=-1)
        gate = jnp.max(probs, axis=-1)
        idx = jnp.argmax(probs, axis=-1)
        h1 = jnp.maximum(jnp.einsum('th,ehf->etf', xt, W1) + b1[:, None, :], 0.0)
        ye = jnp.einsum('etf,efh->eth', h1, W2) + b2[:, None, :]
        onehot = jax.nn.one_hot(idx, n_exp, dtype=xt.dtype)
        y = jnp.einsum('te,eth->th', onehot, ye) * gate[:, None]
        return y.reshape(B, S, Hd)
    x = L0_attn_a_x
    x = x + _L0_attn_a_ref(_layernorm(x, axis=-1), L0_attn_a_gamma, L0_attn_a_beta, L0_attn_a_w_qkv, L0_attn_a_w_out, L0_attn_a_b_out)
    x = x + _L0_ffn_ref(_layernorm(x, axis=-1), L0_ffn_Wr, L0_ffn_br, L0_ffn_W1, L0_ffn_b1, L0_ffn_W2, L0_ffn_b2)
    x = x + _L0_attn_b_ref(_layernorm(x, axis=-1), L0_attn_b_w_qkv, L0_attn_b_b_qkv, L0_attn_b_w_o, L0_attn_b_b_o, L0_attn_b_w_iq, L0_attn_b_b_iq, L0_attn_b_w_ik, L0_attn_b_b_ik, L0_attn_b_w_iw, L0_attn_b_b_iw)
    x = x + _L0_ffn_ref(_layernorm(x, axis=-1), L0_ffn_Wr, L0_ffn_br, L0_ffn_W1, L0_ffn_b1, L0_ffn_W2, L0_ffn_b2)
    return x

_drawn_inputs = setup_inputs


def setup_inputs(seed=0):
    import zlib

    import numpy as np

    out = dict(_drawn_inputs(seed))
    spreads = {'L0_attn_a_gamma': (1.0, 0.2),
     'L0_attn_a_beta': (0.0, 0.1),
     'L0_attn_a_b_out': (0.0, 0.1),
     'L0_attn_b_b_qkv': (0.0, 0.541),
     'L0_attn_b_b_o': (0.0, 0.1),
     'L0_attn_b_b_iq': (0.0, 0.8),
     'L0_attn_b_b_ik': (0.0, 0.8),
     'L0_attn_b_b_iw': (0.0, 0.8),
     'L0_ffn_br': (0.0, 0.1),
     'L0_ffn_b1': (0.0, 0.284),
     'L0_ffn_b2': (0.0, 0.1)}
    factors = {'L0_attn_b_w_qkv': 6.513,
     'L0_attn_b_w_o': 3.758,
     'L0_attn_b_w_iq': 5.925,
     'L0_attn_b_w_ik': 6.482,
     'L0_attn_b_w_iw': 6.57}
    for name, (base, spread) in spreads.items():
        noise = np.random.default_rng([zlib.crc32(name.encode()), seed]).standard_normal(out[name].shape)
        drawn = base * np.exp(spread * noise) if base else spread * noise
        out[name] = jnp.asarray(drawn.astype(out[name].dtype))
    for name, factor in factors.items():
        out[name] = (out[name] * factor).astype(out[name].dtype)
    return out
```

```python
from contextlib import ExitStack

import numpy as np
import concourse.bass as bass
from concourse import mybir

F32 = mybir.dt.float32
BF16 = mybir.dt.bfloat16
I32 = mybir.dt.int32
U32 = mybir.dt.uint32
ALU = mybir.AluOpType
ACT = mybir.ActivationFunctionType
AX = mybir.AxisListType

P = 128
B, S, D = 16, 256, 128
C = S // P
T = B * C
TOKENS = B * S
HEADS, DIM_HEAD = 4, 32
IDX_HEADS, IDX_DIM, TOP_K = 4, 64, 32
E, F = 8, 512
FC = F // P
NT = T + E - 1
EPS = 1e-5
ROW = 2 * D + E
NEG = -3.0e38
MAGIC = 1.5 * 2.0**23
W1_AT, W2_AT, B1_AT, B2_AT = 0, F, 2 * F, 2 * F + FC
W_LEN = 2 * F + FC + D
CONSTS = [("ident", P), ("blocks", P), ("tri", P), ("ones", P), ("cos", S), ("sin", S), ("slot1", P),
          ("tile", NT), ("down", E), ("keep", E * T), ("starts", T), ("col", T), ("part1", 1)]
CONST_AT, CONST_LEN = {}, 0
for _name, _len in CONSTS:
    CONST_AT[_name] = (CONST_LEN, CONST_LEN + _len)
    CONST_LEN += _len


def constant_table():
    half = D // 2
    inv = (1.0 / 10000.0 ** (np.arange(half, dtype=np.float32) / np.float32(half))).astype(np.float32)
    ang = (np.arange(S, dtype=np.float32)[:, None] * inv[None, :]).astype(np.float32)
    cos, sin = np.cos(ang).T, np.sin(ang).T
    rows = np.arange(P)
    t = {
        "ident": np.eye(P),
        "blocks": rows[:, None] // DIM_HEAD == rows[None, :] // DIM_HEAD,
        "tri": rows[:, None] < rows[None, :],
        "ones": np.ones((P, P)),
        "cos": np.concatenate([cos, cos]),
        "sin": np.concatenate([-sin, sin]),
        "slot1": np.broadcast_to(rows + 1, (P, P)),
        "tile": np.broadcast_to(np.arange(NT), (P, NT)),
        "down": np.broadcast_to(E - np.arange(E), (P, E)),
        "keep": np.broadcast_to(np.arange(E * T) % T != 0, (P, E * T)),
        "starts": np.broadcast_to(np.arange(T) * P, (P, T)),
        "col": np.broadcast_to(np.arange(T), (P, T)),
        "part1": rows[:, None] + 1,
    }
    return np.concatenate([np.asarray(t[n], np.float32).reshape(P, -1) for n, _ in CONSTS], axis=1)


class Step:

    def __init__(self, base, unroll=1, turn=0):
        self.base, self.unroll, self.turn = base, unroll, turn

    def item(self, lag):
        return self.base - lag + self.unroll * self.turn

    def slot(self, lag, ring):
        return (self.base - lag) % ring

    def lap(self, lag, ring):
        return (self.base - lag) // ring + self.unroll // ring * self.turn

    def on(self, lag, items):
        return not isinstance(self.turn, int) or 0 <= self.base - lag < items


def steps(eng, items, lag, head, unroll, ahead=0):
    turns = (items - ahead - head) // unroll
    for s in range(head):
        yield Step(s)
    with eng.Fori(0, turns) as turn:
        for k in range(unroll):
            yield Step(head + k, unroll, turn)
    for s in range(head + turns * unroll, items + lag):
        yield Step(s)


def after(eng, sem, count):
    if not isinstance(count, int) or count > 0:
        eng.wait_ge(sem, count)


def alone(eng, sem, count, passed):
    if not isinstance(count, int) or count > 0:
        eng.wait_ge(sem, count)
        eng.sem_inc(passed, 1)


def build(nc, x, w_attn, w_idx, w_experts, b1_cols, b2, w_router, cols, b_out, b_o, b_iw, b_r, consts, out):
    with ExitStack() as ctx:
        def sb(name, shape, dt=F32):
            return ctx.enter_context(nc.sbuf_tensor(name, shape, dt))

        def sem(name):
            return ctx.enter_context(nc.semaphore(name))

        def sems(name, n):
            return [sem(f"{name}{i}") for i in range(n)]

        bank = [ctx.enter_context(nc.psum_tensor(f"bank{i}", [P, 512], F32)) for i in range(8)]

        rows_dram = [nc.dram_tensor(f"rows{i}", [TOKENS, ROW], F32, kind="Internal").ap() for i in range(2)]
        x2_dram = nc.dram_tensor("x2", [TOKENS, D], F32, kind="Internal").ap()

        X = sb("X", [P, T, D])
        cst = sb("cst", [P, CONST_LEN])
        WE = sb("WE", [P, E, W_LEN])
        WA = sb("WA", [P, 4 * D])
        WR = sb("WR", [P, E])
        COL = sb("COL", [P, 10])
        WB = sb("WB", [P, 10 * D])
        WVO = sb("WVO", [P, D])
        bout_bc = sb("bout_bc", [P, D])
        bo_bc = sb("bo_bc", [P, D])
        bv_rep = sb("bv_rep", [P, P])
        rowc = sb("rowc", [1, IDX_HEADS + E])
        mhalf = sb("mhalf", [P, T])
        eps = sb("eps", [P, C])
        xf = [sb(f"xf{i}", [P, C, D]) for i in range(2)]
        xfT = [sb(f"xfT{i}", [P, S]) for i in range(2)]
        stat3 = sb("stat3", [P, C, 6])
        mv3 = [sb(f"mv3_{i}", [P, C, 2]) for i in range(2)]
        vpe3 = sb("vpe3", [P, C])
        rs3 = [sb(f"rs3_{i}", [P, C]) for i in range(2)]
        logits = sb("logits", [P, T, E])

        def const(name):
            a, b = CONST_AT[name]
            return cst[:, a:b]

        ident, ones = const("ident"), const("ones")

        mv1 = sb("mv1", [P, T, 2])
        stat1 = sb("stat1", [P, T, 6])
        ln1 = sb("ln1", [P, 8, T])
        R0, R1, XS, XO, VE, VV, NM = range(7)
        xa = [sb(f"xa{i}", [P, C, D]) for i in range(2)]
        xaT = [sb(f"xaT{i}", [P, S]) for i in range(2)]
        kneg = [sb(f"kneg{i}", [P, 1]) for i in range(2)]
        ekT = [sb(f"ekT{i}", [P, S]) for i in range(2)]
        esum = [sb(f"esum{i}", [P, 1]) for i in range(2)]
        einv = [sb(f"einv{i}", [P, 1]) for i in range(2)]
        ek = [sb(f"ek{i}", [P, C, D]) for i in range(2)]
        va = [sb(f"va{i}", [P, C, D]) for i in range(2)]
        cm = [sb(f"cm{i}", [P, D]) for i in range(2)]
        Gs = [sb(f"Gs{i}", [P, D]) for i in range(2)]
        Hs = [sb(f"Hs{i}", [P, D]) for i in range(2)]
        xres = [sb(f"xres{i}", [P, C, D]) for i in range(2)]

        r_a = sb("r_a", [P, T, E])
        r_b = sb("r_b", [P, T, E])
        oh = sb("oh", [P, E, T])
        incl = sb("incl", [P, E, T])
        rr = sb("rr", [P, E, T])
        r_m = sb("r_m", [P, 8, T])
        rtot = sb("rtot", [P, E])
        nt = sb("nt", [P, 3, E])
        oneh_slot = sb("oneh_slot", [P, T, P], BF16)
        oneh_tile = sb("oneh_tile", [P, T, 2, NT], BF16)
        colbf = sb("colbf", [P, T], BF16)
        idxf = sb("idxf", [P, 3, NT])
        gidx = sb("gidx", [P, NT], U32)
        sidx = sb("sidx", [P, NT], U32)
        tef = sb("tef", [1, NT, E])
        tes = sb("tes", [1, NT])
        te = sb("te", [1, NT], I32)

        G_RING, Y_RING = 6, 3
        xg = [sb(f"xg{i}", [P, ROW]) for i in range(G_RING)]
        gcur = [sb(f"gcur{i}", [P, 1], U32) for i in range(G_RING)]
        scur = [sb(f"scur{i}", [P, 1], U32) for i in range(Y_RING)]
        xgT = [sb(f"xgT{i}", [P, P]) for i in range(2)]
        w1 = [sb(f"w1_{i}", [P, F]) for i in range(2)]
        w2 = [sb(f"w2_{i}", [P, W_LEN - F]) for i in range(2)]
        hT = [sb(f"hT{i}", [P, FC, P]) for i in range(2)]
        lneg = [sb(f"lneg{i}", [P, 1]) for i in range(2)]
        lexp = [sb(f"lexp{i}", [P, E]) for i in range(2)]
        lsum = [sb(f"lsum{i}", [P, 1]) for i in range(2)]
        gate = sb("gate", [P, 1])
        yb = sb("yb", [P, D])
        yo = [sb(f"yo{i}", [P, D]) for i in range(Y_RING)]

        stat2 = sb("stat2", [P, C, 6])
        mv2 = [sb(f"mv2_{i}", [P, C, 2]) for i in range(2)]
        vpe2 = sb("vpe2", [P, C])
        rs2 = [sb(f"rs2_{i}", [P, C]) for i in range(2)]
        xb = [sb(f"xb{i}", [P, C, D]) for i in range(2)]
        xbT = [sb(f"xbT{i}", [P, S]) for i in range(2)]
        qk = [sb(f"qk{i}", [P, 4, S]) for i in range(2)]
        rp = sb("rp", [P, 2, S])
        qr = [sb(f"qr{i}", [P, 2, S]) for i in range(2)]
        iq = [sb(f"iq{i}", [P, 2, S]) for i in range(2)]
        ik = [sb(f"ik{i}", [P, S]) for i in range(2)]
        vb = [sb(f"vb{i}", [P, C, D]) for i in range(2)]
        iw = [sb(f"iw{i}", [P, C, IDX_HEADS]) for i in range(2)]
        rel = [sb(f"rel{i}", [P, C, IDX_HEADS, S]) for i in range(2)]
        part = [sb(f"part{i}", [P, C, 2, S]) for i in range(2)]
        half_sum = [sb(f"half_sum{i}", [P, C, S]) for i in range(2)]
        wk = sb("wk", [P, C, S])
        m8 = sb("m8", [P, C, 8])
        pen = sb("pen", [P, C, S])
        lg = [sb(f"lg{i}", [P, C, S]) for i in range(2)]
        lmax = sb("lmax", [P, C])
        lnb = [sb(f"lnb{i}", [P, C]) for i in range(2)]
        pr = lg
        psm = [sb(f"psm{i}", [P, C]) for i in range(2)]
        pinv = sb("pinv", [P, C])
        prT = [sb(f"prT{i}", [P, C, S]) for i in range(2)]
        xbias = [sb(f"xbias{i}", [P, C, D]) for i in range(2)]
        x3 = [sb(f"x3_{i}", [P, C, D]) for i in range(2)]

        ld_c, ld_w, ld_x = sem("ld_c"), sem("ld_w"), sems("ld_x", 4)
        passed = {k: sem(f"passed_{k}") for k in ("dve", "pool", "sp")}
        ld_wb, ld_we = sem("ld_wb"), sem("ld_we")
        a_stat, a_pool, a_coef = sem("a_stat"), sem("a_pool"), sem("a_coef")
        a_xa, a_T, a_xaT, a_K, a_V = sem("a_xa"), sem("a_T"), sem("a_xaT"), sem("a_K"), sem("a_V")
        a_kneg, a_exp, a_va, a_ekT, a_ek = sem("a_kneg"), sem("a_exp"), sem("a_va"), sem("a_ekT"), sem("a_ek")
        a_ctx, a_cm, a_einv, a_G, a_Gs = sem("a_ctx"), sem("a_cm"), sem("a_einv"), sem("a_G"), sem("a_Gs")
        a_H, a_Hs, a_out, a_xres, a_pt = sem("a_H"), sem("a_Hs"), sem("a_out"), sem("a_xres"), sem("a_pt")
        tails = []
        for n in "ab":
            tails.append({k: sem(f"{n}t_{k}") for k in
                          ("x", "st", "mv", "ve", "rs", "xf", "T", "xfT", "R", "lg")} | {
                          "store": sems(f"{n}t_store", 2), "rest": sem(f"{n}t_rest")})
        rt = {k: sem(f"r_{k}") for k in ("v", "sub", "exp", "rtot", "tot", "slots", "inv", "idx", "te")}
        ffns = [{k: sem(f"f{n}_{k}") for k in
                 ("gc", "sc", "T", "xgT", "w1", "w2", "H", "hA", "hV", "Y", "neg", "exp", "v", "y")} | {
                 "g": sems(f"f{n}_g", G_RING), "s": sems(f"f{n}_s", Y_RING)} for n in range(2)]
        b_ = {k: sem(f"b_{k}") for k in
              ("init", "bo", "wvo", "bvr", "x", "st", "mv", "ve", "rs", "xb", "T", "xbT", "pj", "pje", "rp", "qr", "iwe",
               "idx", "rel", "prt", "hs", "s1", "wk", "v", "S", "ttr", "lnb", "exp", "PT", "prT", "PV", "pinv",
               "xbias", "fin")}

        def xrows(dram, b, lo, hi):
            return dram[bass.ds(b * S, S), lo:hi].rearrange("(c p) d -> p c d", p=P)

        def tiles(b):
            return bass.ds(b * C, C)

        block = ctx.enter_context(nc.Block())

        @block.sync
        def _(sp):
            sp.dma_start(cst[:, :], consts).then_inc(ld_c, 16)
            per = T // 4
            for g in range(4):
                sp.dma_start(X[:, g * per:(g + 1) * per, :],
                             x[g * per * P:(g + 1) * per * P, :].rearrange("(c p) d -> p c d", p=P)).then_inc(ld_x[g], 16)
                if g == 0:
                    sp.dma_start(WA[:, :], w_attn).then_inc(ld_w, 16)
                    sp.dma_start(COL[:, :], cols).then_inc(ld_w, 16)
                    sp.dma_start(bout_bc[:, :], b_out.partition_broadcast(P)).then_inc(ld_w, 16)
                    sp.dma_start(WR[:, :], w_router).then_inc(ld_w, 16)
                    sp.dma_start(rowc[:, 0:IDX_HEADS], b_iw).then_inc(ld_w, 16)
                    sp.dma_start(rowc[:, IDX_HEADS:], b_r).then_inc(ld_w, 16)
            sp.dma_start(WB[:, :], w_idx).then_inc(ld_wb, 16)
            sp.dma_start(bo_bc[:, :], b_o.partition_broadcast(P)).then_inc(ld_wb, 16)
            sp.dma_start(WE[:, :, W1_AT:B1_AT], w_experts).then_inc(ld_we, 16)
            sp.dma_start(WE[:, :, B1_AT:B2_AT], b1_cols).then_inc(ld_we, 16)
            sp.dma_start(WE[:, :, B2_AT:W_LEN], b2.partition_broadcast(P)).then_inc(ld_we, 16)

            def store_rows(n, st, lag, x_of):
                t, dram = tails[n], rows_dram[n]
                b, r = st.item(lag), st.slot(lag, 2)
                sp.wait_ge(t["xf"], b + 1)
                sp.dma_start(xrows(dram, b, 0, D), xf[r][:, :, :]).then_inc(t["store"][r], 16)
                sp.wait_ge(t["x"], b + 1)
                sp.dma_start(xrows(dram, b, D, 2 * D), x_of(b, r)).then_inc(t["store"][r], 16)
                sp.wait_ge(t["lg"], b + 1)
                sp.dma_start(xrows(dram, b, 2 * D, ROW), logits[:, tiles(b), :]).then_inc(t["rest"], 16)

            for st in steps(sp, B, 0, 4, 2):
                store_rows(0, st, 0, lambda b, r: X[:, tiles(b), :])
            for i in range(Y_RING):
                sp.wait_ge(ffns[0]["s"][i], 16 * len(range(i, NT, Y_RING)))
            for st in steps(sp, B, 5, 6, 2):
                if st.on(0, B):
                    sp.dma_start(X[:, tiles(st.item(0)), :], xrows(x2_dram, st.item(0), 0, D)).then_inc(b_["x"], 16)
                    alone(sp, b_["x"], 16 * (st.item(0) + 1), passed["sp"])
                if st.on(5, B):
                    store_rows(1, st, 5, lambda b, r: x3[r][:, :, :])
            for i in range(Y_RING):
                sp.wait_ge(ffns[1]["s"][i], 16 * len(range(i, NT, Y_RING)))

        @block.gpsimd
        def _(pool):
            pool.memset(eps[:, :], EPS)
            pool.memset(mhalf[:, :], -0.5).then_inc(a_pool, 1)
            n = 1

            def link(ins):
                nonlocal n
                n += 1
                ins.then_inc(a_pool, 1)
                pool.wait_ge(a_pool, n)

            pool.wait_ge(a_pool, 1)
            per = T // 4
            for g in range(4):
                cs = slice(g * per, (g + 1) * per)
                pool.wait_ge(a_stat, 2 * (g + 1))
                mean, var = mv1[:, cs, 0], mv1[:, cs, 1]
                v = lambda k: ln1[:, k, cs]
                link(pool.tensor_scalar(v(VE), var, EPS, None, ALU.add))
                link(pool.tensor_tensor(v(R0), v(VE), mhalf[:, cs], ALU.pow))
                link(pool.tensor_tensor(v(VV), v(R0), v(R0), ALU.mult))
                link(pool.tensor_tensor(v(VV), v(VV), var, ALU.mult))
                link(pool.tensor_scalar(v(VE), v(VV), EPS, None, ALU.add))
                link(pool.tensor_tensor(v(VV), v(VE), mhalf[:, cs], ALU.pow))
                link(pool.tensor_tensor(v(R1), v(R0), v(VV), ALU.mult))
                link(pool.tensor_scalar(v(XS), v(R0), 1.0, None, ALU.add))
                link(pool.tensor_tensor(v(NM), mean, v(R0), ALU.mult))
                link(pool.tensor_scalar(v(XO), v(NM), -1.0, None, ALU.mult))
                pool.sem_inc(a_coef, 1)

            def rstd(t, vpe, mv, rs, b, r):
                pool.wait_ge(t["mv"], b + 1)
                pool.tensor_tensor(vpe[:, :], mv[r][:, :, 1], eps[:, :], ALU.add).then_inc(t["ve"], 1)
                pool.wait_ge(t["ve"], b + 1)
                after(pool, t["xf"] if "xf" in t else t["xb"], b - 1)
                pool.tensor_tensor(rs[r][:, :], vpe[:, :], mhalf[:, 0:C], ALU.pow).then_inc(t["rs"], 1)

            pool.wait_ge(ld_w, 96)
            for st in steps(pool, B, 2, 4, 2):
                if st.on(0, B):
                    b, r = st.item(0), st.slot(0, 2)
                    pool.wait_ge(a_pt, b + 1)
                    pool.tensor_tensor(xres[r][:, :, :], xres[r][:, :, :],
                                       bout_bc[:, :].unsqueeze(1).to_broadcast([P, C, D]), ALU.add).then_inc(a_xres, 1)
                if st.on(1, B):
                    rstd(tails[0], vpe3, mv3, rs3, st.item(1), st.slot(1, 2))

            def experts_pool(n):
                f = ffns[n]
                dest = x2_dram if n == 0 else out
                for i in range(2):
                    pool.wait_ge(tails[n]["store"][i], 32 * (B // 2))
                pool.wait_ge(tails[n]["rest"], 16 * B)
                pool.wait_ge(rt["idx"], 2 * n + 2)
                for st in steps(pool, NT, 5, 9, 6):
                    if st.on(5, NT):
                        j, r = st.item(5), st.slot(5, Y_RING)
                        pool.wait_ge(f["y"], j + 1)
                        after(pool, f["s"][r], 16 * st.lap(5, Y_RING))
                        pool.tensor_copy(scur[r][:, :], sidx[:, bass.ds(j, 1)]).then_inc(f["sc"], 1)
                        alone(pool, f["sc"], j + 1, passed["pool"])
                        pool.indirect_dma_start(dest, bass.IndirectOffsetOnAxis(ap=scur[r][:, :], axis=0), yo[r][:, :],
                                                None, bounds_check=TOKENS - 1, oob_is_err=False).then_inc(f["s"][r], 16)
                    if st.on(0, NT):
                        j, r = st.item(0), st.slot(0, G_RING)
                        after(pool, f["y"], j + 1 - G_RING)
                        pool.tensor_copy(gcur[r][:, :], gidx[:, bass.ds(j, 1)]).then_inc(f["gc"], 1)
                        alone(pool, f["gc"], j + 1, passed["pool"])
                        pool.indirect_dma_start(xg[r][:, :], None, rows_dram[n],
                                                bass.IndirectOffsetOnAxis(ap=gcur[r][:, :], axis=0)).then_inc(f["g"][r], 16)

            experts_pool(0)

            def add_bias(b, r):
                pool.wait_ge(b_["x"], 16 * (b + 1))
                after(pool, tails[1]["x"], b - 1)
                pool.tensor_tensor(xbias[r][:, :, :], X[:, tiles(b), :],
                                   bo_bc[:, :].unsqueeze(1).to_broadcast([P, C, D]), ALU.add).then_inc(b_["xbias"], 1)

            pool.wait_ge(b_["bo"], 1)
            rstd(b_, vpe2, mv2, rs2, 0, 0)
            for st in steps(pool, B, 3, 6, 2, ahead=1):
                if st.on(-1, B):
                    rstd(b_, vpe2, mv2, rs2, st.item(-1), st.slot(-1, 2))
                if st.on(0, B):
                    b, r = st.item(0), st.slot(0, 2)
                    add_bias(b, r)
                    for i in range(2):
                        pool.wait_ge(b_["pje"], 8 * b + 2 * i + 2)
                        pool.tensor_tensor(rp[:, 0, :], qk[r][:, 2 * i, :], const("cos"), ALU.mult).then_inc(b_["rp"], 1)
                        pool.tensor_tensor(rp[:, 1, :], qk[r][:, 2 * i + 1, :], const("sin"), ALU.mult).then_inc(b_["rp"], 1)
                        pool.wait_ge(b_["rp"], 4 * b + 2 * i + 2)
                        if i == 0:
                            after(pool, b_["S"], C * (b - 1))
                        pool.tensor_tensor(qr[r][:, i, :], rp[:, 0, :], rp[:, 1, :], ALU.add).then_inc(b_["qr"], 1)
                        pool.wait_ge(b_["qr"], 2 * b + i + 1)
                    for c in range(C):
                        pool.wait_ge(b_["prt"], C * b + c + 1)
                        after(pool, b_["s1"], C * (b - 1))
                        pool.tensor_tensor(half_sum[r][:, c, :], part[r][:, c, 0, :], part[r][:, c, 1, :],
                                           ALU.add).then_inc(b_["hs"], 1)
                if st.on(2, B):
                    rstd(tails[1], vpe3, mv3, rs3, st.item(2), st.slot(2, 2))
            experts_pool(1)

        @block.tensor
        def _(pe):
            def router(n, b, r, where):
                t = tails[n]
                pe.wait_ge(t["xfT"], b + 1)
                after(pe, t["lg"], b)
                for c in range(C):
                    pe.matmul(where[:, c * E:(c + 1) * E], ones[0:1, :], rowc[:, IDX_HEADS:], start=True, stop=False)
                    mm = pe.matmul(where[:, c * E:(c + 1) * E], xfT[r][:, c * P:(c + 1) * P], WR[:, :],
                                   start=False, stop=True)
                mm.then_inc(t["R"], 1)

            def turn_xf(n, b, r, where):
                t = tails[n]
                pe.wait_ge(t["xf"], b + 1)
                after(pe, t["xfT"], b)
                after(pe, t["lg"], b)
                for c in range(C):
                    mm = pe.transpose(where[:, c * P:(c + 1) * P], xf[r][:, c, :], ident)
                mm.then_inc(t["T"], 1)

            pe.wait_ge(ld_c, 16)
            pe.wait_ge(ld_w, 96)
            for st in steps(pe, B, 2, 4, 2, ahead=1):
                b, r = st.item(0), st.slot(0, 2)
                p, q = st.item(1), st.slot(1, 2)
                if st.on(0, B):
                    pe.wait_ge(a_xa, b + 1)
                    after(pe, a_xaT, b)
                    for c in range(C):
                        mm = pe.transpose(bank[2][:, c * P:(c + 1) * P], xa[r][:, c, :], ident)
                    mm.then_inc(a_T, 1)
                if st.on(1, B):
                    pe.wait_ge(a_exp, p + 1)
                    after(pe, a_ek, p)
                    for c in range(C):
                        mm = pe.transpose(bank[5][:, c * P:(c + 1) * P], ekT[q][:, c * P:(c + 1) * P], ident)
                    mm.then_inc(a_ekT, 1)
                if st.on(0, B):
                    pe.wait_ge(a_xaT, b + 1)
                    after(pe, a_exp, b)
                    pe.matmul(bank[0][:, 0:S], WA[:, D:2 * D], xaT[r][:, :], start=True, stop=True).then_inc(a_K, 1)
                if st.on(1, B):
                    pe.wait_ge(a_ek, p + 1)
                    pe.wait_ge(a_va, p + 1)
                    after(pe, a_Hs, p)
                    for c in range(C):
                        mm = pe.matmul(bank[3][:, 0:D], va[q][:, c, :], ek[q][:, c, :], start=(c == 0), stop=(c == C - 1))
                    mm.then_inc(a_ctx, 1)
                if st.on(0, B):
                    after(pe, a_va, b)
                    for c in range(C):
                        mm = pe.matmul(bank[1][:, c * D:(c + 1) * D], xaT[r][:, c * P:(c + 1) * P],
                                       WA[:, 2 * D:3 * D], start=True, stop=True)
                    mm.then_inc(a_V, 1)
                if st.on(1, B):
                    pe.wait_ge(a_cm, p + 1)
                    pe.matmul(bank[3][:, D:2 * D], cm[q][:, :], WA[:, 3 * D:4 * D], start=True, stop=True).then_inc(a_G, 1)
                    pe.wait_ge(a_Gs, p + 1)
                    pe.matmul(bank[3][:, 2 * D:3 * D], WA[:, 0:D], Gs[q][:, :], start=True, stop=True).then_inc(a_H, 1)
                if st.on(2, B):
                    turn_xf(0, st.item(2), st.slot(2, 2), bank[6])
                if st.on(1, B):
                    pe.wait_ge(a_Hs, p + 1)
                    after(pe, tails[0]["x"], p)
                    for c in range(C):
                        mm = pe.matmul(bank[4][:, c * D:(c + 1) * D], xaT[q][:, c * P:(c + 1) * P], Hs[q][:, :],
                                       start=True, stop=True)
                    mm.then_inc(a_out, 1)
                if st.on(2, B):
                    router(0, st.item(2), st.slot(2, 2), bank[7])

            def route_tensor(n):
                pe.wait_ge(rt["rtot"], n + 1)
                pe.matmul(bank[0][:, 0:E], const("tri"), rtot[:, :], start=True, stop=True)
                pe.matmul(bank[0][:, E:2 * E], ones, rtot[:, :], start=True, stop=True).then_inc(rt["tot"], 1)
                for c in range(T):
                    if c % 8 == 0:
                        pe.wait_ge(rt["slots"], 5 * n + c // 8 + 2)
                    mm = pe.matmul(bank[1][:, 0:2 * NT], oneh_slot[:, c, :],
                                   oneh_tile[:, c, :, :].rearrange("p a b -> p (a b)"), start=(c == 0), stop=(c == T - 1))
                mm.then_inc(rt["inv"], 1)

            def experts_tensor(n):
                f = ffns[n]
                pe.wait_ge(rt["idx"], 2 * n + 2)
                for st in steps(pe, NT, 2, 9, 6):
                    if st.on(0, NT):
                        j, r, g = st.item(0), st.slot(0, 2), st.slot(0, G_RING)
                        pe.wait_ge(f["g"][g], 16 * (st.lap(0, G_RING) + 1))
                        after(pe, f["xgT"], j - 1)
                        pe.transpose(bank[6 + r][:, 0:P], xg[g][:, 0:D], ident).then_inc(f["T"], 1)
                    if st.on(1, NT):
                        j, r = st.item(1), st.slot(1, 2)
                        pe.wait_ge(f["xgT"], j + 1)
                        pe.wait_ge(f["w1"], j + 1)
                        after(pe, f["hA"], 2 * (j - 1))
                        after(pe, f["hV"], 2 * (j - 1))
                        for k in range(FC):
                            mm = pe.matmul(bank[r + 2 * (k // 2)][:, k % 2 * P:(k % 2 + 1) * P],
                                           w1[r][:, k * P:(k + 1) * P], xgT[r][:, :], start=True, stop=True)
                            if k % 2:
                                mm.then_inc(f["H"], 1)
                    if st.on(2, NT):
                        j, r = st.item(2), st.slot(2, 2)
                        pe.wait_ge(f["hA"], 2 * (j + 1))
                        pe.wait_ge(f["hV"], 2 * (j + 1))
                        pe.wait_ge(f["w2"], j + 1)
                        after(pe, f["y"], j - 1)
                        for k in range(FC):
                            mm = pe.matmul(bank[4 + r][:, 0:D], hT[r][:, k, :], w2[r][:, k * D:(k + 1) * D],
                                           start=(k == 0), stop=(k == FC - 1))
                        mm.then_inc(f["Y"], 1)

            route_tensor(0)
            experts_tensor(0)

            pe.wait_ge(ffns[0]["y"], NT)
            pe.wait_ge(ld_wb, 32)
            pe.wait_ge(b_["bvr"], 1)
            pe.matmul(bank[2][:, 0:D], WB[:, 8 * D:9 * D], WB[:, 7 * D:8 * D], start=True, stop=True)
            pe.matmul(bank[3][:, 0:D], bv_rep[:, :], WB[:, 7 * D:8 * D], start=True, stop=True).then_inc(b_["wvo"], 1)
            pe.wait_ge(b_["init"], 1)
            pe.wait_ge(b_["bo"], 1)
            half = [bank[2][:, 0:S], bank[3][:, 0:S]]
            for st in steps(pe, B, 3, 6, 2, ahead=1):
                if st.on(1, B):
                    b, r = st.item(1), st.slot(1, 2)
                    pe.wait_ge(b_["qr"], 2 * (b + 1))
                    after(pe, b_["ttr"], C * b)
                    for c in range(C):
                        pe.matmul(bank[6][:, c * S:(c + 1) * S], qr[r][:, 0, c * P:(c + 1) * P], qr[r][:, 1, :],
                                  start=True, stop=True).then_inc(b_["S"], 1)
                if st.on(2, B):
                    b, r = st.item(2), st.slot(2, 2)
                    for c in range(C):
                        pe.wait_ge(b_["exp"], C * b + c + 1)
                        after(pe, b_["prT"], C * b + c)
                        for k in range(C):
                            mm = pe.transpose(bank[4][:, k * P:(k + 1) * P], pr[r][:, c, k * P:(k + 1) * P], ident)
                        mm.then_inc(b_["PT"], 1)
                if st.on(0, B):
                    b, r = st.item(0), st.slot(0, 2)
                    pe.wait_ge(b_["xb"], b + 1)
                    after(pe, b_["xbT"], b)
                    after(pe, tails[1]["lg"], b - 3)
                    for c in range(C):
                        mm = pe.transpose(bank[5][:, c * P:(c + 1) * P], xb[r][:, c, :], ident)
                    mm.then_inc(b_["T"], 1)
                if st.on(2, B):
                    b, r = st.item(2), st.slot(2, 2)
                    after(pe, tails[1]["x"], b)
                    for c in range(C):
                        pe.wait_ge(b_["prT"], C * b + c + 1)
                        for k in range(C):
                            mm = pe.matmul(bank[7][:, c * D:(c + 1) * D], prT[r][:, c, k * P:(k + 1) * P], vb[r][:, k, :],
                                           start=(k == 0), stop=(k == C - 1))
                        mm.then_inc(b_["PV"], 1)
                if st.on(0, B):
                    b, r = st.item(0), st.slot(0, 2)
                    pe.wait_ge(b_["xbT"], b + 1)
                    for i in range(7):
                        after(pe, b_["pje"], 8 * b + i - 1)
                        pe.matmul(half[i % 2], WB[:, i * D:(i + 1) * D], xbT[r][:, :], start=True, stop=True).then_inc(b_["pj"], 1)
                    pe.wait_ge(b_["pje"], 8 * b + 6)
                    for c in range(C):
                        mm = pe.matmul(half[1][:, c * D:(c + 1) * D], xbT[r][:, c * P:(c + 1) * P], WVO[:, :],
                                       start=True, stop=True)
                    mm.then_inc(b_["pj"], 1)
                    for c in range(C):
                        at = bank[5][:, S + c * IDX_HEADS:S + (c + 1) * IDX_HEADS]
                        pe.matmul(at, ones[0:1, :], rowc[:, 0:IDX_HEADS], start=True, stop=False)
                        mm = pe.matmul(at, xbT[r][:, c * P:(c + 1) * P], WB[:, 9 * D:9 * D + IDX_HEADS], start=False, stop=True)
                    mm.then_inc(b_["pj"], 1)
                    pe.wait_ge(b_["pje"], 8 * b + 7)
                    for c in range(C):
                        for h in range(IDX_HEADS):
                            lo = IDX_DIM * (h % 2)
                            if h < 2:
                                after(pe, b_["rel"], 2 * (C * b + c - 1) + h + 1)
                            mm = pe.matmul(bank[h % 2][:, h // 2 * S:(h // 2 + 1) * S],
                                           iq[r][lo:lo + IDX_DIM, h // 2, c * P:(c + 1) * P], ik[r][lo:lo + IDX_DIM, :],
                                           start=True, stop=True)
                            if h >= 2:
                                mm.then_inc(b_["idx"], 1)
                if st.on(3, B):
                    pe.wait_ge(b_["iwe"], st.item(0) + 1 if st.on(0, B) else B)
                    turn_xf(1, st.item(3), st.slot(3, 2), bank[5][:, 0:S])
                    router(1, st.item(3), st.slot(3, 2), bank[5][:, S + C * IDX_HEADS:S + C * IDX_HEADS + C * E])
            route_tensor(1)
            experts_tensor(1)

        @block.scalar
        def _(act):
            def xf_out(n, b, r, where):
                t = tails[n]
                act.wait_ge(t["T"], b + 1)
                after(act, t["R"], b - 1)
                act.activation(xfT[r][:, :], where, ACT.Copy).then_inc(t["xfT"], 1)

            def logits_out(n, b, where):
                t = tails[n]
                act.wait_ge(t["R"], b + 1)
                act.activation(logits[:, tiles(b), :], where.rearrange("p (c e) -> p c e", c=C), ACT.Copy).then_inc(t["lg"], 1)

            act.preload_act_table(ACT.Exp)
            act.wait_ge(ld_w, 96)
            act.wait_ge(a_coef, 4)
            for st in steps(act, B, 2, 4, 2, ahead=1):
                b, r = st.item(0), st.slot(0, 2)
                if st.on(0, B):
                    act.wait_ge(a_T, b + 1)
                    after(act, a_out, b - 1)
                    act.activation(xaT[r][:, :], bank[2][:, 0:S], ACT.Identity, scale=COL[:, 0:1],
                                   bias=COL[:, 1:2]).then_inc(a_xaT, 1)
                    act.wait_ge(a_kneg, b + 1)
                    after(act, a_ekT, b - 1)
                    after(act, a_einv, b - 1)
                    act.activation(ekT[r][:, :], bank[0][:, 0:S], ACT.Exp, bias=kneg[r][:, :],
                                   accum_out=esum[r][:, :]).then_inc(a_exp, 1)
                    act.wait_ge(a_V, b + 1)
                    after(act, a_ctx, b - 1)
                    act.activation(va[r][:, :, :], bank[1][:, 0:S].rearrange("p (c d) -> p c d", c=C),
                                   ACT.Copy).then_inc(a_va, 1)
                    after(act, tails[0]["x"], b - 1)
                    for c in range(C):
                        at = bass.ds(b * C + c, 1)
                        ins = act.activation(xres[r][:, c, :], X[:, at, :].rearrange("p a d -> p (a d)"), ACT.Identity,
                                             scale=ln1[:, XS, at], bias=ln1[:, XO, at])
                    ins.then_inc(a_pt, 1)
                if st.on(1, B):
                    p, q = st.item(1), st.slot(1, 2)
                    act.wait_ge(a_H, p + 1)
                    after(act, a_out, p - 1)
                    act.activation(Hs[q][:, :], bank[3][:, 2 * D:3 * D], ACT.Copy).then_inc(a_Hs, 1)
                if st.on(2, B):
                    xf_out(0, st.item(2), st.slot(2, 2), bank[6][:, 0:S])
                    logits_out(0, st.item(2), bank[7][:, 0:C * E])

            def route_scalar(n):
                act.wait_ge(rt["sub"], n + 1)
                act.activation(r_b[:, :, :], r_a[:, :, :], ACT.Exp).then_inc(rt["exp"], 1)

            def experts_scalar(n):
                f = ffns[n]
                if n == 0:
                    act.wait_ge(ld_we, 48)
                act.wait_ge(rt["te"], n + 1)
                act.preload_act_table(ACT.Exp)
                for st in steps(act, NT, 2, 9, 6):
                    if st.on(0, NT):
                        j, r, g = st.item(0), st.slot(0, 2), st.slot(0, G_RING)
                        expert = act.value_load(te[0:1, bass.ds(j, 1)], min_val=0, max_val=E - 1)
                        after(act, f["H"], 2 * (j - 1))
                        act.activation(w1[r][:, :], WE[:, bass.ds(expert, 1), W1_AT:W1_AT + F].rearrange("p a w -> p (a w)"),
                                       ACT.Copy).then_inc(f["w1"], 1)
                        act.wait_ge(f["T"], j + 1)
                        act.activation(xgT[r][:, :], bank[6 + r][:, 0:P], ACT.Copy).then_inc(f["xgT"], 1)
                        act.wait_ge(f["neg"], j + 1)
                        after(act, f["y"], j - 1)
                        act.activation(lexp[r][:, :], xg[g][:, 2 * D:ROW], ACT.Exp, bias=lneg[r][:, :],
                                       accum_out=lsum[r][:, :]).then_inc(f["exp"], 1)
                    if st.on(1, NT):
                        j, r = st.item(1), st.slot(1, 2)
                        act.wait_ge(f["w2"], j + 1)
                        after(act, f["Y"], j - 1)
                        act.wait_ge(f["H"], 2 * j + 1)
                        for k in range(FC // 2):
                            act.activation(hT[r][:, k, :], bank[r][:, k * P:(k + 1) * P], ACT.Relu,
                                           bias=w2[r][:, F + k:F + k + 1]).then_inc(f["hA"], 1)

            route_scalar(0)
            experts_scalar(0)

            act.wait_ge(b_["wvo"], 1)
            act.activation(WVO[:, :], bank[2][:, 0:D], ACT.Copy).then_inc(b_["init"], 1)
            act.preload_act_table(ACT.Exp)
            half = [bank[2][:, 0:S], bank[3][:, 0:S]]
            scale = float(D) ** -0.5
            for st in steps(act, B, 4, 6, 2, ahead=1):
                if st.on(2, B):
                    b, r = st.item(2), st.slot(2, 2)
                    for c in range(C):
                        act.wait_ge(b_["lnb"], C * b + c + 1)
                        after(act, b_["pinv"], b - 1)
                        act.activation(pr[r][:, c, :], lg[r][:, c, :], ACT.Exp, bias=lnb[r][:, c:c + 1], scale=scale,
                                       accum_out=psm[r][:, c:c + 1]).then_inc(b_["exp"], 1)
                    for c in range(C):
                        act.wait_ge(b_["PT"], C * b + c + 1)
                        after(act, b_["PV"], C * (b - 2) + c + 1)
                        act.activation(prT[r][:, c, :], bank[4][:, 0:S], ACT.Copy).then_inc(b_["prT"], 1)
                if st.on(0, B):
                    b, r = st.item(0), st.slot(0, 2)
                    act.wait_ge(b_["T"], b + 1)
                    after(act, b_["idx"], 2 * C * (b - 1))
                    act.activation(xbT[r][:, :], bank[5][:, 0:S], ACT.Copy).then_inc(b_["xbT"], 1)
                    for i in range(7):
                        act.wait_ge(b_["pj"], 9 * b + i + 1)
                        if i == 0:
                            after(act, b_["qr"], 2 * (b - 1))
                        dst = qk[r][:, i, :] if i < 4 else iq[r][:, i - 4, :] if i < 6 else ik[r][:, :]
                        act.activation(dst, half[i % 2], ACT.Identity, bias=COL[:, 2 + i:3 + i]).then_inc(b_["pje"], 1)
                    act.wait_ge(b_["pj"], 9 * b + 8)
                    after(act, b_["PV"], C * (b - 1))
                    act.activation(vb[r][:, :, :], half[1].rearrange("p (c d) -> p c d", c=C), ACT.Copy).then_inc(b_["pje"], 1)
                    act.wait_ge(b_["pj"], 9 * (b + 1))
                    after(act, b_["wk"], C * (b - 1))
                    act.activation(iw[r][:, :, :],
                                   bank[5][:, S:S + C * IDX_HEADS].rearrange("p (c h) -> p c h", c=C),
                                   ACT.Copy).then_inc(b_["iwe"], 1)
                    after(act, b_["hs"], C * (b - 1))
                    act.wait_ge(b_["iwe"], b + 1)
                    for c in range(C):
                        for i in range(2):
                            act.wait_ge(b_["idx"], 2 * (C * b + c) + i + 1)
                            act.activation(rel[r][:, c, i::2, :],
                                           bank[i][:, :].rearrange("p (h k) -> p h k", h=2), ACT.Relu).then_inc(b_["rel"], 1)
                        act.wait_ge(b_["rel"], 2 * (C * b + c + 1))
                        for h in range(2):
                            ins = act.activation(part[r][:, c, h, :], rel[r][:, c, h, :], ACT.Copy,
                                                 scale=iw[r][:, c, h:h + 1])
                        ins.then_inc(b_["prt"], 1)
                if st.on(3, B):
                    xf_out(1, st.item(3), st.slot(3, 2), bank[5][:, 0:S])
                    logits_out(1, st.item(3), bank[5][:, S + C * IDX_HEADS:S + C * IDX_HEADS + C * E])
            route_scalar(1)
            experts_scalar(1)

        @block.vector
        def _(dve):
            def stats(t, x_of, stat, mv, b, r, free, count):
                for c in range(C):
                    ins = dve.bn_stats(stat[:, c, :], x_of(c))
                ins.then_inc(t["st"], 1)
                alone(dve, t["st"], b + 1, passed["dve"])
                alone(dve, free, count, passed["dve"])
                for c in range(C):
                    ins = dve.bn_aggr(mv[r][:, c, :], stat[:, c, :])
                ins.then_inc(t["mv"], 1)

            def normalise(t, key, x_of, dst, mv, rs, b, r):
                dve.wait_ge(t["rs"], b + 1)
                dve.wait_ge(t["mv"], b + 1)
                for c in range(C):
                    ins = dve.tensor_scalar(dst[:, c, :], x_of(c), mv[r][:, c, 0:1], rs[r][:, c:c + 1],
                                            ALU.subtract, ALU.mult)
                ins.then_inc(t[key], 1)

            def one_tile(b, c):
                return X[:, bass.ds(b * C + c, 1), :].rearrange("p a d -> p (a d)")

            per = T // 4
            for g in range(4):
                dve.wait_ge(ld_x[g], 16)
                for c in range(g * per, (g + 1) * per):
                    ins = dve.bn_stats(stat1[:, c, :], X[:, c, :])
                ins.then_inc(a_stat, 1)
                dve.wait_ge(a_stat, 2 * g + 1)
                for c in range(g * per, (g + 1) * per):
                    ins = dve.bn_aggr(mv1[:, c, :], stat1[:, c, :])
                ins.then_inc(a_stat, 1)

            def twice_normal(b, r):
                after(dve, a_T, b - 1)
                for c in range(C):
                    at = bass.ds(b * C + c, 1)
                    ins = dve.tensor_scalar(xa[r][:, c, :], one_tile(b, c), mv1[:, at, 0], ln1[:, R1, at],
                                            ALU.subtract, ALU.mult)
                ins.then_inc(a_xa, 1)

            dve.wait_ge(a_coef, 4)
            dve.wait_ge(ld_c, 16)
            twice_normal(0, 0)
            for st in steps(dve, B, 2, 4, 2, ahead=1):
                b, r = st.item(0), st.slot(0, 2)
                p, q = st.item(1), st.slot(1, 2)
                if st.on(1, B):
                    dve.wait_ge(a_ekT, p + 1)
                    after(dve, a_ctx, p - 1)
                    dve.tensor_copy(ek[q][:, :, :], bank[5][:, 0:S].rearrange("p (c d) -> p c d", c=C)).then_inc(a_ek, 1)
                    after(dve, a_Gs, p - 1)
                    dve.reciprocal(einv[q][:, :], esum[q][:, :]).then_inc(a_einv, 1)
                if st.on(0, B):
                    dve.wait_ge(a_K, b + 1)
                    after(dve, a_exp, b - 1)
                    dve.tensor_reduce(kneg[r][:, :], bank[0][:, 0:S], AX.X, ALU.max, negate=True).then_inc(a_kneg, 1)
                if st.on(1, B):
                    dve.wait_ge(a_ctx, p + 1)
                    after(dve, a_G, p - 1)
                    dve.tensor_tensor(cm[q][:, :], bank[3][:, 0:D], const("blocks"), ALU.mult).then_inc(a_cm, 1)
                    dve.wait_ge(a_G, p + 1)
                    dve.wait_ge(a_einv, p + 1)
                    after(dve, a_H, p - 1)
                    dve.tensor_scalar(Gs[q][:, :], bank[3][:, D:2 * D], einv[q][:, :], float(DIM_HEAD) ** -0.5,
                                      ALU.mult, ALU.mult).then_inc(a_Gs, 1)
                if st.on(2, B):
                    n, m = st.item(2), st.slot(2, 2)
                    after(dve, tails[0]["store"][m], 32 * st.lap(2, 2))
                    after(dve, tails[0]["T"], n - 1)
                    normalise(tails[0], "xf", lambda c: one_tile(n, c), xf[m], mv3, rs3, n, m)
                if st.on(-1, B):
                    twice_normal(st.item(-1), st.slot(-1, 2))
                if st.on(1, B):
                    dve.wait_ge(a_out, p + 1)
                    dve.wait_ge(a_xres, p + 1)
                    dve.tensor_tensor(X[:, tiles(p), :], bank[4][:, 0:S].rearrange("p (c d) -> p c d", c=C),
                                      xres[q][:, :, :], ALU.add).then_inc(tails[0]["x"], 1)
                    alone(dve, tails[0]["x"], p + 1, passed["dve"])
                    stats(tails[0], lambda c: one_tile(p, c), stat3, mv3, p, q, tails[0]["xf"], p - 1)

            def route_vector(n):
                count = 100 * n

                def link(ins):
                    nonlocal count
                    count += 1
                    ins.then_inc(rt["v"], 1)
                    dve.wait_ge(rt["v"], count)

                if n == 0:
                    link(dve.tensor_copy(colbf[:, :], const("col")))
                dve.wait_ge(tails[n]["lg"], B)
                v = lambda k: r_m[:, k, :]
                over_e = lambda a: a.unsqueeze(2).to_broadcast([P, T, E])
                link(dve.tensor_reduce(v(0), logits[:, :, :], AX.X, ALU.max))
                dve.tensor_tensor(r_a[:, :, :], logits[:, :, :], over_e(v(0)), ALU.subtract).then_inc(rt["sub"], 1)
                dve.wait_ge(rt["exp"], n + 1)
                link(dve.tensor_reduce(v(1), r_b[:, :, :], AX.X, ALU.max))
                link(dve.tensor_tensor(r_a[:, :, :], r_b[:, :, :], over_e(v(1)), ALU.is_equal))
                link(dve.tensor_tensor(r_b[:, :, :], r_a[:, :, :], const("down").unsqueeze(1).to_broadcast([P, T, E]), ALU.mult))
                link(dve.tensor_reduce(v(2), r_b[:, :, :], AX.X, ALU.max))
                link(dve.tensor_tensor(oh[:, :, :].rearrange("p e t -> p t e"), r_b[:, :, :], over_e(v(2)), ALU.is_equal))
                link(dve.tensor_tensor_scan(incl[:, :, :].rearrange("p e t -> p (e t)"), const("keep"),
                                            oh[:, :, :].rearrange("p e t -> p (e t)"), 0.0, ALU.mult, ALU.add))
                dve.tensor_copy(rtot[:, :], incl[:, :, T - 1]).then_inc(rt["rtot"], 1)
                dve.wait_ge(rt["tot"], n + 1)
                over_t = lambda a: a.unsqueeze(2).to_broadcast([P, E, T])
                link(dve.tensor_copy(nt[:, 0, :], bank[0][:, 0:E]))
                link(dve.tensor_tensor(rr[:, :, :], over_t(bank[0][:, E:2 * E]),
                                       const("starts").unsqueeze(1).to_broadcast([P, E, T]), ALU.is_gt))
                link(dve.tensor_reduce(nt[:, 1, :], rr[:, :, :], AX.X, ALU.add))
                link(dve.tensor_tensor_scan(nt[:, 2, :], ones[:, 0:E], nt[:, 1, :], 0.0, ALU.mult, ALU.add))
                link(dve.tensor_tensor(rr[:, :, :], incl[:, :, :], over_t(nt[:, 0, :]), ALU.add))
                link(dve.tensor_tensor(rr[:, :, :], rr[:, :, :], oh[:, :, :], ALU.mult))
                link(dve.tensor_reduce(v(3), rr[:, :, :].rearrange("p e t -> p t e"), AX.X, ALU.add))
                link(dve.tensor_tensor(nt[:, 1, :], nt[:, 2, :], nt[:, 1, :], ALU.subtract))
                link(dve.tensor_tensor(rr[:, :, :], oh[:, :, :], over_t(nt[:, 1, :]), ALU.mult))
                link(dve.tensor_reduce(v(4), rr[:, :, :].rearrange("p e t -> p t e"), AX.X, ALU.add))
                link(dve.tensor_scalar(v(5), v(3), 1.0 / P, -(P / 2 + 0.5) / P, ALU.mult, ALU.add))
                link(dve.tensor_scalar(v(5), v(5), MAGIC, MAGIC, ALU.add, ALU.subtract))
                link(dve.tensor_tensor(v(4), v(4), v(5), ALU.add))
                link(dve.scalar_tensor_tensor(v(6), v(5), float(-P), v(3), ALU.mult, ALU.add))
                by_tile = lambda k: oneh_tile[:, :, k, :]
                link(dve.tensor_tensor(by_tile(1), const("tile").unsqueeze(1).to_broadcast([P, T, NT]),
                                       v(4).unsqueeze(2).to_broadcast([P, T, NT]), ALU.is_equal))
                link(dve.tensor_scalar(by_tile(0), by_tile(1), const("part1"), None, ALU.mult))
                dve.tensor_tensor(by_tile(1), by_tile(1), colbf[:, :].unsqueeze(2).to_broadcast([P, T, NT]),
                                  ALU.mult).then_inc(rt["slots"], 1)
                for g in range(4):
                    cs = slice(g * per, (g + 1) * per)
                    dve.tensor_tensor(oneh_slot[:, cs, :], const("slot1").unsqueeze(1).to_broadcast([P, per, P]),
                                      r_m[:, 6, cs].unsqueeze(2).to_broadcast([P, per, P]), ALU.is_equal).then_inc(rt["slots"], 1)
                link(dve.tensor_tensor(tef[:, :, :], const("tile")[0:1, :].unsqueeze(2).to_broadcast([1, NT, E]),
                                       nt[0:1, 2, :].unsqueeze(1).to_broadcast([1, NT, E]), ALU.is_ge))
                link(dve.tensor_reduce(tes[:, :], tef[:, :, :], AX.X, ALU.add))
                dve.tensor_scalar(te[:, :], tes[:, :], float(E - 1), None, ALU.min).then_inc(rt["te"], 1)
                dve.wait_ge(rt["inv"], n + 1)
                link(dve.tensor_scalar(idxf[:, 0, :], bank[1][:, 0:NT], -1.0, None, ALU.add))
                link(dve.scalar_tensor_tensor(idxf[:, 1, :], bank[1][:, NT:2 * NT], float(P), idxf[:, 0, :], ALU.mult, ALU.add))
                dve.tensor_scalar(gidx[:, :], idxf[:, 1, :], 0.0, None, ALU.max).then_inc(rt["idx"], 1)
                link(dve.tensor_scalar(idxf[:, 2, :], idxf[:, 1, :], 0.0, float(2 * TOKENS), ALU.is_lt, ALU.mult))
                dve.tensor_tensor(sidx[:, :], idxf[:, 1, :], idxf[:, 2, :], ALU.add).then_inc(rt["idx"], 1)
                if n == 0:
                    dve.sem_inc(rt["v"], 100 - count)

            def experts_vector(n):
                f = ffns[n]
                if n == 0:
                    dve.wait_ge(ld_we, 48)
                dve.wait_ge(rt["te"], n + 1)
                for st in steps(dve, NT, 2, 9, 6):
                    if st.on(1, NT):
                        j, r = st.item(1), st.slot(1, 2)
                        dve.wait_ge(f["w2"], j + 1)
                        after(dve, f["Y"], j - 1)
                        dve.wait_ge(f["H"], 2 * (j + 1))
                        for k in range(FC // 2, FC):
                            dve.tensor_scalar(hT[r][:, k, :], bank[2 + r][:, k % 2 * P:(k % 2 + 1) * P], w2[r][:, F + k:F + k + 1], 0.0,
                                              ALU.add, ALU.max).then_inc(f["hV"], 1)
                    if st.on(0, NT):
                        j, r, g = st.item(0), st.slot(0, 2), st.slot(0, G_RING)
                        dve.wait_ge(f["g"][g], 16 * (st.lap(0, G_RING) + 1))
                        after(dve, f["exp"], j - 1)
                        dve.tensor_reduce(lneg[r][:, :], xg[g][:, 2 * D:ROW], AX.X, ALU.max, negate=True).then_inc(f["neg"], 1)
                    if st.on(2, NT):
                        j, r, g, o = st.item(2), st.slot(2, 2), st.slot(2, G_RING), st.slot(2, Y_RING)
                        dve.wait_ge(f["exp"], j + 1)
                        after(dve, f["y"], j)
                        dve.reciprocal(gate[:, :], lsum[r][:, :]).then_inc(f["v"], 1)
                        dve.wait_ge(f["Y"], j + 1)
                        dve.tensor_tensor(yb[:, :], bank[4 + r][:, 0:D], w2[r][:, F + FC:F + FC + D], ALU.add).then_inc(f["v"], 1)
                        dve.wait_ge(f["v"], 2 * (j + 1))
                        after(dve, f["s"][o], 16 * st.lap(2, Y_RING))
                        dve.scalar_tensor_tensor(yo[o][:, :], yb[:, :], gate[:, :], xg[g][:, D:2 * D],
                                                 ALU.mult, ALU.add).then_inc(f["y"], 1)
                    if st.on(0, NT):
                        j, r = st.item(0), st.slot(0, 2)
                        expert = dve.value_load(te[0:1, bass.ds(j, 1)], min_val=0, max_val=E - 1)
                        after(dve, f["y"], j - 1)
                        dve.tensor_copy(w2[r][:, :], WE[:, bass.ds(expert, 1), W2_AT:W_LEN].rearrange("p a w -> p (a w)")
                                        ).then_inc(f["w2"], 1)

            route_vector(0)
            experts_vector(0)

            dve.wait_ge(ld_wb, 32)
            dve.tensor_scalar(bv_rep[:, :], ones, COL[:, 9:10], None, ALU.mult).then_inc(b_["bvr"], 1)
            dve.wait_ge(b_["wvo"], 1)
            dve.tensor_tensor(bo_bc[:, :], bank[3][:, 0:D], bo_bc[:, :], ALU.add).then_inc(b_["bo"], 1)

            def stats_b(b, r):
                alone(dve, b_["x"], 16 * (b + 1), passed["dve"])
                stats(b_, lambda c: one_tile(b, c), stat2, mv2, b, r, b_["xb"], b - 1)

            stats_b(0, 0)
            scale = float(D) ** -0.5
            for st in steps(dve, B, 3, 6, 2, ahead=1):
                if st.on(0, B):
                    b, r = st.item(0), st.slot(0, 2)
                    after(dve, b_["T"], b - 1)
                    normalise(b_, "xb", lambda c: one_tile(b, c), xb[r], mv2, rs2, b, r)
                if st.on(-1, B):
                    stats_b(st.item(-1), st.slot(-1, 2))
                if st.on(1, B):
                    b, r = st.item(1), st.slot(1, 2)
                    for c in range(C):
                        dve.wait_ge(b_["hs"], C * b + c + 1)
                        dve.scalar_tensor_tensor(wk[:, c, :], rel[r][:, c, 2, :], iw[r][:, c, 2:3], half_sum[r][:, c, :],
                                                 ALU.mult, ALU.add).then_inc(b_["s1"], 1)
                    for c in range(C):
                        dve.wait_ge(b_["s1"], C * b + c + 1)
                        dve.scalar_tensor_tensor(wk[:, c, :], rel[r][:, c, 3, :], iw[r][:, c, 3:4], wk[:, c, :],
                                                 ALU.mult, ALU.add).then_inc(b_["wk"], 1)
                    rounds = TOP_K // 8
                    for i in range(rounds):
                        for c in range(C):
                            if i == 0:
                                alone(dve, b_["wk"], C * b + c + 1, passed["dve"])
                            else:
                                alone(dve, b_["v"], 2 * C * (rounds * b + i - 1) + C + c + 1, passed["dve"])
                            dve.max(m8[:, c, :], wk[:, c, :]).then_inc(b_["v"], 1)
                        for c in range(C):
                            alone(dve, b_["v"], 2 * C * (rounds * b + i) + c + 1, passed["dve"])
                            dve.match_replace(wk[:, c, :], m8[:, c, :], wk[:, c, :], NEG).then_inc(b_["v"], 1)
                if st.on(2, B):
                    b, r = st.item(2), st.slot(2, 2)
                    dve.wait_ge(b_["exp"], C * (b + 1))
                    dve.reciprocal(pinv[:, :], psm[r][:, :]).then_inc(b_["pinv"], 1)
                    dve.wait_ge(b_["pinv"], b + 1)
                    dve.wait_ge(b_["PV"], C * (b + 1))
                    dve.wait_ge(b_["xbias"], b + 1)
                    after(dve, tails[1]["store"][r], 32 * st.lap(2, 2))
                    for c in range(C):
                        ins = dve.scalar_tensor_tensor(x3[r][:, c, :], bank[7][:, c * D:(c + 1) * D], pinv[:, c:c + 1],
                                                       xbias[r][:, c, :], ALU.mult, ALU.add)
                    ins.then_inc(tails[1]["x"], 1)
                if st.on(1, B):
                    b, r = st.item(1), st.slot(1, 2)
                    for c in range(C):
                        dve.wait_ge(b_["v"], 2 * C * (rounds * (b + 1) - 1) + C + c + 1)
                        dve.tensor_scalar(pen[:, c, :], wk[:, c, :], -1.0e38, -1.0e30, ALU.is_gt, ALU.mult).then_inc(b_["fin"], 1)
                    for c in range(C):
                        alone(dve, b_["fin"], C * b + c + 1, passed["dve"])
                        alone(dve, b_["S"], C * (b + 1), passed["dve"])
                        alone(dve, b_["PT"], C * (b - 2) + c + 1, passed["dve"])
                        dve.tensor_tensor_reduce(lg[r][:, c, :], bank[6][:, c * S:(c + 1) * S], pen[:, c, :], 1.0, -3.0e38,
                                                 ALU.add, ALU.max, lmax[:, c:c + 1]).then_inc(b_["ttr"], 1)
                if st.on(2, B):
                    b, r = st.item(2), st.slot(2, 2)
                    alone(dve, tails[1]["x"], b + 1, passed["dve"])
                    stats(tails[1], lambda c: x3[r][:, c, :], stat3, mv3, b, r, tails[1]["xf"], b - 1)
                if st.on(1, B):
                    b, r = st.item(1), st.slot(1, 2)
                    for c in range(C):
                        dve.wait_ge(b_["ttr"], C * b + c + 1)
                        dve.tensor_scalar(lnb[r][:, c:c + 1], lmax[:, c:c + 1], -scale, None, ALU.mult).then_inc(b_["lnb"], 1)
                if st.on(2, B):
                    b, r = st.item(2), st.slot(2, 2)
                    after(dve, tails[1]["T"], b - 1)
                    normalise(tails[1], "xf", lambda c: x3[r][:, c, :], xf[r], mv3, rs3, b, r)
            route_vector(1)
            experts_vector(1)


def kernel(**inputs):
    import concourse.bacc as bacc
    from concourse.bass_utils import run_bass_kernel_spmd

    a = {k: np.asarray(v) for k, v in inputs.items()}

    def row(v):
        return np.ascontiguousarray(v).reshape(1, -1)

    w = a["L0_attn_a_w_qkv"]
    w_attn = np.concatenate([w[:, :D].T, w[:, D:2 * D], w[:, 2 * D:], a["L0_attn_a_w_out"]], axis=1)
    wt = a["L0_attn_b_w_qkv"].T
    other = np.r_[D // 2:D, 0:D // 2]
    wiq, wik = a["L0_attn_b_w_iq"].T, a["L0_attn_b_w_ik"].T
    wiw = np.zeros((D, D), np.float32)
    wiw[:, :IDX_HEADS] = a["L0_attn_b_w_iw"].T
    w_idx = np.concatenate([wt[:, :D], wt[:, :D][:, other], wt[:, D:2 * D], wt[:, D:2 * D][:, other], wiq, wik, wik,
                            a["L0_attn_b_w_o"].T, a["L0_attn_b_w_qkv"][2 * D:], wiw], axis=1)
    bq, bk, bv = np.split(a["L0_attn_b_b_qkv"], 3)
    biq, bik = a["L0_attn_b_b_iq"], a["L0_attn_b_b_ik"]
    cols = np.stack([a["L0_attn_a_gamma"].reshape(D), a["L0_attn_a_beta"].reshape(D), bq, bq[other], bk, bk[other],
                     biq[:D], biq[D:], np.concatenate([bik, bik]), bv], axis=1)
    w1 = a["L0_ffn_W1"].transpose(1, 0, 2)
    w2 = a["L0_ffn_W2"].reshape(E, FC, P, D).transpose(2, 0, 1, 3).reshape(P, E, F)
    arrays = {
        "x": a["L0_attn_a_x"].reshape(TOKENS, D),
        "w_attn": w_attn,
        "w_idx": w_idx,
        "w_experts": np.concatenate([w1, w2], axis=2),
        "b1_cols": a["L0_ffn_b1"].reshape(E, FC, P).transpose(2, 0, 1),
        "b2": a["L0_ffn_b2"],
        "w_router": a["L0_ffn_Wr"],
        "cols": cols,
        "b_out": a["L0_attn_a_b_out"],
        "b_o": a["L0_attn_b_b_o"],
        "b_iw": row(a["L0_attn_b_b_iw"]),
        "b_r": row(a["L0_ffn_br"]),
        "consts": constant_table(),
    }
    arrays = {k: np.ascontiguousarray(v) for k, v in arrays.items()}
    nc = bacc.Bacc("TRN2", target_bir_lowering=False, num_devices=1)
    aps = {k: nc.dram_tensor(k, v.shape, mybir.dt.from_np(v.dtype), kind="ExternalInput").ap() for k, v in arrays.items()}
    out = nc.dram_tensor("out", (TOKENS, D), F32, kind="ExternalOutput").ap()
    build(nc, **aps, out=out)
    r = run_bass_kernel_spmd(nc, [arrays], core_ids=[0])
    return r.results[0]["out"].reshape(B, S, D)
```

```python
from contextlib import ExitStack

import numpy as np
import concourse.bass as bass
from concourse import mybir

F32 = mybir.dt.float32
BF16 = mybir.dt.bfloat16
I32 = mybir.dt.int32
U32 = mybir.dt.uint32
ALU = mybir.AluOpType
ACT = mybir.ActivationFunctionType
AX = mybir.AxisListType

P = 128
B, S, D = 16, 256, 128
C = S // P
T = B * C
TOKENS = B * S
HEADS, DIM_HEAD = 4, 32
IDX_HEADS, IDX_DIM, TOP_K = 4, 64, 32
E, F = 8, 512
FC = F // P
NT = T + E - 1
TURN = 6
TE_LEN = 8 * -(-NT // TURN)
EPS = 1e-5
ROW = 2 * D + E
NEG = -3.0e38
MAGIC = 1.5 * 2.0**23
W1_AT, W2_AT, B1_AT, B2_AT = 0, F, 2 * F, 2 * F + FC
W_LEN = 2 * F + FC + D
CONSTS = [("ident", P), ("blocks", P), ("tri", P), ("ones", P), ("cos", S), ("sin", S), ("slot1", P),
          ("tile", NT), ("turns", TE_LEN), ("down", E), ("keep", E * T), ("starts", T), ("col", T), ("part1", 1)]
CONST_AT, CONST_LEN = {}, 0
for _name, _len in CONSTS:
    CONST_AT[_name] = (CONST_LEN, CONST_LEN + _len)
    CONST_LEN += _len


def constant_table():
    half = D // 2
    inv = (1.0 / 10000.0 ** (np.arange(half, dtype=np.float32) / np.float32(half))).astype(np.float32)
    ang = (np.arange(S, dtype=np.float32)[:, None] * inv[None, :]).astype(np.float32)
    cos, sin = np.cos(ang).T, np.sin(ang).T
    rows = np.arange(P)
    t = {
        "ident": np.eye(P),
        "blocks": rows[:, None] // DIM_HEAD == rows[None, :] // DIM_HEAD,
        "tri": rows[:, None] < rows[None, :],
        "ones": np.ones((P, P)),
        "cos": np.concatenate([cos, cos]),
        "sin": np.concatenate([-sin, sin]),
        "slot1": np.broadcast_to(rows + 1, (P, P)),
        "tile": np.broadcast_to(np.arange(NT), (P, NT)),
        "turns": np.broadcast_to(np.arange(TE_LEN) // 8 * TURN + np.minimum(np.arange(TE_LEN) % 8, TURN - 1), (P, TE_LEN)),
        "down": np.broadcast_to(E - np.arange(E), (P, E)),
        "keep": np.broadcast_to(np.arange(E * T) % T != 0, (P, E * T)),
        "starts": np.broadcast_to(np.arange(T) * P, (P, T)),
        "col": np.broadcast_to(np.arange(T), (P, T)),
        "part1": rows[:, None] + 1,
    }
    return np.concatenate([np.asarray(t[n], np.float32).reshape(P, -1) for n, _ in CONSTS], axis=1)


class Step:

    def __init__(self, base, unroll=1, turn=0):
        self.base, self.unroll, self.turn = base, unroll, turn

    def item(self, lag):
        return self.base - lag + self.unroll * self.turn

    def slot(self, lag, ring):
        return (self.base - lag) % ring

    def lap(self, lag, ring):
        return (self.base - lag) // ring + self.unroll // ring * self.turn

    def on(self, lag, items):
        return not isinstance(self.turn, int) or 0 <= self.base - lag < items


def steps(eng, items, lag, head, unroll, ahead=0):
    turns = (items - ahead - head) // unroll
    for s in range(head):
        yield Step(s)
    with eng.Fori(0, turns) as turn:
        for k in range(unroll):
            yield Step(head + k, unroll, turn)
    for s in range(head + turns * unroll, items + lag):
        yield Step(s)


def after(eng, sem, count):
    if not isinstance(count, int) or count > 0:
        eng.wait_ge(sem, count)


def alone(eng, sem, count, passed):
    if not isinstance(count, int) or count > 0:
        eng.wait_ge(sem, count)
        eng.sem_inc(passed, 1)


def build(nc, x, w_attn, w_idx, w_experts, b1_cols, b2, w_router, cols, b_out, b_o, b_iw, b_r, consts, out):
    with ExitStack() as ctx:
        def sb(name, shape, dt=F32):
            return ctx.enter_context(nc.sbuf_tensor(name, shape, dt))

        def sem(name):
            return ctx.enter_context(nc.semaphore(name))

        def sems(name, n):
            return [sem(f"{name}{i}") for i in range(n)]

        bank = [ctx.enter_context(nc.psum_tensor(f"bank{i}", [P, 512], F32)) for i in range(8)]

        rows_dram = [nc.dram_tensor(f"rows{i}", [TOKENS, ROW], F32, kind="Internal").ap() for i in range(2)]
        x2_dram = nc.dram_tensor("x2", [NT * P, D], F32, kind="Internal").ap()

        X = sb("X", [P, T, D])
        cst = sb("cst", [P, CONST_LEN])
        WE = sb("WE", [P, E, W_LEN])
        WA = sb("WA", [P, 4 * D])
        WR = sb("WR", [P, E])
        COL = sb("COL", [P, 10])
        WB = sb("WB", [P, 10 * D])
        WVO = sb("WVO", [P, D])
        bout_bc = sb("bout_bc", [P, D])
        bo_bc = sb("bo_bc", [P, D])
        bv_rep = sb("bv_rep", [P, P])
        rowc = sb("rowc", [1, C * (IDX_HEADS + E)])
        mhalf = sb("mhalf", [P, 2, T // 4])
        eps = sb("eps", [P, C])
        xf = [sb(f"xf{i}", [P, C, D]) for i in range(2)]
        xfT = [sb(f"xfT{i}", [P, S]) for i in range(2)]
        stat3 = sb("stat3", [P, C, 6])
        mv3 = [sb(f"mv3_{i}", [P, C, 2]) for i in range(2)]
        vpe3 = sb("vpe3", [P, C])
        rs3 = [sb(f"rs3_{i}", [P, C]) for i in range(2)]
        logits = sb("logits", [P, T, E])

        def const(name):
            a, b = CONST_AT[name]
            return cst[:, a:b]

        ident, ones = const("ident"), const("ones")

        mv1 = sb("mv1", [P, T, 2])
        stat1 = sb("stat1", [P, T, 6])
        v1 = sb("v1", [P, 2, T])
        r1 = sb("r1", [P, 2, T])
        xs = sb("xs", [P, 2, T])
        xa = [sb(f"xa{i}", [P, C, D]) for i in range(2)]
        xaT = [sb(f"xaT{i}", [P, S]) for i in range(4)]
        kneg = [sb(f"kneg{i}", [P, 1]) for i in range(2)]
        ekT = [sb(f"ekT{i}", [P, S]) for i in range(2)]
        esum = [sb(f"esum{i}", [P, 1]) for i in range(4)]
        einv = [sb(f"einv{i}", [P, 1]) for i in range(2)]
        ek = [sb(f"ek{i}", [P, C, D]) for i in range(2)]
        va = [sb(f"va{i}", [P, C, D]) for i in range(2)]
        cm = [sb(f"cm{i}", [P, D]) for i in range(2)]
        Gs = [sb(f"Gs{i}", [P, D]) for i in range(2)]
        Hs = [sb(f"Hs{i}", [P, D]) for i in range(2)]
        xres = [sb(f"xres{i}", [P, C, D]) for i in range(2)]

        r_a = sb("r_a", [P, T, E])
        r_b = sb("r_b", [P, T, E])
        oh = sb("oh", [P, E, T])
        incl = sb("incl", [P, E, T])
        rr = sb("rr", [P, E, T])
        r_m = sb("r_m", [P, 8, T])
        rtot = sb("rtot", [P, E])
        nt = sb("nt", [P, 3, E])
        oneh_slot = sb("oneh_slot", [P, T, P], BF16)
        oneh_tile = sb("oneh_tile", [P, T, 2, NT], BF16)
        colbf = sb("colbf", [P, T], BF16)
        idxf = sb("idxf", [P, 3, NT])
        gidx = sb("gidx", [P, NT], U32)
        sidx = sb("sidx", [P, NT], U32)
        pidx = sb("pidx", [P, T], U32)
        pcur = [sb(f"pcur{i}", [P, C], U32) for i in range(2)]
        tef = sb("tef", [1, TE_LEN, E])
        tes = sb("tes", [1, TE_LEN])
        te = sb("te", [1, TE_LEN], I32)

        G_RING, Y_RING = 6, 6
        xg = [sb(f"xg{i}", [P, ROW]) for i in range(G_RING)]
        xgT = [sb(f"xgT{i}", [P, P]) for i in range(2)]
        w1 = [sb(f"w1_{i}", [P, F]) for i in range(2)]
        w2 = [sb(f"w2_{i}", [P, W_LEN - F]) for i in range(2)]
        hT = [sb(f"hT{i}", [P, FC, P]) for i in range(2)]
        lneg = [sb(f"lneg{i}", [P, 1]) for i in range(2)]
        lexp = [sb(f"lexp{i}", [P, E]) for i in range(2)]
        lsum = [sb(f"lsum{i}", [P, 1]) for i in range(Y_RING)]
        gate = sb("gate", [P, 1])
        yb = sb("yb", [P, D])
        yo = [sb(f"yo{i}", [P, D]) for i in range(Y_RING)]

        xin = [X[:, i * C:(i + 1) * C, :] for i in range(2)]
        stat2 = sb("stat2", [P, C, 6])
        mv2 = [sb(f"mv2_{i}", [P, C, 2]) for i in range(2)]
        vpe2 = sb("vpe2", [P, C])
        rs2 = [sb(f"rs2_{i}", [P, C]) for i in range(2)]
        xb = [sb(f"xb{i}", [P, C, D]) for i in range(2)]
        xbT = [sb(f"xbT{i}", [P, S]) for i in range(2)]
        qk = [sb(f"qk{i}", [P, 4, S]) for i in range(2)]
        qr = [sb(f"qr{i}", [P, 2, S]) for i in range(2)]
        iq = [sb(f"iq{i}", [P, 2, S]) for i in range(2)]
        ik = [sb(f"ik{i}", [P, S]) for i in range(2)]
        vb = [sb(f"vb{i}", [P, C, D]) for i in range(2)]
        iw = [sb(f"iw{i}", [P, C, IDX_HEADS]) for i in range(2)]
        rel = [sb(f"rel{i}", [P, C, IDX_HEADS, S]) for i in range(2)]
        part = [sb(f"part{i}", [P, C, 2, S]) for i in range(2)]
        half_sum = [sb(f"half_sum{i}", [P, C, S]) for i in range(2)]
        wk = sb("wk", [P, C, S])
        m8 = sb("m8", [P, C, 8])
        pen = sb("pen", [P, C, S])
        lg = [sb(f"lg{i}", [P, C, S]) for i in range(2)]
        lmax = sb("lmax", [P, C])
        lnb = [sb(f"lnb{i}", [P, C]) for i in range(2)]
        pr = lg
        psm = [sb(f"psm{i}", [P, C]) for i in range(2)]
        pinv = sb("pinv", [P, C])
        prT = [sb(f"prT{i}", [P, C, S]) for i in range(2)]
        xbias = [sb(f"xbias{i}", [P, C, D]) for i in range(2)]
        x3 = [sb(f"x3_{i}", [P, C, D]) for i in range(2)]

        ld_c, ld_w, ld_x = sem("ld_c"), sem("ld_w"), sems("ld_x", 4)
        passed = {k: sem(f"passed_{k}") for k in ("dve", "pool", "sp")}
        ld_wb, ld_we = sem("ld_wb"), sem("ld_we")
        a_stat, a_var, a_pow, a_coef = sem("a_stat"), sem("a_var"), sem("a_pow"), sem("a_coef")
        a_xa, a_T, a_xaT, a_K, a_V = sem("a_xa"), sem("a_T"), sem("a_xaT"), sem("a_K"), sem("a_V")
        a_kneg, a_exp, a_va, a_ekT, a_ek = sem("a_kneg"), sem("a_exp"), sem("a_va"), sem("a_ekT"), sem("a_ek")
        a_ctx, a_cm, a_einv, a_G, a_Gs = sem("a_ctx"), sem("a_cm"), sem("a_einv"), sem("a_G"), sem("a_Gs")
        a_H, a_Hs, a_out, a_xres, a_pt = sem("a_H"), sem("a_Hs"), sem("a_out"), sem("a_xres"), sem("a_pt")
        c_half = sem("c_half")
        tails = []
        for n in "ab":
            tails.append({k: sem(f"{n}t_{k}") for k in
                          ("x", "st", "mv", "ve", "rs", "xf", "T", "xfT", "R", "lg")} | {
                          "store": sems(f"{n}t_store", 2), "rest": sem(f"{n}t_rest")})
        rt = {k: sem(f"r_{k}") for k in ("v", "sub", "exp", "rtot", "tot", "slots", "inv", "idx", "te")}
        ffns = [{k: sem(f"f{n}_{k}") for k in
                 ("T", "xgT", "w1", "w2", "H", "hA", "hV", "Y", "neg", "exp", "v", "y")} | {
                 "g": sems(f"f{n}_g", G_RING), "s": sems(f"f{n}_s", Y_RING)} for n in range(2)]
        b_ = {k: sem(f"b_{k}") for k in
              ("init", "bo", "wvo", "bvr", "st", "mv", "ve", "rs", "xb", "T", "xbT", "pj", "pje", "rp", "qr", "iwe",
               "idx", "rel", "prt", "hs", "s1", "wk", "v", "S", "ttr", "lnb", "exp", "PT", "prT", "PV", "pinv",
               "xbias", "fin", "pc")} | {"x": sems("b_x", 2)}

        def xrows(dram, b, lo, hi):
            return dram[bass.ds(b * S, S), lo:hi].rearrange("(c p) d -> p c d", p=P)

        def tiles(b):
            return bass.ds(b * C, C)

        def experts_of(engine, st):
            at = (st.base // TURN + st.turn) * 8
            _, values = nc.values_load_multi_w_load_instructions(
                te[0:1, bass.ds(at, TURN)], engines=(engine,), min_val=0, max_val=E - 1,
                skip_runtime_bounds_check_because="they were clamped to the last expert when they were written")
            return values

        block = ctx.enter_context(nc.Block())

        @block.sync
        def _(sp):
            per = T // 4
            for g in range(4):
                sp.dma_start(X[:, g * per:(g + 1) * per, :],
                             x[g * per * P:(g + 1) * per * P, :].rearrange("(c p) d -> p c d", p=P)).then_inc(ld_x[g], 16)
                if g == 1:
                    sp.dma_start(cst[:, :], consts).then_inc(ld_c, 16)
                    sp.dma_start(WA[:, :], w_attn).then_inc(ld_w, 16)
                    sp.dma_start(COL[:, :], cols).then_inc(ld_w, 16)
            sp.dma_start(bout_bc[:, :], b_out.partition_broadcast(P)).then_inc(ld_w, 16)
            sp.dma_start(WR[:, :], w_router).then_inc(ld_w, 16)
            for c in range(C):
                sp.dma_start(rowc[:, c * IDX_HEADS:(c + 1) * IDX_HEADS], b_iw).then_inc(ld_w, 16)
                sp.dma_start(rowc[:, C * IDX_HEADS + c * E:C * IDX_HEADS + (c + 1) * E], b_r).then_inc(ld_w, 16)
            sp.dma_start(WB[:, :], w_idx).then_inc(ld_wb, 16)
            sp.dma_start(bo_bc[:, :], b_o.partition_broadcast(P)).then_inc(ld_wb, 16)
            sp.dma_start(WE[:, :, W1_AT:B1_AT], w_experts).then_inc(ld_we, 16)
            sp.dma_start(WE[:, :, B1_AT:B2_AT], b1_cols).then_inc(ld_we, 16)
            sp.dma_start(WE[:, :, B2_AT:W_LEN], b2.partition_broadcast(P)).then_inc(ld_we, 16)

            def store_rows(n, st, lag, x_of):
                t, dram = tails[n], rows_dram[n]
                b, r = st.item(lag), st.slot(lag, 2)
                sp.wait_ge(t["xf"], b + 1)
                sp.dma_start(xrows(dram, b, 0, D), xf[r][:, :, :]).then_inc(t["store"][r], 16)
                sp.wait_ge(t["x"], b + 1)
                sp.dma_start(xrows(dram, b, D, 2 * D), x_of(b, r)).then_inc(t["store"][r], 16)
                sp.wait_ge(t["lg"], b + 1)
                sp.dma_start(xrows(dram, b, 2 * D, ROW), logits[:, tiles(b), :]).then_inc(t["rest"], 16)

            for st in steps(sp, B, 0, 4, 2):
                store_rows(0, st, 0, lambda b, r: X[:, tiles(b), :])
            for st in steps(sp, NT, 0, 2 * TURN, TURN):
                j, r = st.item(0), st.slot(0, Y_RING)
                sp.wait_ge(ffns[0]["y"], j + 1)
                sp.dma_start(x2_dram[bass.ds(j * P, P), :], yo[r][:, :]).then_inc(ffns[0]["s"][r], 16)
            for st in steps(sp, B, 0, 4, 2):
                store_rows(1, st, 0, lambda b, r: x3[r][:, :, :])
            for i in range(Y_RING):
                sp.wait_ge(ffns[1]["s"][i], 16 * len(range(i, NT, Y_RING)))

        @block.gpsimd
        def _(pool):
            pool.memset(eps[:, :], EPS)
            pool.memset(mhalf[:, :, :], -0.5).then_inc(c_half, 1)
            pool.wait_ge(c_half, 1)
            per = T // 4
            for g in range(4):
                cs = slice(g * per, (g + 1) * per)
                pool.wait_ge(a_var, g + 1)
                pool.tensor_tensor(r1[:, :, cs], v1[:, :, cs], mhalf[:, :, :], ALU.pow).then_inc(a_pow, 1)

            def rstd(t, vpe, mv, rs, b, r):
                pool.wait_ge(t["mv"], b + 1)
                after(pool, t["rs"], b)
                pool.tensor_tensor(vpe[:, :], mv[r][:, :, 1], eps[:, :], ALU.add).then_inc(t["ve"], 1)
                pool.wait_ge(t["ve"], b + 1)
                after(pool, t["xf"] if "xf" in t else t["xb"], b - 1)
                pool.tensor_tensor(rs[r][:, :], vpe[:, :], mhalf[:, 0, 0:C], ALU.pow).then_inc(t["rs"], 1)

            pool.wait_ge(ld_w, 128)
            for st in steps(pool, B, 3, 7, 4, ahead=1):
                if st.on(1, B):
                    b, r = st.item(1), st.slot(1, 2)
                    pool.wait_ge(a_pt, b + 1)
                    pool.tensor_tensor(xres[r][:, :, :], xres[r][:, :, :],
                                       bout_bc[:, :].unsqueeze(1).to_broadcast([P, C, D]), ALU.add).then_inc(a_xres, 1)
                if st.on(3, B):
                    rstd(tails[0], vpe3, mv3, rs3, st.item(3), st.slot(3, 2))

            def experts_pool(n):
                f = ffns[n]
                for i in range(2):
                    pool.wait_ge(tails[n]["store"][i], 32 * (B // 2))
                pool.wait_ge(tails[n]["rest"], 16 * B)
                pool.wait_ge(rt["idx"], 3 * n + 2)
                for j in range(NT + G_RING):
                    if j < NT:
                        after(pool, f["y"], j + 1 - G_RING)
                        pool.indirect_dma_start(xg[j % G_RING][:, :], None, rows_dram[n],
                                                bass.IndirectOffsetOnAxis(ap=gidx[:, j:j + 1], axis=0)
                                                ).then_inc(f["g"][j % G_RING], 16)
                    k = j - G_RING
                    if n == 1 and k >= 0:
                        pool.wait_ge(f["y"], k + 1)
                        pool.indirect_dma_start(out, bass.IndirectOffsetOnAxis(ap=sidx[:, k:k + 1], axis=0),
                                                yo[k % Y_RING][:, :], None, bounds_check=TOKENS - 1,
                                                oob_is_err=False).then_inc(f["s"][k % Y_RING], 16)

            experts_pool(0)

            def gather_x(st, lag):
                b, r = st.item(lag), st.slot(lag, 2)
                after(pool, b_["xb"], b - 1)
                after(pool, b_["xbias"], b - 1)
                for c in range(C):
                    after(pool, b_["x"][r], 16 * C * st.lap(lag, 2))
                    pool.tensor_copy(pcur[r][:, c:c + 1], pidx[:, bass.ds(b * C + c, 1)]).then_inc(b_["pc"], 1)
                for c in range(C):
                    alone(pool, b_["pc"], C * b + c + 1, passed["pool"])
                    pool.indirect_dma_start(xin[r][:, c, :], None, x2_dram,
                                            bass.IndirectOffsetOnAxis(ap=pcur[r][:, c:c + 1], axis=0)
                                            ).then_inc(b_["x"][r], 16)

            for i in range(Y_RING):
                pool.wait_ge(ffns[0]["s"][i], 16 * len(range(i, NT, Y_RING)))
            pool.wait_ge(rt["idx"], 3)
            gather_x(Step(0), 0)
            pool.wait_ge(b_["bo"], 1)
            rstd(b_, vpe2, mv2, rs2, 0, 0)
            for st in steps(pool, B, 2, 6, 2, ahead=1):
                b, r = st.item(0), st.slot(0, 2)
                if st.on(-1, B):
                    gather_x(st, -1)
                    rstd(b_, vpe2, mv2, rs2, st.item(-1), st.slot(-1, 2))
                if st.on(0, B):
                    pool.wait_ge(b_["pje"], 8 * b + 7)
                    pool.tensor_tensor(qk[r][:, 0:2, :], qk[r][:, 0:2, :], const("cos").unsqueeze(1).to_broadcast([P, 2, S]),
                                       ALU.mult).then_inc(b_["rp"], 1)
                    pool.tensor_tensor(qk[r][:, 2:4, :], qk[r][:, 2:4, :], const("sin").unsqueeze(1).to_broadcast([P, 2, S]),
                                       ALU.mult).then_inc(b_["rp"], 1)
                    pool.wait_ge(b_["rp"], 2 * (b + 1))
                    after(pool, b_["S"], C * (b - 1))
                    pool.tensor_tensor(qr[r][:, :, :], qk[r][:, 0:2, :], qk[r][:, 2:4, :], ALU.add).then_inc(b_["qr"], 1)
                    after(pool, tails[1]["x"], b - 1)
                    pool.wait_ge(b_["x"][r], 16 * C * (st.lap(0, 2) + 1))
                    pool.tensor_tensor(xbias[r][:, :, :], xin[r], bo_bc[:, :].unsqueeze(1).to_broadcast([P, C, D]),
                                       ALU.add).then_inc(b_["xbias"], 1)
                if st.on(0, B):
                    for c in range(C):
                        pool.wait_ge(b_["prt"], C * b + c + 1)
                        after(pool, b_["s1"], C * (b - 1))
                        pool.tensor_tensor(half_sum[r][:, c, :], part[r][:, c, 0, :], part[r][:, c, 1, :],
                                           ALU.add).then_inc(b_["hs"], 1)
                if st.on(2, B):
                    rstd(tails[1], vpe3, mv3, rs3, st.item(2), st.slot(2, 2))
            experts_pool(1)

        @block.tensor
        def _(pe):
            def router(n, b, r, where):
                t = tails[n]
                pe.wait_ge(t["xfT"], b + 1)
                after(pe, t["lg"], b)
                pe.matmul(where, ones[0:1, :], rowc[:, C * IDX_HEADS:], start=True, stop=False)
                for c in range(C):
                    mm = pe.matmul(where[:, c * E:(c + 1) * E], xfT[r][:, c * P:(c + 1) * P], WR[:, :],
                                   start=False, stop=(c == C - 1))
                mm.then_inc(t["R"], 1)

            def turn_xf(n, b, r, where):
                t = tails[n]
                pe.wait_ge(t["xf"], b + 1)
                after(pe, t["xfT"], b)
                after(pe, t["lg"], b)
                for c in range(C):
                    mm = pe.transpose(where[:, c * P:(c + 1) * P], xf[r][:, c, :], ident)
                mm.then_inc(t["T"], 1)

            pe.wait_ge(ld_c, 16)
            pe.wait_ge(ld_w, 128)
            for st in steps(pe, B, 6, 7, 4, ahead=1):
                b, r = st.item(0), st.slot(0, 2)
                if st.on(0, B):
                    pe.wait_ge(a_xa, b + 1)
                    after(pe, a_xaT, b)
                    for c in range(C):
                        mm = pe.transpose(bank[2][:, c * P:(c + 1) * P], xa[r][:, c, :], ident)
                    mm.then_inc(a_T, 1)
                if st.on(1, B):
                    p, q = st.item(1), st.slot(1, 2)
                    pe.wait_ge(a_exp, p + 1)
                    after(pe, a_ek, p)
                    for c in range(C):
                        mm = pe.transpose(bank[5][:, c * P:(c + 1) * P], ekT[q][:, c * P:(c + 1) * P], ident)
                    mm.then_inc(a_ekT, 1)
                if st.on(2, B):
                    p, q = st.item(2), st.slot(2, 2)
                    pe.wait_ge(a_cm, p + 1)
                    pe.matmul(bank[3][:, D:2 * D], cm[q][:, :], WA[:, 3 * D:4 * D], start=True, stop=True).then_inc(a_G, 1)
                if st.on(6, B):
                    router(0, st.item(6), st.slot(6, 2), bank[6][:, S:S + C * E])
                if st.on(0, B):
                    k = st.slot(0, 4)
                    pe.wait_ge(a_xaT, b + 1)
                    after(pe, a_exp, b)
                    pe.matmul(bank[0][:, 0:S], WA[:, D:2 * D], xaT[k][:, :], start=True, stop=True).then_inc(a_K, 1)
                    after(pe, a_va, b)
                    for c in range(C):
                        mm = pe.matmul(bank[1][:, c * D:(c + 1) * D], xaT[k][:, c * P:(c + 1) * P],
                                       WA[:, 2 * D:3 * D], start=True, stop=True)
                    mm.then_inc(a_V, 1)
                if st.on(2, B):
                    p, q = st.item(2), st.slot(2, 2)
                    pe.wait_ge(a_Gs, p + 1)
                    after(pe, a_Hs, p)
                    pe.matmul(bank[7][:, 0:D], WA[:, 0:D], Gs[q][:, :], start=True, stop=True).then_inc(a_H, 1)
                if st.on(5, B):
                    turn_xf(0, st.item(5), st.slot(5, 2), bank[6])
                if st.on(1, B):
                    p, q = st.item(1), st.slot(1, 2)
                    pe.wait_ge(a_ek, p + 1)
                    pe.wait_ge(a_va, p + 1)
                    after(pe, a_Gs, p)
                    for c in range(C):
                        mm = pe.matmul(bank[3][:, 0:D], va[q][:, c, :], ek[q][:, c, :], start=(c == 0), stop=(c == C - 1))
                    mm.then_inc(a_ctx, 1)
                if st.on(2, B):
                    p, q = st.item(2), st.slot(2, 2)
                    pe.wait_ge(a_Hs, p + 1)
                    after(pe, tails[0]["x"], p)
                    for c in range(C):
                        mm = pe.matmul(bank[4][:, c * D:(c + 1) * D], xaT[st.slot(2, 4)][:, c * P:(c + 1) * P], Hs[q][:, :],
                                       start=True, stop=True)
                    mm.then_inc(a_out, 1)

            def route_tensor(n):
                pe.wait_ge(rt["rtot"], n + 1)
                pe.matmul(bank[0][:, 0:E], const("tri"), rtot[:, :], start=True, stop=True)
                pe.matmul(bank[0][:, E:2 * E], ones, rtot[:, :], start=True, stop=True).then_inc(rt["tot"], 1)
                for c in range(T):
                    if c % 8 == 0:
                        pe.wait_ge(rt["slots"], 5 * n + c // 8 + 2)
                    mm = pe.matmul(bank[1][:, 0:2 * NT], oneh_slot[:, c, :],
                                   oneh_tile[:, c, :, :].rearrange("p a b -> p (a b)"), start=(c == 0), stop=(c == T - 1))
                mm.then_inc(rt["inv"], 1)

            def experts_tensor(n):
                f = ffns[n]
                pe.wait_ge(rt["idx"], 3 * n + 2)
                for st in steps(pe, NT, 2, 2 * TURN, TURN):
                    if st.on(0, NT):
                        j, r, g = st.item(0), st.slot(0, 2), st.slot(0, G_RING)
                        pe.wait_ge(f["g"][g], 16 * (st.lap(0, G_RING) + 1))
                        after(pe, f["xgT"], j - 1)
                        pe.transpose(bank[6 + r][:, 0:P], xg[g][:, 0:D], ident).then_inc(f["T"], 1)
                    if st.on(1, NT):
                        j, r = st.item(1), st.slot(1, 2)
                        pe.wait_ge(f["xgT"], j + 1)
                        pe.wait_ge(f["w1"], j + 1)
                        after(pe, f["hA"], 2 * (j - 1))
                        after(pe, f["hV"], 2 * (j - 1))
                        for k in range(FC):
                            mm = pe.matmul(bank[r + 2 * (k // 2)][:, k % 2 * P:(k % 2 + 1) * P],
                                           w1[r][:, k * P:(k + 1) * P], xgT[r][:, :], start=True, stop=True)
                            if k % 2:
                                mm.then_inc(f["H"], 1)
                    if st.on(2, NT):
                        j, r = st.item(2), st.slot(2, 2)
                        pe.wait_ge(f["hA"], 2 * (j + 1))
                        pe.wait_ge(f["hV"], 2 * (j + 1))
                        pe.wait_ge(f["w2"], j + 1)
                        after(pe, f["y"], j - 1)
                        for k in range(FC):
                            mm = pe.matmul(bank[4 + r][:, 0:D], hT[r][:, k, :], w2[r][:, k * D:(k + 1) * D],
                                           start=(k == 0), stop=(k == FC - 1))
                        mm.then_inc(f["Y"], 1)

            route_tensor(0)
            experts_tensor(0)

            pe.wait_ge(ffns[0]["y"], NT)
            pe.wait_ge(ld_wb, 32)
            pe.wait_ge(b_["bvr"], 1)
            pe.matmul(bank[2][:, 0:D], WB[:, 8 * D:9 * D], WB[:, 7 * D:8 * D], start=True, stop=True)
            pe.matmul(bank[3][:, 0:D], bv_rep[:, :], WB[:, 7 * D:8 * D], start=True, stop=True).then_inc(b_["wvo"], 1)
            pe.wait_ge(b_["init"], 1)
            pe.wait_ge(b_["bo"], 1)
            half = [bank[2][:, 0:S], bank[3][:, 0:S]]
            for st in steps(pe, B, 3, 6, 2, ahead=1):
                if st.on(0, B):
                    b, r = st.item(0), st.slot(0, 2)
                    pe.wait_ge(b_["xb"], b + 1)
                    after(pe, b_["iwe"], b)
                    after(pe, tails[1]["lg"], b - 3)
                    for c in range(C):
                        mm = pe.transpose(bank[5][:, c * P:(c + 1) * P], xb[r][:, c, :], ident)
                    mm.then_inc(b_["T"], 1)
                if st.on(1, B):
                    b, r = st.item(1), st.slot(1, 2)
                    pe.wait_ge(b_["qr"], b + 1)
                    after(pe, b_["ttr"], C * b)
                    for c in range(C):
                        pe.matmul(bank[6][:, c * S:(c + 1) * S], qr[r][:, 0, c * P:(c + 1) * P], qr[r][:, 1, :],
                                  start=True, stop=True).then_inc(b_["S"], 1)

                def project(lo, hi):
                    b, r = st.item(0), st.slot(0, 2)
                    for i in range(lo, hi):
                        after(pe, b_["pje"], 8 * b + i - 1)
                        pe.matmul(half[i % 2], WB[:, i * D:(i + 1) * D], xbT[r][:, :], start=True, stop=True).then_inc(b_["pj"], 1)

                if st.on(0, B):
                    pe.wait_ge(b_["xbT"], st.item(0) + 1)
                    project(0, 4)
                if st.on(2, B):
                    b, r = st.item(2), st.slot(2, 2)
                    after(pe, b_["prT"], b)
                    for c in range(C):
                        pe.wait_ge(b_["exp"], C * b + c + 1)
                        for k in range(C):
                            mm = pe.transpose(bank[4][:, c * S + k * P:c * S + (k + 1) * P], pr[r][:, c, k * P:(k + 1) * P], ident)
                    mm.then_inc(b_["PT"], 1)
                if st.on(0, B):
                    b, r = st.item(0), st.slot(0, 2)
                    project(4, 7)
                    pe.matmul(bank[5][:, S:S + C * IDX_HEADS], ones[0:1, :], rowc[:, 0:C * IDX_HEADS], start=True, stop=False)
                    for c in range(C):
                        mm = pe.matmul(bank[5][:, S + c * IDX_HEADS:S + (c + 1) * IDX_HEADS], xbT[r][:, c * P:(c + 1) * P],
                                       WB[:, 9 * D:9 * D + IDX_HEADS], start=False, stop=(c == C - 1))
                    mm.then_inc(b_["pj"], 1)

                def index_scores(c):
                    b, r = st.item(0), st.slot(0, 2)
                    for h in range(IDX_HEADS):
                        lo = IDX_DIM * (h % 2)
                        if h < 2:
                            after(pe, b_["rel"], 2 * (C * b + c - 1) + h + 1)
                        mm = pe.matmul(bank[h % 2][:, h // 2 * S:(h // 2 + 1) * S],
                                       iq[r][lo:lo + IDX_DIM, h // 2, c * P:(c + 1) * P], ik[r][lo:lo + IDX_DIM, :],
                                       start=True, stop=True)
                        if h >= 2:
                            mm.then_inc(b_["idx"], 1)

                if st.on(0, B):
                    index_scores(0)
                if st.on(2, B):
                    b, r = st.item(2), st.slot(2, 2)
                    pe.wait_ge(b_["prT"], b + 1)
                    after(pe, tails[1]["x"], b)
                    for c in range(C):
                        for k in range(C):
                            mm = pe.matmul(bank[7][:, c * D:(c + 1) * D], prT[r][:, c, k * P:(k + 1) * P], vb[r][:, k, :],
                                           start=(k == 0), stop=(k == C - 1))
                        mm.then_inc(b_["PV"], 1)
                if st.on(0, B):
                    b, r = st.item(0), st.slot(0, 2)
                    pe.wait_ge(b_["pje"], 8 * b + 6)
                    for c in range(C):
                        mm = pe.matmul(half[1][:, c * D:(c + 1) * D], xbT[r][:, c * P:(c + 1) * P], WVO[:, :],
                                       start=True, stop=True)
                    mm.then_inc(b_["pj"], 1)
                if st.on(3, B):
                    pe.wait_ge(b_["iwe"], st.item(0) + 1 if st.on(0, B) else B)
                    turn_xf(1, st.item(3), st.slot(3, 2), bank[5][:, 0:S])
                if st.on(0, B):
                    index_scores(1)
                if st.on(3, B):
                    router(1, st.item(3), st.slot(3, 2), bank[5][:, S + C * IDX_HEADS:S + C * IDX_HEADS + C * E])
            route_tensor(1)
            experts_tensor(1)

        @block.scalar
        def _(act):
            def xf_out(n, b, r, where):
                t = tails[n]
                act.wait_ge(t["T"], b + 1)
                after(act, t["R"], b - 1)
                act.activation(xfT[r][:, :], where, ACT.Copy).then_inc(t["xfT"], 1)

            def logits_out(n, b, where):
                t = tails[n]
                act.wait_ge(t["R"], b + 1)
                act.activation(logits[:, tiles(b), :], where.rearrange("p (c e) -> p c e", c=C), ACT.Copy).then_inc(t["lg"], 1)

            act.preload_act_table(ACT.Exp)
            act.wait_ge(ld_w, 128)
            act.wait_ge(a_coef, 4)
            for st in steps(act, B, 6, 7, 4, ahead=1):
                b, r = st.item(0), st.slot(0, 2)
                if st.on(0, B):
                    k = st.slot(0, 4)
                    act.wait_ge(a_T, b + 1)
                    after(act, a_out, b - 3)
                    act.activation(xaT[k][:, :], bank[2][:, 0:S], ACT.Identity, scale=COL[:, 0:1],
                                   bias=COL[:, 1:2]).then_inc(a_xaT, 1)
                if st.on(1, B):
                    p, q = st.item(1), st.slot(1, 2)
                    act.wait_ge(a_ekT, p + 1)
                    after(act, a_ctx, p - 1)
                    act.activation(ek[q][:, :, :], bank[5][:, 0:S].rearrange("p (c d) -> p c d", c=C), ACT.Copy).then_inc(a_ek, 1)
                if st.on(6, B):
                    logits_out(0, st.item(6), bank[6][:, S:S + C * E])
                if st.on(2, B):
                    p, q = st.item(2), st.slot(2, 2)
                    act.wait_ge(a_H, p + 1)
                    after(act, a_out, p - 1)
                    act.activation(Hs[q][:, :], bank[7][:, 0:D], ACT.Copy).then_inc(a_Hs, 1)
                if st.on(0, B):
                    act.wait_ge(a_kneg, b + 1)
                    after(act, a_ekT, b - 1)
                    after(act, a_einv, b - 3)
                    act.activation(ekT[r][:, :], bank[0][:, 0:S], ACT.Exp, bias=kneg[r][:, :],
                                   accum_out=esum[k][:, :]).then_inc(a_exp, 1)
                    act.wait_ge(a_V, b + 1)
                    after(act, a_ctx, b - 1)
                    act.activation(va[r][:, :, :], bank[1][:, 0:S].rearrange("p (c d) -> p c d", c=C),
                                   ACT.Copy).then_inc(a_va, 1)
                if st.on(5, B):
                    xf_out(0, st.item(5), st.slot(5, 2), bank[6][:, 0:S])
                if st.on(1, B):
                    p, q = st.item(1), st.slot(1, 2)
                    after(act, tails[0]["x"], p - 1)
                    for c in range(C):
                        at = bass.ds(p * C + c, 1)
                        ins = act.activation(xres[q][:, c, :], X[:, at, :].rearrange("p a d -> p (a d)"), ACT.Identity,
                                             scale=xs[:, 0, at], bias=xs[:, 1, at])
                    ins.then_inc(a_pt, 1)

            def route_scalar(n):
                act.wait_ge(rt["sub"], n + 1)
                act.activation(r_b[:, :, :], r_a[:, :, :], ACT.Exp).then_inc(rt["exp"], 1)

            def experts_scalar(n):
                f = ffns[n]
                if n == 0:
                    act.wait_ge(ld_we, 48)
                act.wait_ge(rt["te"], n + 1)
                act.preload_act_table(ACT.Exp)
                for st in steps(act, NT, 2, 2 * TURN, TURN):
                    if st.base % TURN == 0 and st.on(0, NT):
                        experts = experts_of(mybir.EngineType.Activation, st)
                    if st.on(0, NT):
                        j, r = st.item(0), st.slot(0, 2)
                        after(act, f["H"], 2 * (j - 1))
                        act.activation(w1[r][:, :], WE[:, bass.ds(experts[st.base % TURN], 1), W1_AT:W1_AT + F
                                                       ].rearrange("p a w -> p (a w)"), ACT.Copy).then_inc(f["w1"], 1)
                        act.wait_ge(f["T"], j + 1)
                        act.activation(xgT[r][:, :], bank[6 + r][:, 0:P], ACT.Copy).then_inc(f["xgT"], 1)
                    if st.on(1, NT):
                        j, r = st.item(1), st.slot(1, 2)
                        act.wait_ge(f["w2"], j + 1)
                        act.wait_ge(f["H"], 2 * j + 1)
                        for k in range(FC // 2):
                            act.activation(hT[r][:, k, :], bank[r][:, k * P:(k + 1) * P], ACT.Relu,
                                           bias=w2[r][:, F + k:F + k + 1]).then_inc(f["hA"], 1)
                    if st.on(0, NT):
                        j, r, g = st.item(0), st.slot(0, 2), st.slot(0, G_RING)
                        act.wait_ge(f["neg"], j + 1)
                        after(act, f["y"], j + 1 - Y_RING)
                        act.activation(lexp[r][:, :], xg[g][:, 2 * D:ROW], ACT.Exp, bias=lneg[r][:, :],
                                       accum_out=lsum[st.slot(0, Y_RING)][:, :]).then_inc(f["exp"], 1)

            route_scalar(0)
            experts_scalar(0)

            act.wait_ge(b_["wvo"], 1)
            act.activation(WVO[:, :], bank[2][:, 0:D], ACT.Copy).then_inc(b_["init"], 1)
            act.preload_act_table(ACT.Exp)
            half = [bank[2][:, 0:S], bank[3][:, 0:S]]
            scale = float(D) ** -0.5
            for st in steps(act, B, 3, 6, 2, ahead=1):
                b, r = st.item(0), st.slot(0, 2)

                def projected(lo, hi):
                    for i in range(lo, hi):
                        act.wait_ge(b_["pj"], 9 * b + i + 1)
                        if i == 3:
                            after(act, b_["qr"], b - 1)
                        dst = iq[r][:, i, :] if i < 2 else ik[r][:, :] if i == 2 else qk[r][:, (0, 2, 1, 3)[i - 3], :]
                        act.activation(dst, half[i % 2], ACT.Identity, bias=COL[:, 2 + i:3 + i]).then_inc(b_["pje"], 1)

                if st.on(0, B):
                    act.wait_ge(b_["T"], b + 1)
                    after(act, b_["idx"], 2 * C * (b - 1))
                    act.activation(xbT[r][:, :], bank[5][:, 0:S], ACT.Copy).then_inc(b_["xbT"], 1)
                if st.on(2, B):
                    p, q = st.item(2), st.slot(2, 2)
                    for c in range(C):
                        act.wait_ge(b_["lnb"], C * p + c + 1)
                        after(act, b_["pinv"], p - 1)
                        act.activation(pr[q][:, c, :], lg[q][:, c, :], ACT.Exp, bias=lnb[q][:, c:c + 1], scale=scale,
                                       accum_out=psm[q][:, c:c + 1]).then_inc(b_["exp"], 1)
                if st.on(0, B):
                    projected(0, 4)
                if st.on(2, B):
                    act.wait_ge(b_["PT"], p + 1)
                    after(act, b_["PV"], C * (p - 1))
                    act.activation(prT[q][:, :, :], bank[4][:, :].rearrange("p (c k) -> p c k", c=C), ACT.Copy).then_inc(b_["prT"], 1)
                if st.on(0, B):
                    projected(4, 7)
                    act.wait_ge(b_["pj"], 9 * b + 8)
                    after(act, b_["wk"], C * (b - 1))
                    act.activation(iw[r][:, :, :],
                                   bank[5][:, S:S + C * IDX_HEADS].rearrange("p (c h) -> p c h", c=C),
                                   ACT.Copy).then_inc(b_["iwe"], 1)
                    after(act, b_["hs"], C * (b - 1))
                    act.wait_ge(b_["iwe"], b + 1)
                for c in range(C):
                    if st.on(0, B):
                        for i in range(2):
                            act.wait_ge(b_["idx"], 2 * (C * b + c) + i + 1)
                            act.activation(rel[r][:, c, i::2, :],
                                           bank[i][:, :].rearrange("p (h k) -> p h k", h=2), ACT.Relu).then_inc(b_["rel"], 1)
                        act.wait_ge(b_["rel"], 2 * (C * b + c + 1))
                        for h in range(2):
                            ins = act.activation(part[r][:, c, h, :], rel[r][:, c, h, :], ACT.Copy,
                                                 scale=iw[r][:, c, h:h + 1])
                        ins.then_inc(b_["prt"], 1)
                        if c == 0:
                            act.wait_ge(b_["pj"], 9 * (b + 1))
                            after(act, b_["PV"], C * (b - 1))
                            act.activation(vb[r][:, :, :], half[1].rearrange("p (c d) -> p c d", c=C), ACT.Copy).then_inc(b_["pje"], 1)
                    if c == 0 and st.on(3, B):
                        xf_out(1, st.item(3), st.slot(3, 2), bank[5][:, 0:S])
                if st.on(3, B):
                    logits_out(1, st.item(3), bank[5][:, S + C * IDX_HEADS:S + C * IDX_HEADS + C * E])
            route_scalar(1)
            experts_scalar(1)

        @block.vector
        def _(dve):
            def stats(t, x_of, stat, mv, b, r, free, count):
                spread(t, x_of, stat)
                aggregate(t, stat, mv, b, r, free, count)

            def spread(t, x_of, stat):
                for c in range(C):
                    ins = dve.bn_stats(stat[:, c, :], x_of(c))
                ins.then_inc(t["st"], 1)

            def aggregate(t, stat, mv, b, r, free, count):
                alone(dve, t["st"], b + 1, passed["dve"])
                alone(dve, free, count, passed["dve"])
                for c in range(C):
                    ins = dve.bn_aggr(mv[r][:, c, :], stat[:, c, :])
                ins.then_inc(t["mv"], 1)

            def normalise(t, key, x_of, dst, mv, rs, b, r):
                dve.wait_ge(t["rs"], b + 1)
                dve.wait_ge(t["mv"], b + 1)
                for c in range(C):
                    ins = dve.tensor_scalar(dst[:, c, :], x_of(c), mv[r][:, c, 0:1], rs[r][:, c:c + 1],
                                            ALU.subtract, ALU.mult)
                ins.then_inc(t[key], 1)

            def one_tile(b, c):
                return X[:, bass.ds(b * C + c, 1), :].rearrange("p a d -> p (a d)")

            per = T // 4

            def coefficients(g):
                cs = slice(g * per, (g + 1) * per)
                dve.wait_ge(a_pow, g + 1)
                dve.tensor_scalar(xs[:, 0, cs], r1[:, 0, cs], 1.0, None, ALU.add)
                dve.scalar_tensor_tensor(xs[:, 1, cs], mv1[:, cs, 0], -1.0, r1[:, 0, cs], ALU.mult, ALU.mult).then_inc(a_coef, 1)

            for g in range(4):
                cs = slice(g * per, (g + 1) * per)
                dve.wait_ge(ld_x[g], 16)
                for c in range(g * per, (g + 1) * per):
                    ins = dve.bn_stats(stat1[:, c, :], X[:, c, :])
                ins.then_inc(a_stat, 1)
                dve.wait_ge(a_stat, 2 * g + 1)
                for c in range(g * per, (g + 1) * per):
                    ins = dve.bn_aggr(mv1[:, c, :], stat1[:, c, :])
                ins.then_inc(a_stat, 1)
                dve.wait_ge(a_stat, 2 * g + 2)
                dve.tensor_scalar(v1[:, 0, cs], mv1[:, cs, 1], EPS, None, ALU.add)
                dve.tensor_scalar(v1[:, 1, cs], mv1[:, cs, 1], 1.0 + EPS, EPS * EPS, ALU.mult, ALU.add).then_inc(a_var, 1)
                if g >= 1:
                    coefficients(g - 1)
            coefficients(3)

            def twice_normal(b, r):
                after(dve, a_T, b - 1)
                for c in range(C):
                    at = bass.ds(b * C + c, 1)
                    ins = dve.tensor_scalar(xa[r][:, c, :], one_tile(b, c), mv1[:, at, 0], r1[:, 1, at],
                                            ALU.subtract, ALU.mult)
                ins.then_inc(a_xa, 1)

            dve.wait_ge(ld_c, 16)
            twice_normal(0, 0)
            for st in steps(dve, B, 4, 7, 4, ahead=1):
                b, r = st.item(0), st.slot(0, 2)
                if st.on(2, B):
                    p, q = st.item(2), st.slot(2, 2)
                    dve.wait_ge(a_exp, p + 1)
                    after(dve, a_Gs, p - 1)
                    dve.reciprocal(einv[q][:, :], esum[st.slot(2, 4)][:, :]).then_inc(a_einv, 1)
                if st.on(3, B):
                    n, m = st.item(3), st.slot(3, 2)
                    alone(dve, tails[0]["x"], n + 1, passed["dve"])
                    alone(dve, tails[0]["mv"], n, passed["dve"])
                    spread(tails[0], lambda c: one_tile(n, c), stat3)
                if st.on(2, B):
                    dve.wait_ge(a_G, p + 1)
                    dve.wait_ge(a_einv, p + 1)
                    after(dve, a_H, p - 1)
                    dve.tensor_scalar(Gs[q][:, :], bank[3][:, D:2 * D], einv[q][:, :], float(DIM_HEAD) ** -0.5,
                                      ALU.mult, ALU.mult).then_inc(a_Gs, 1)
                if st.on(3, B):
                    aggregate(tails[0], stat3, mv3, n, m, tails[0]["xf"], n - 1)
                if st.on(0, B):
                    dve.wait_ge(a_K, b + 1)
                    after(dve, a_exp, b - 1)
                    dve.tensor_reduce(kneg[r][:, :], bank[0][:, 0:S], AX.X, ALU.max, negate=True).then_inc(a_kneg, 1)
                if st.on(-1, B):
                    twice_normal(st.item(-1), st.slot(-1, 2))
                if st.on(4, B):
                    n, m = st.item(4), st.slot(4, 2)
                    after(dve, tails[0]["store"][m], 32 * st.lap(4, 2))
                    after(dve, tails[0]["T"], n - 1)
                    normalise(tails[0], "xf", lambda c: one_tile(n, c), xf[m], mv3, rs3, n, m)
                if st.on(1, B):
                    p, q = st.item(1), st.slot(1, 2)
                    dve.wait_ge(a_ctx, p + 1)
                    after(dve, a_G, p - 1)
                    dve.tensor_tensor(cm[q][:, :], bank[3][:, 0:D], const("blocks"), ALU.mult).then_inc(a_cm, 1)
                if st.on(2, B):
                    p, q = st.item(2), st.slot(2, 2)
                    dve.wait_ge(a_out, p + 1)
                    dve.wait_ge(a_xres, p + 1)
                    dve.tensor_tensor(X[:, tiles(p), :], bank[4][:, 0:S].rearrange("p (c d) -> p c d", c=C),
                                      xres[q][:, :, :], ALU.add).then_inc(tails[0]["x"], 1)

            def route_vector(n):
                count = 100 * n

                def link(ins):
                    nonlocal count
                    count += 1
                    ins.then_inc(rt["v"], 1)
                    dve.wait_ge(rt["v"], count)

                if n == 0:
                    link(dve.tensor_copy(colbf[:, :], const("col")))
                dve.wait_ge(tails[n]["lg"], B)
                v = lambda k: r_m[:, k, :]
                over_e = lambda a: a.unsqueeze(2).to_broadcast([P, T, E])
                link(dve.tensor_reduce(v(0), logits[:, :, :], AX.X, ALU.max))
                dve.tensor_tensor(r_a[:, :, :], logits[:, :, :], over_e(v(0)), ALU.subtract).then_inc(rt["sub"], 1)
                dve.wait_ge(rt["exp"], n + 1)
                link(dve.tensor_reduce(v(1), r_b[:, :, :], AX.X, ALU.max))
                link(dve.tensor_tensor(r_a[:, :, :], r_b[:, :, :], over_e(v(1)), ALU.is_equal))
                link(dve.tensor_tensor(r_b[:, :, :], r_a[:, :, :], const("down").unsqueeze(1).to_broadcast([P, T, E]), ALU.mult))
                link(dve.tensor_reduce(v(2), r_b[:, :, :], AX.X, ALU.max))
                link(dve.tensor_tensor(oh[:, :, :].rearrange("p e t -> p t e"), r_b[:, :, :], over_e(v(2)), ALU.is_equal))
                link(dve.tensor_tensor_scan(incl[:, :, :].rearrange("p e t -> p (e t)"), const("keep"),
                                            oh[:, :, :].rearrange("p e t -> p (e t)"), 0.0, ALU.mult, ALU.add))
                dve.tensor_copy(rtot[:, :], incl[:, :, T - 1]).then_inc(rt["rtot"], 1)
                dve.wait_ge(rt["tot"], n + 1)
                over_t = lambda a: a.unsqueeze(2).to_broadcast([P, E, T])
                link(dve.tensor_copy(nt[:, 0, :], bank[0][:, 0:E]))
                link(dve.tensor_tensor(rr[:, :, :], over_t(bank[0][:, E:2 * E]),
                                       const("starts").unsqueeze(1).to_broadcast([P, E, T]), ALU.is_gt))
                link(dve.tensor_reduce(nt[:, 1, :], rr[:, :, :], AX.X, ALU.add))
                link(dve.tensor_tensor_scan(nt[:, 2, :], ones[:, 0:E], nt[:, 1, :], 0.0, ALU.mult, ALU.add))
                link(dve.tensor_tensor(rr[:, :, :], incl[:, :, :], over_t(nt[:, 0, :]), ALU.add))
                link(dve.tensor_tensor(rr[:, :, :], rr[:, :, :], oh[:, :, :], ALU.mult))
                link(dve.tensor_reduce(v(3), rr[:, :, :].rearrange("p e t -> p t e"), AX.X, ALU.add))
                link(dve.tensor_tensor(nt[:, 1, :], nt[:, 2, :], nt[:, 1, :], ALU.subtract))
                link(dve.tensor_tensor(rr[:, :, :], oh[:, :, :], over_t(nt[:, 1, :]), ALU.mult))
                link(dve.tensor_reduce(v(4), rr[:, :, :].rearrange("p e t -> p t e"), AX.X, ALU.add))
                link(dve.tensor_scalar(v(5), v(3), 1.0 / P, -(P / 2 + 0.5) / P, ALU.mult, ALU.add))
                link(dve.tensor_scalar(v(5), v(5), MAGIC, MAGIC, ALU.add, ALU.subtract))
                link(dve.tensor_tensor(v(4), v(4), v(5), ALU.add))
                link(dve.scalar_tensor_tensor(v(6), v(5), float(-P), v(3), ALU.mult, ALU.add))
                by_tile = lambda k: oneh_tile[:, :, k, :]
                link(dve.tensor_tensor(by_tile(1), const("tile").unsqueeze(1).to_broadcast([P, T, NT]),
                                       v(4).unsqueeze(2).to_broadcast([P, T, NT]), ALU.is_equal))
                link(dve.tensor_scalar(by_tile(0), by_tile(1), const("part1"), None, ALU.mult))
                dve.tensor_tensor(by_tile(1), by_tile(1), colbf[:, :].unsqueeze(2).to_broadcast([P, T, NT]),
                                  ALU.mult).then_inc(rt["slots"], 1)
                for g in range(4):
                    cs = slice(g * per, (g + 1) * per)
                    dve.tensor_tensor(oneh_slot[:, cs, :], const("slot1").unsqueeze(1).to_broadcast([P, per, P]),
                                      r_m[:, 6, cs].unsqueeze(2).to_broadcast([P, per, P]), ALU.is_equal).then_inc(rt["slots"], 1)
                link(dve.tensor_tensor(tef[:, :, :], const("turns")[0:1, :].unsqueeze(2).to_broadcast([1, TE_LEN, E]),
                                       nt[0:1, 2, :].unsqueeze(1).to_broadcast([1, TE_LEN, E]), ALU.is_ge))
                link(dve.tensor_reduce(tes[:, :], tef[:, :, :], AX.X, ALU.add))
                dve.tensor_scalar(te[:, :], tes[:, :], float(E - 1), None, ALU.min).then_inc(rt["te"], 1)
                dve.wait_ge(rt["inv"], n + 1)
                link(dve.tensor_scalar(idxf[:, 0, :], bank[1][:, 0:NT], -1.0, None, ALU.add))
                link(dve.scalar_tensor_tensor(idxf[:, 1, :], bank[1][:, NT:2 * NT], float(P), idxf[:, 0, :], ALU.mult, ALU.add))
                dve.tensor_scalar(gidx[:, :], idxf[:, 1, :], 0.0, None, ALU.max).then_inc(rt["idx"], 1)
                link(dve.tensor_scalar(idxf[:, 2, :], idxf[:, 1, :], 0.0, float(2 * TOKENS), ALU.is_lt, ALU.mult))
                dve.tensor_tensor(sidx[:, :], idxf[:, 1, :], idxf[:, 2, :], ALU.add).then_inc(rt["idx"], 1)
                if n == 0:
                    link(dve.scalar_tensor_tensor(v(7), v(4), float(P), v(6), ALU.mult, ALU.add))
                    dve.tensor_scalar(pidx[:, :], v(7), -1.0, None, ALU.add).then_inc(rt["idx"], 1)
                    dve.sem_inc(rt["v"], 100 - count)

            def experts_vector(n):
                f = ffns[n]
                if n == 0:
                    dve.wait_ge(ld_we, 48)
                dve.wait_ge(rt["te"], n + 1)
                for st in steps(dve, NT, 2, 2 * TURN, TURN):
                    if st.base % TURN == 0 and st.on(0, NT):
                        experts = experts_of(mybir.EngineType.DVE, st)
                    if st.on(1, NT):
                        j, r = st.item(1), st.slot(1, 2)
                        dve.wait_ge(f["w2"], j + 1)
                        dve.wait_ge(f["H"], 2 * (j + 1))
                        for k in range(FC // 2, FC):
                            dve.tensor_scalar(hT[r][:, k, :], bank[2 + r][:, k % 2 * P:(k % 2 + 1) * P], w2[r][:, F + k:F + k + 1], 0.0,
                                              ALU.add, ALU.max).then_inc(f["hV"], 1)
                    if st.on(2, NT):
                        j, r, g, o = st.item(2), st.slot(2, 2), st.slot(2, G_RING), st.slot(2, Y_RING)
                        dve.wait_ge(f["exp"], j + 1)
                        after(dve, f["y"], j)
                        dve.reciprocal(gate[:, :], lsum[o][:, :]).then_inc(f["v"], 1)
                        dve.wait_ge(f["Y"], j + 1)
                        dve.tensor_tensor(yb[:, :], bank[4 + r][:, 0:D], w2[r][:, F + FC:F + FC + D], ALU.add).then_inc(f["v"], 1)
                    if st.on(0, NT):
                        j, r, g = st.item(0), st.slot(0, 2), st.slot(0, G_RING)
                        dve.wait_ge(f["g"][g], 16 * (st.lap(0, G_RING) + 1))
                        after(dve, f["exp"], j - 1)
                        dve.tensor_reduce(lneg[r][:, :], xg[g][:, 2 * D:ROW], AX.X, ALU.max, negate=True).then_inc(f["neg"], 1)
                        after(dve, f["v"], 2 * (j - 1))
                        dve.tensor_copy(w2[r][:, :], WE[:, bass.ds(experts[st.base % TURN], 1), W2_AT:W_LEN
                                                        ].rearrange("p a w -> p (a w)")).then_inc(f["w2"], 1)
                    if st.on(2, NT):
                        j, g, o = st.item(2), st.slot(2, G_RING), st.slot(2, Y_RING)
                        dve.wait_ge(f["v"], 2 * (j + 1))
                        after(dve, f["s"][o], 16 * st.lap(2, Y_RING))
                        dve.scalar_tensor_tensor(yo[o][:, :], yb[:, :], gate[:, :], xg[g][:, D:2 * D],
                                                 ALU.mult, ALU.add).then_inc(f["y"], 1)

            route_vector(0)
            experts_vector(0)

            dve.wait_ge(ld_wb, 32)
            dve.tensor_scalar(bv_rep[:, :], ones, COL[:, 9:10], None, ALU.mult).then_inc(b_["bvr"], 1)
            dve.wait_ge(b_["wvo"], 1)
            dve.tensor_tensor(bo_bc[:, :], bank[3][:, 0:D], bo_bc[:, :], ALU.add).then_inc(b_["bo"], 1)

            def stats_b(st, lag):
                b, r = st.item(lag), st.slot(lag, 2)
                alone(dve, b_["x"][r], 16 * C * (st.lap(lag, 2) + 1), passed["dve"])
                stats(b_, lambda c: xin[r][:, c, :], stat2, mv2, b, r, b_["xb"], b - 1)

            def normalise_b(b, r):
                after(dve, b_["T"], b - 1)
                normalise(b_, "xb", lambda c: xin[r][:, c, :], xb[r], mv2, rs2, b, r)

            stats_b(Step(0), 0)
            normalise_b(0, 0)
            scale = float(D) ** -0.5
            for st in steps(dve, B, 3, 6, 2, ahead=1):
                if st.on(1, B):
                    b, r = st.item(1), st.slot(1, 2)
                    for c in range(C):
                        dve.wait_ge(b_["hs"], C * b + c + 1)
                        dve.scalar_tensor_tensor(wk[:, c, :], rel[r][:, c, 2, :], iw[r][:, c, 2:3], half_sum[r][:, c, :],
                                                 ALU.mult, ALU.add).then_inc(b_["s1"], 1)
                    for c in range(C):
                        dve.wait_ge(b_["s1"], C * b + c + 1)
                        dve.scalar_tensor_tensor(wk[:, c, :], rel[r][:, c, 3, :], iw[r][:, c, 3:4], wk[:, c, :],
                                                 ALU.mult, ALU.add).then_inc(b_["wk"], 1)
                    rounds = TOP_K // 8
                    for i in range(rounds):
                        for c in range(C):
                            if i == 0:
                                alone(dve, b_["wk"], C * b + c + 1, passed["dve"])
                            else:
                                alone(dve, b_["v"], 2 * C * (rounds * b + i - 1) + C + c + 1, passed["dve"])
                            dve.max(m8[:, c, :], wk[:, c, :]).then_inc(b_["v"], 1)
                        for c in range(C):
                            alone(dve, b_["v"], 2 * C * (rounds * b + i) + c + 1, passed["dve"])
                            dve.match_replace(wk[:, c, :], m8[:, c, :], wk[:, c, :], NEG).then_inc(b_["v"], 1)
                if st.on(-1, B):
                    stats_b(st, -1)
                if st.on(1, B):
                    for c in range(C):
                        dve.wait_ge(b_["v"], 2 * C * (rounds * (b + 1) - 1) + C + c + 1)
                        dve.tensor_scalar(pen[:, c, :], wk[:, c, :], -1.0e38, -1.0e30, ALU.is_gt, ALU.mult).then_inc(b_["fin"], 1)
                    for c in range(C):
                        alone(dve, b_["fin"], C * b + c + 1, passed["dve"])
                        alone(dve, b_["S"], C * (b + 1), passed["dve"])
                        alone(dve, b_["PT"], b - 1, passed["dve"])
                        dve.tensor_tensor_reduce(lg[r][:, c, :], bank[6][:, c * S:(c + 1) * S], pen[:, c, :], 1.0, -3.0e38,
                                                 ALU.add, ALU.max, lmax[:, c:c + 1]).then_inc(b_["ttr"], 1)
                    for c in range(C):
                        dve.wait_ge(b_["ttr"], C * b + c + 1)
                        dve.tensor_scalar(lnb[r][:, c:c + 1], lmax[:, c:c + 1], -scale, None, ALU.mult).then_inc(b_["lnb"], 1)
                if st.on(3, B):
                    b, r = st.item(3), st.slot(3, 2)
                    after(dve, tails[1]["T"], b - 1)
                    after(dve, tails[1]["store"][r], 32 * st.lap(3, 2))
                    normalise(tails[1], "xf", lambda c: x3[r][:, c, :], xf[r], mv3, rs3, b, r)
                if st.on(-1, B):
                    normalise_b(st.item(-1), st.slot(-1, 2))
                if st.on(2, B):
                    b, r = st.item(2), st.slot(2, 2)
                    dve.wait_ge(b_["exp"], C * (b + 1))
                    dve.reciprocal(pinv[:, :], psm[r][:, :]).then_inc(b_["pinv"], 1)
                    dve.wait_ge(b_["pinv"], b + 1)
                    dve.wait_ge(b_["PV"], C * (b + 1))
                    dve.wait_ge(b_["xbias"], b + 1)
                    after(dve, tails[1]["store"][r], 32 * st.lap(2, 2))
                    for c in range(C):
                        ins = dve.scalar_tensor_tensor(x3[r][:, c, :], bank[7][:, c * D:(c + 1) * D], pinv[:, c:c + 1],
                                                       xbias[r][:, c, :], ALU.mult, ALU.add)
                    ins.then_inc(tails[1]["x"], 1)
                    alone(dve, tails[1]["x"], b + 1, passed["dve"])
                    stats(tails[1], lambda c: x3[r][:, c, :], stat3, mv3, b, r, tails[1]["xf"], b - 1)
            route_vector(1)
            experts_vector(1)


def kernel(**inputs):
    import concourse.bacc as bacc
    from concourse.bass_utils import run_bass_kernel_spmd

    a = {k: np.asarray(v) for k, v in inputs.items()}

    def row(v):
        return np.ascontiguousarray(v).reshape(1, -1)

    w = a["L0_attn_a_w_qkv"]
    w_attn = np.concatenate([w[:, :D].T, w[:, D:2 * D], w[:, 2 * D:], a["L0_attn_a_w_out"]], axis=1)
    wt = a["L0_attn_b_w_qkv"].T
    other = np.r_[D // 2:D, 0:D // 2]
    wiq, wik = a["L0_attn_b_w_iq"].T, a["L0_attn_b_w_ik"].T
    wiw = np.zeros((D, D), np.float32)
    wiw[:, :IDX_HEADS] = a["L0_attn_b_w_iw"].T
    w_idx = np.concatenate([wiq, wik, wik, wt[:, :D], wt[:, :D][:, other], wt[:, D:2 * D], wt[:, D:2 * D][:, other],
                            a["L0_attn_b_w_o"].T, a["L0_attn_b_w_qkv"][2 * D:], wiw], axis=1)
    bq, bk, bv = np.split(a["L0_attn_b_b_qkv"], 3)
    biq, bik = a["L0_attn_b_b_iq"], a["L0_attn_b_b_ik"]
    cols = np.stack([a["L0_attn_a_gamma"].reshape(D), a["L0_attn_a_beta"].reshape(D), biq[:D], biq[D:],
                     np.concatenate([bik, bik]), bq, bq[other], bk, bk[other], bv], axis=1)
    w1 = a["L0_ffn_W1"].transpose(1, 0, 2)
    w2 = a["L0_ffn_W2"].reshape(E, FC, P, D).transpose(2, 0, 1, 3).reshape(P, E, F)
    arrays = {
        "x": a["L0_attn_a_x"].reshape(TOKENS, D),
        "w_attn": w_attn,
        "w_idx": w_idx,
        "w_experts": np.concatenate([w1, w2], axis=2),
        "b1_cols": a["L0_ffn_b1"].reshape(E, FC, P).transpose(2, 0, 1),
        "b2": a["L0_ffn_b2"],
        "w_router": a["L0_ffn_Wr"],
        "cols": cols,
        "b_out": a["L0_attn_a_b_out"],
        "b_o": a["L0_attn_b_b_o"],
        "b_iw": row(a["L0_attn_b_b_iw"]),
        "b_r": row(a["L0_ffn_br"]),
        "consts": constant_table(),
    }
    arrays = {k: np.ascontiguousarray(v) for k, v in arrays.items()}
    nc = bacc.Bacc("TRN2", target_bir_lowering=False, num_devices=1)
    aps = {k: nc.dram_tensor(k, v.shape, mybir.dt.from_np(v.dtype), kind="ExternalInput").ap() for k, v in arrays.items()}
    out = nc.dram_tensor("out", (TOKENS, D), F32, kind="ExternalOutput").ap()
    build(nc, **aps, out=out)
    r = run_bass_kernel_spmd(nc, [arrays], core_ids=[0])
    return r.results[0]["out"].reshape(B, S, D)
```

```python
from contextlib import ExitStack

import numpy as np
import concourse.bass as bass
from concourse import mybir

F32 = mybir.dt.float32
BF16 = mybir.dt.bfloat16
I32 = mybir.dt.int32
U32 = mybir.dt.uint32
ALU = mybir.AluOpType
ACT = mybir.ActivationFunctionType
AX = mybir.AxisListType

P = 128
B, S, D = 16, 256, 128
C = S // P
T = B * C
TOKENS = B * S
HEADS, DIM_HEAD = 4, 32
IDX_HEADS, IDX_DIM, TOP_K = 4, 64, 32
E, F = 8, 512
FC = F // P
NT = T + E - 1
GROUP_STEPS = {0: 1, 2: 2, 4: 3}
TURN = 6
TE_LEN = 8 * -(-NT // TURN)
EPS = 1e-5
ROW = 2 * D + E
NEG = -3.0e38
KEEP_ROUTE, KEEP_GATHER = 32, 60
MAGIC = 1.5 * 2.0**23
W1_AT, W2_AT, B1_AT, B2_AT = 0, F, 2 * F, 2 * F + FC
W_LEN = 2 * F + FC + D
CONSTS = [("ident", P), ("blocks", P), ("ones", P), ("tri", P), ("cos", S), ("sin", S), ("slot1", P),
          ("tile", NT), ("turns", TE_LEN), ("down", E), ("keep", E * T), ("starts", T), ("col", T), ("part1", 1)]
FIRST = 3 * P
CONST_AT, CONST_LEN = {}, 0
for _name, _len in CONSTS:
    CONST_AT[_name] = (CONST_LEN, CONST_LEN + _len)
    CONST_LEN += _len


def constant_table():
    half = D // 2
    inv = (1.0 / 10000.0 ** (np.arange(half, dtype=np.float32) / np.float32(half))).astype(np.float32)
    ang = (np.arange(S, dtype=np.float32)[:, None] * inv[None, :]).astype(np.float32)
    cos, sin = np.cos(ang).T, np.sin(ang).T
    rows = np.arange(P)
    t = {
        "ident": np.eye(P),
        "blocks": rows[:, None] // DIM_HEAD == rows[None, :] // DIM_HEAD,
        "tri": rows[:, None] < rows[None, :],
        "ones": np.ones((P, P)),
        "cos": np.concatenate([cos, cos]),
        "sin": np.concatenate([-sin, sin]),
        "slot1": np.broadcast_to(rows + 1, (P, P)),
        "tile": np.broadcast_to(np.arange(NT), (P, NT)),
        "turns": np.broadcast_to(np.arange(TE_LEN) // 8 * TURN + np.minimum(np.arange(TE_LEN) % 8, TURN - 1), (P, TE_LEN)),
        "down": np.broadcast_to(E - np.arange(E), (P, E)),
        "keep": np.broadcast_to(np.arange(E * T) % T != 0, (P, E * T)),
        "starts": np.broadcast_to(np.arange(T) * P, (P, T)),
        "col": np.broadcast_to(np.arange(T), (P, T)),
        "part1": rows[:, None] + 1,
    }
    return np.concatenate([np.asarray(t[n], np.float32).reshape(P, -1) for n, _ in CONSTS], axis=1)


class Step:

    def __init__(self, base, unroll=1, turn=0):
        self.base, self.unroll, self.turn = base, unroll, turn

    def item(self, lag):
        return self.base - lag + self.unroll * self.turn

    def slot(self, lag, ring):
        return (self.base - lag) % ring

    def lap(self, lag, ring):
        return (self.base - lag) // ring + self.unroll // ring * self.turn

    def on(self, lag, items):
        return not isinstance(self.turn, int) or 0 <= self.base - lag < items


def steps(eng, items, lag, head, unroll, ahead=0):
    turns = (items - ahead - head) // unroll
    for s in range(head):
        yield Step(s)
    with eng.Fori(0, turns) as turn:
        for k in range(unroll):
            yield Step(head + k, unroll, turn)
    for s in range(head + turns * unroll, items + lag):
        yield Step(s)


def after(eng, sem, count):
    if not isinstance(count, int) or count > 0:
        eng.wait_ge(sem, count)


def alone(eng, sem, count, passed):
    if not isinstance(count, int) or count > 0:
        eng.wait_ge(sem, count)
        eng.sem_inc(passed, 1)


def build(nc, x, w_attn, w_idx, w_experts, b1_cols, b2, w_router, cols, b_out, b_o, b_iw, b_r, consts, out):
    with ExitStack() as ctx:
        def sb(name, shape, dt=F32):
            return ctx.enter_context(nc.sbuf_tensor(name, shape, dt))

        def sem(name):
            return ctx.enter_context(nc.semaphore(name))

        def sems(name, n):
            return [sem(f"{name}{i}") for i in range(n)]

        bank = [ctx.enter_context(nc.psum_tensor(f"bank{i}", [P, 512], F32)) for i in range(8)]

        rows_dram = [nc.dram_tensor(f"rows{i}", [TOKENS, ROW], F32, kind="Internal").ap() for i in range(2)]
        x2_dram = nc.dram_tensor("x2", [NT * P, D], F32, kind="Internal").ap()

        X = sb("X", [P, T, D])
        cst = sb("cst", [P, CONST_LEN])
        WE = sb("WE", [P, E, W_LEN])
        WA = sb("WA", [P, 4 * D])
        WR = sb("WR", [P, E])
        COL = sb("COL", [P, 10])
        WB = sb("WB", [P, 10 * D])
        WVO = sb("WVO", [P, D])
        bout_bc = sb("bout_bc", [P, D])
        bo_bc = sb("bo_bc", [P, D])
        bv_rep = sb("bv_rep", [P, P])
        rowc = sb("rowc", [1, C * (IDX_HEADS + E)])
        mhalf = sb("mhalf", [P, 2, T // 4])
        eps = sb("eps", [P, C])
        xf = [sb(f"xf{i}", [P, C, D]) for i in range(2)]
        xfT = [sb(f"xfT{i}", [P, S]) for i in range(2)]
        stat3 = sb("stat3", [P, C, 6])
        mv3 = [sb(f"mv3_{i}", [P, C, 2]) for i in range(2)]
        vpe3 = sb("vpe3", [P, C])
        rs3 = [sb(f"rs3_{i}", [P, C]) for i in range(2)]
        logits = sb("logits", [P, T, E])

        def const(name):
            a, b = CONST_AT[name]
            return cst[:, a:b]

        ident, ones = const("ident"), const("ones")

        mv1 = sb("mv1", [P, T, 2])
        stat1 = sb("stat1", [P, T, 6])
        v1 = sb("v1", [P, 2, T])
        r1 = sb("r1", [P, 2, T])
        xs = sb("xs", [P, 2, T])
        xa = [sb(f"xa{i}", [P, C, D]) for i in range(2)]
        xaT = [sb(f"xaT{i}", [P, S]) for i in range(4)]
        kneg = [sb(f"kneg{i}", [P, 1]) for i in range(2)]
        ekT = [sb(f"ekT{i}", [P, S]) for i in range(2)]
        esum = [sb(f"esum{i}", [P, 1]) for i in range(4)]
        einv = [sb(f"einv{i}", [P, 1]) for i in range(2)]
        ek = [sb(f"ek{i}", [P, C, D]) for i in range(2)]
        va = [sb(f"va{i}", [P, C, D]) for i in range(2)]
        cm = [sb(f"cm{i}", [P, D]) for i in range(2)]
        Gs = [sb(f"Gs{i}", [P, D]) for i in range(2)]
        Hs = [sb(f"Hs{i}", [P, D]) for i in range(2)]
        xres = [sb(f"xres{i}", [P, C, D]) for i in range(2)]

        r_a = sb("r_a", [P, T, E])
        r_b = sb("r_b", [P, T, E])
        oh = sb("oh", [P, E, T])
        incl = sb("incl", [P, E, T])
        rr = sb("rr", [P, E, T])
        r_m = sb("r_m", [P, 6, T])
        rtot = sb("rtot", [P, E])
        nt = sb("nt", [P, 3, E])
        oneh_slot = sb("oneh_slot", [P, T, P], BF16)
        is_tile = sb("is_tile", [P, T, NT], BF16)
        oneh_tile = sb("oneh_tile", [P, T, 2, NT], BF16)
        colbf = sb("colbf", [P, T], BF16)
        idxf = sb("idxf", [P, 3, NT])
        gidx = sb("gidx", [P, NT], U32)
        sidx = sb("sidx", [P, NT], U32)
        pidx = sb("pidx", [P, T], U32)
        pcur = [sb(f"pcur{i}", [P, C], U32) for i in range(2)]
        tef = sb("tef", [1, TE_LEN, E])
        tes = sb("tes", [1, TE_LEN])
        te = sb("te", [1, TE_LEN], I32)

        G_RING, Y_RING = 6, 6
        xg = [sb(f"xg{i}", [P, ROW]) for i in range(G_RING)]
        xgT = [sb(f"xgT{i}", [P, P]) for i in range(2)]
        w1 = [sb(f"w1_{i}", [P, F]) for i in range(2)]
        w2 = [sb(f"w2_{i}", [P, W_LEN - F]) for i in range(2)]
        hT = [sb(f"hT{i}", [P, FC, P]) for i in range(2)]
        lneg = [sb(f"lneg{i}", [P, 1]) for i in range(2)]
        lexp = [sb(f"lexp{i}", [P, E]) for i in range(2)]
        lsum = [sb(f"lsum{i}", [P, 1]) for i in range(Y_RING)]
        gate = sb("gate", [P, 1])
        yb = sb("yb", [P, D])
        yo = [sb(f"yo{i}", [P, D]) for i in range(Y_RING)]

        xin = [X[:, i * C:(i + 1) * C, :] for i in range(2)]
        stat2 = sb("stat2", [P, C, 6])
        mv2 = [sb(f"mv2_{i}", [P, C, 2]) for i in range(2)]
        vpe2 = sb("vpe2", [P, C])
        rs2 = [sb(f"rs2_{i}", [P, C]) for i in range(2)]
        xb = [sb(f"xb{i}", [P, C, D]) for i in range(2)]
        xbT = [sb(f"xbT{i}", [P, S]) for i in range(2)]
        qk = [sb(f"qk{i}", [P, 4, S]) for i in range(2)]
        qr = [sb(f"qr{i}", [P, 2, S]) for i in range(2)]
        iq = [sb(f"iq{i}", [P, 2, S]) for i in range(2)]
        ik = [sb(f"ik{i}", [P, S]) for i in range(2)]
        vb = [sb(f"vb{i}", [P, C, D]) for i in range(2)]
        iw = [sb(f"iw{i}", [P, C, IDX_HEADS]) for i in range(2)]
        rel = [sb(f"rel{i}", [P, C, IDX_HEADS, S]) for i in range(2)]
        part = [sb(f"part{i}", [P, C, 2, S]) for i in range(2)]
        head_sum = [sb(f"head_sum{i}", [P, C, S]) for i in range(2)]
        wk = sb("wk", [P, C, S])
        m8 = sb("m8", [P, C, 8])
        pen = sb("pen", [P, C, S])
        lg = [sb(f"lg{i}", [P, C, S]) for i in range(2)]
        lmax = sb("lmax", [P, C])
        lnb = [sb(f"lnb{i}", [P, C]) for i in range(2)]
        pr = lg
        psm = [sb(f"psm{i}", [P, C]) for i in range(2)]
        pinv = sb("pinv", [P, C])
        prT = [sb(f"prT{i}", [P, C, S]) for i in range(2)]
        xbias = [sb(f"xbias{i}", [P, C, D]) for i in range(2)]
        x3 = xres

        ld_c, ld_w, ld_x = sem("ld_c"), sem("ld_w"), sems("ld_x", 4)
        passed = {k: sem(f"passed_{k}") for k in ("dve", "pool", "sp")}
        ld_wb, ld_we = sem("ld_wb"), sem("ld_we")
        a_stat, a_var, a_pow, a_coef = sem("a_stat"), sem("a_var"), sem("a_pow"), sem("a_coef")
        a_xa, a_T, a_xaT, a_K, a_V = sem("a_xa"), sem("a_T"), sem("a_xaT"), sem("a_K"), sem("a_V")
        a_kneg, a_exp, a_va, a_ekT, a_ek = sem("a_kneg"), sem("a_exp"), sem("a_va"), sem("a_ekT"), sem("a_ek")
        a_ctx, a_cm, a_einv, a_G, a_Gs = sem("a_ctx"), sem("a_cm"), sem("a_einv"), sem("a_G"), sem("a_Gs")
        a_H, a_Hs, a_out, a_xres, a_pt = sem("a_H"), sem("a_Hs"), sem("a_out"), sem("a_xres"), sem("a_pt")
        c_half = sem("c_half")
        tails = []
        for n in "ab":
            tails.append({k: sem(f"{n}t_{k}") for k in
                          ("x", "st", "mv", "ve", "rs", "xf", "T", "xfT", "R", "lg")} | {
                          "store": sems(f"{n}t_store", 2), "rest": sem(f"{n}t_rest")})
        rt = {k: sem(f"r_{k}") for k in ("v", "sub", "exp", "rtot", "tot", "slots", "part", "tiles", "inv", "idx", "te")}
        ffns = [{k: sem(f"f{n}_{k}") for k in
                 ("T", "xgT", "w1", "w2", "H", "hA", "hV", "Y", "neg", "exp", "v", "y")} | {
                 "g": sems(f"f{n}_g", G_RING), "s": sems(f"f{n}_s", Y_RING)} for n in range(2)]
        b_ = {k: sem(f"b_{k}") for k in
              ("init", "bo", "wvo", "sc", "st", "mv", "ve", "rs", "xb", "T", "xbT", "pj", "pje", "rp", "qr", "iwe",
               "idx", "rel", "prt", "hs", "s1", "wk", "v", "S", "ttr", "lnb", "exp", "PT", "prT", "PV", "pinv",
               "xbias", "fin", "pc")} | {"x": sems("b_x", 2)}

        def xrows(dram, b, lo, hi):
            return dram[bass.ds(b * S, S), lo:hi].rearrange("(c p) d -> p c d", p=P)

        def tiles(b):
            return bass.ds(b * C, C)

        def experts_of(engine, st):
            at = (st.base // TURN + st.turn) * 8
            _, values = nc.values_load_multi_w_load_instructions(
                te[0:1, bass.ds(at, TURN)], engines=(engine,), min_val=0, max_val=E - 1,
                skip_runtime_bounds_check_because="they were clamped to the last expert when they were written")
            return values

        block = ctx.enter_context(nc.Block())

        @block.sync
        def _(sp):
            per = T // 4
            for g in range(4):
                sp.dma_start(X[:, g * per:(g + 1) * per, :],
                             x[g * per * P:(g + 1) * per * P, :].rearrange("(c p) d -> p c d", p=P)).then_inc(ld_x[g], 16)
                if g == 0:
                    sp.dma_start(cst[:, 0:FIRST], consts[:, 0:FIRST]).then_inc(ld_c, 16)
                    sp.dma_start(COL[:, :], cols).then_inc(ld_c, 16)
                    sp.dma_start(WA[:, :], w_attn).then_inc(ld_c, 16)
            sp.dma_start(bout_bc[:, :], b_out.partition_broadcast(P)).then_inc(ld_w, 16)
            sp.dma_start(cst[:, FIRST:], consts[:, FIRST:]).then_inc(ld_wb, 16)
            sp.dma_start(WR[:, :], w_router).then_inc(ld_w, 16)
            for c in range(C):
                sp.dma_start(rowc[:, c * IDX_HEADS:(c + 1) * IDX_HEADS], b_iw).then_inc(ld_w, 16)
                sp.dma_start(rowc[:, C * IDX_HEADS + c * E:C * IDX_HEADS + (c + 1) * E], b_r).then_inc(ld_w, 16)
            sp.dma_start(WB[:, :], w_idx).then_inc(ld_wb, 16)
            sp.dma_start(bo_bc[:, :], b_o.partition_broadcast(P)).then_inc(ld_wb, 16)
            sp.dma_start(WE[:, :, W1_AT:B1_AT], w_experts).then_inc(ld_we, 16)
            sp.dma_start(WE[:, :, B1_AT:B2_AT], b1_cols).then_inc(ld_we, 16)
            sp.dma_start(WE[:, :, B2_AT:W_LEN], b2.partition_broadcast(P)).then_inc(ld_we, 16)

            def store_rows(n, st, lag, x_of):
                t, dram = tails[n], rows_dram[n]
                b, r = st.item(lag), st.slot(lag, 2)
                sp.wait_ge(t["xf"], b + 1)
                sp.dma_start(xrows(dram, b, 0, D), xf[r][:, :, :]).then_inc(t["store"][r], 16)
                sp.wait_ge(t["x"], b + 1)
                sp.dma_start(xrows(dram, b, D, 2 * D), x_of(b, r)).then_inc(t["store"][r], 16)
                sp.wait_ge(t["lg"], b + 1)
                sp.dma_start(xrows(dram, b, 2 * D, ROW), logits[:, tiles(b), :]).then_inc(t["rest"], 16)

            for st in steps(sp, B, 0, 4, 2):
                store_rows(0, st, 0, lambda b, r: X[:, tiles(b), :])
            for st in steps(sp, NT, 0, 2 * TURN, TURN):
                j, r = st.item(0), st.slot(0, Y_RING)
                sp.wait_ge(ffns[0]["y"], j + 1)
                sp.dma_start(x2_dram[bass.ds(j * P, P), :], yo[r][:, :]).then_inc(ffns[0]["s"][r], 16)
            for st in steps(sp, B, 0, 4, 2):
                store_rows(1, st, 0, lambda b, r: x3[r][:, :, :])
            for i in range(Y_RING):
                sp.wait_ge(ffns[1]["s"][i], 16 * len(range(i, NT, Y_RING)))

        @block.gpsimd
        def _(pool):
            pool.memset(eps[:, :], EPS)
            pool.memset(mhalf[:, :, :], -0.5).then_inc(c_half, 1)
            pool.wait_ge(c_half, 1)
            per = T // 4

            def deviations(g, lo=0, hi=per):
                cs = slice(g * per + lo, g * per + hi)
                pool.wait_ge(a_var, g + 1)
                pool.tensor_tensor(r1[:, :, cs], v1[:, :, cs], mhalf[:, :, lo:hi], ALU.pow).then_inc(a_pow, 1)

            deviations(0, 0, C)
            deviations(0, C)

            def rstd(t, vpe, mv, rs, b, r):
                pool.wait_ge(t["mv"], b + 1)
                after(pool, t["rs"], b)
                pool.tensor_tensor(vpe[:, :], mv[r][:, :, 1], eps[:, :], ALU.add).then_inc(t["ve"], 1)
                pool.wait_ge(t["ve"], b + 1)
                after(pool, t["xf"] if "xf" in t else t["xb"], b - 1)
                pool.tensor_tensor(rs[r][:, :], vpe[:, :], mhalf[:, 0, 0:C], ALU.pow).then_inc(t["rs"], 1)

            for st in steps(pool, B, 3, 7, 4, ahead=1):
                if st.base in GROUP_STEPS and st.on(-1, B):
                    deviations(GROUP_STEPS[st.base])
                if st.on(1, B):
                    b, r = st.item(1), st.slot(1, 2)
                    pool.wait_ge(ld_w, 96)
                    pool.wait_ge(a_pt, b + 1)
                    pool.tensor_tensor(xres[r][:, :, :], xres[r][:, :, :],
                                       bout_bc[:, :].unsqueeze(1).to_broadcast([P, C, D]), ALU.add).then_inc(a_xres, 1)
                if st.on(3, B):
                    rstd(tails[0], vpe3, mv3, rs3, st.item(3), st.slot(3, 2))

            def route_pool(n):
                pool.wait_ge(rt["slots"], 5 * n + 1)
                pool.tensor_tensor(oneh_tile[:, :, 1, :], is_tile[:, :, :], colbf[:, :].unsqueeze(2).to_broadcast([P, T, NT]),
                                   ALU.mult).then_inc(rt["tiles"], 1)

            def experts_pool(n):
                f = ffns[n]
                for i in range(2):
                    pool.wait_ge(tails[n]["store"][i], 32 * (B // 2))
                pool.wait_ge(tails[n]["rest"], 16 * B)
                pool.wait_ge(rt["idx"], 3 * n + 2)
                for j in range(NT + G_RING):
                    if j < NT:
                        after(pool, f["y"], j + 1 - G_RING)
                        pool.indirect_dma_start(xg[j % G_RING][:, :], None, rows_dram[n],
                                                bass.IndirectOffsetOnAxis(ap=gidx[:, j:j + 1], axis=0)
                                                ).then_inc(f["g"][j % G_RING], 16)
                    k = j - G_RING
                    if n == 1 and k >= 0:
                        pool.wait_ge(f["y"], k + 1)
                        pool.indirect_dma_start(out, bass.IndirectOffsetOnAxis(ap=sidx[:, k:k + 1], axis=0),
                                                yo[k % Y_RING][:, :], None, bounds_check=TOKENS - 1,
                                                oob_is_err=False).then_inc(f["s"][k % Y_RING], 16)

            route_pool(0)
            experts_pool(0)

            def gather_x(st, lag):
                b, r = st.item(lag), st.slot(lag, 2)
                after(pool, b_["xb"], b - 1)
                after(pool, b_["xbias"], b - 1)
                for c in range(C):
                    after(pool, b_["x"][r], 16 * C * st.lap(lag, 2))
                    pool.tensor_copy(pcur[r][:, c:c + 1], pidx[:, bass.ds(b * C + c, 1)]).then_inc(b_["pc"], 1)
                for c in range(C):
                    alone(pool, b_["pc"], C * b + c + 1, passed["pool"])
                    pool.indirect_dma_start(xin[r][:, c, :], None, x2_dram,
                                            bass.IndirectOffsetOnAxis(ap=pcur[r][:, c:c + 1], axis=0)
                                            ).then_inc(b_["x"][r], 16)

            def add_heads(b, r, c):
                pool.wait_ge(b_["prt"], C * b + c + 1)
                after(pool, b_["s1"], C * (b - 1))
                pool.tensor_tensor(head_sum[r][:, c, :], part[r][:, c, 0, :], part[r][:, c, 1, :],
                                   ALU.add).then_inc(b_["hs"], 1)

            for i in range(Y_RING):
                pool.wait_ge(ffns[0]["s"][i], 16 * len(range(i, NT, Y_RING)))
            pool.wait_ge(rt["idx"], 3)
            gather_x(Step(0), 0)
            gather_x(Step(1), 0)
            pool.wait_ge(b_["bo"], 2)
            rstd(b_, vpe2, mv2, rs2, 0, 0)
            for st in steps(pool, B, 3, 6, 2, ahead=2):
                b, r = st.item(0), st.slot(0, 2)
                if st.on(3, B):
                    rstd(tails[1], vpe3, mv3, rs3, st.item(3), st.slot(3, 2))
                if st.on(0, B):
                    pool.wait_ge(b_["pje"], 8 * b + 7)
                    pool.tensor_tensor(qk[r][:, 0:2, :], qk[r][:, 0:2, :], const("cos").unsqueeze(1).to_broadcast([P, 2, S]),
                                       ALU.mult).then_inc(b_["rp"], 1)
                if st.on(-1, B):
                    rstd(b_, vpe2, mv2, rs2, st.item(-1), st.slot(-1, 2))
                if st.on(0, B):
                    pool.tensor_tensor(qk[r][:, 2:4, :], qk[r][:, 2:4, :], const("sin").unsqueeze(1).to_broadcast([P, 2, S]),
                                       ALU.mult).then_inc(b_["rp"], 1)
                if st.on(2, B):
                    p, q = st.item(2), st.slot(2, 2)
                    pool.wait_ge(b_["sc"], p + 1)
                    pool.wait_ge(b_["xbias"], p + 1)
                    pool.tensor_tensor(x3[q][:, :, :], x3[q][:, :, :], xbias[q][:, :, :], ALU.add).then_inc(tails[1]["x"], 1)
                if st.on(0, B):
                    add_heads(b, r, 0)
                    pool.wait_ge(b_["rp"], 2 * (b + 1))
                    after(pool, b_["S"], C * (b - 1))
                    pool.tensor_tensor(qr[r][:, :, :], qk[r][:, 0:2, :], qk[r][:, 2:4, :], ALU.add).then_inc(b_["qr"], 1)
                    add_heads(b, r, 1)
                    after(pool, tails[1]["x"], b - 1)
                    pool.wait_ge(b_["x"][r], 16 * C * (st.lap(0, 2) + 1))
                    pool.tensor_tensor(xbias[r][:, :, :], xin[r], bo_bc[:, :].unsqueeze(1).to_broadcast([P, C, D]),
                                       ALU.add).then_inc(b_["xbias"], 1)
                if st.on(-2, B):
                    gather_x(st, -2)
            route_pool(1)
            experts_pool(1)

        @block.tensor
        def _(pe):
            def router(n, b, r, where):
                t = tails[n]
                pe.wait_ge(t["xfT"], b + 1)
                after(pe, t["lg"], b)
                pe.matmul(where, ones[0:1, :], rowc[:, C * IDX_HEADS:], start=True, stop=False)
                for c in range(C):
                    mm = pe.matmul(where[:, c * E:(c + 1) * E], xfT[r][:, c * P:(c + 1) * P], WR[:, :],
                                   start=False, stop=(c == C - 1))
                mm.then_inc(t["R"], 1)

            def keep_clock(count, where):
                for i in range(count):
                    pe.transpose(where, ident, ident)

            def turn_xf(n, b, r, where):
                t = tails[n]
                pe.wait_ge(t["xf"], b + 1)
                after(pe, t["xfT"], b)
                after(pe, t["lg"], b)
                for c in range(C):
                    mm = pe.transpose(where[:, c * P:(c + 1) * P], xf[r][:, c, :], ident)
                mm.then_inc(t["T"], 1)

            pe.wait_ge(ld_c, 48)
            for st in steps(pe, B, 6, 7, 4, ahead=1):
                b, r = st.item(0), st.slot(0, 2)
                if st.on(0, B):
                    pe.wait_ge(a_xa, b + 1)
                    after(pe, a_xaT, b)
                    for c in range(C):
                        mm = pe.transpose(bank[2][:, c * P:(c + 1) * P], xa[r][:, c, :], ident)
                    mm.then_inc(a_T, 1)
                if st.on(1, B):
                    p, q = st.item(1), st.slot(1, 2)
                    pe.wait_ge(a_exp, p + 1)
                    after(pe, a_ek, p)
                    for c in range(C):
                        mm = pe.transpose(bank[5][:, c * P:(c + 1) * P], ekT[q][:, c * P:(c + 1) * P], ident)
                    mm.then_inc(a_ekT, 1)
                if st.on(2, B):
                    p, q = st.item(2), st.slot(2, 2)
                    pe.wait_ge(a_cm, p + 1)
                    pe.matmul(bank[3][:, D:2 * D], cm[q][:, :], WA[:, 3 * D:4 * D], start=True, stop=True).then_inc(a_G, 1)
                if st.base == 6:
                    pe.wait_ge(ld_w, 96)
                if st.on(6, B):
                    router(0, st.item(6), st.slot(6, 2), bank[6][:, S:S + C * E])
                if st.on(0, B):
                    k = st.slot(0, 4)
                    pe.wait_ge(a_xaT, b + 1)
                    after(pe, a_exp, b)
                    pe.matmul(bank[0][:, 0:S], WA[:, D:2 * D], xaT[k][:, :], start=True, stop=True).then_inc(a_K, 1)
                    after(pe, a_va, b)
                    for c in range(C):
                        mm = pe.matmul(bank[1][:, c * D:(c + 1) * D], xaT[k][:, c * P:(c + 1) * P],
                                       WA[:, 2 * D:3 * D], start=True, stop=True)
                    mm.then_inc(a_V, 1)
                if st.on(2, B):
                    p, q = st.item(2), st.slot(2, 2)
                    pe.wait_ge(a_Gs, p + 1)
                    after(pe, a_Hs, p)
                    pe.matmul(bank[7][:, 0:D], WA[:, 0:D], Gs[q][:, :], start=True, stop=True).then_inc(a_H, 1)
                if st.on(5, B):
                    turn_xf(0, st.item(5), st.slot(5, 2), bank[6])
                if st.on(1, B):
                    p, q = st.item(1), st.slot(1, 2)
                    pe.wait_ge(a_ek, p + 1)
                    pe.wait_ge(a_va, p + 1)
                    after(pe, a_Gs, p)
                    for c in range(C):
                        mm = pe.matmul(bank[3][:, 0:D], va[q][:, c, :], ek[q][:, c, :], start=(c == 0), stop=(c == C - 1))
                    mm.then_inc(a_ctx, 1)
                if st.on(2, B):
                    p, q = st.item(2), st.slot(2, 2)
                    pe.wait_ge(a_Hs, p + 1)
                    after(pe, tails[0]["x"], p)
                    for c in range(C):
                        mm = pe.matmul(bank[4][:, c * D:(c + 1) * D], xaT[st.slot(2, 4)][:, c * P:(c + 1) * P], Hs[q][:, :],
                                       start=True, stop=True)
                    mm.then_inc(a_out, 1)

            def route_tensor(n):
                pe.wait_ge(rt["rtot"], n + 1)
                pe.matmul(bank[0][:, 0:E], const("tri"), rtot[:, :], start=True, stop=True)
                pe.matmul(bank[0][:, E:2 * E], ones, rtot[:, :], start=True, stop=True).then_inc(rt["tot"], 1)
                pe.wait_ge(rt["part"], n + 1)
                pe.wait_ge(rt["tiles"], n + 1)
                for c in range(T):
                    if c % 8 == 0:
                        pe.wait_ge(rt["slots"], 5 * n + c // 8 + 2)
                    mm = pe.matmul(bank[1][:, 0:2 * NT], oneh_slot[:, c, :],
                                   oneh_tile[:, c, :, :].rearrange("p a b -> p (a b)"), start=(c == 0), stop=(c == T - 1))
                mm.then_inc(rt["inv"], 1)
                keep_clock(KEEP_ROUTE, bank[2][:, 0:P])

            def experts_tensor(n):
                f = ffns[n]
                pe.wait_ge(rt["idx"], 3 * n + 2)
                for st in steps(pe, NT, 2, 2 * TURN, TURN):
                    if st.on(0, NT):
                        j, r, g = st.item(0), st.slot(0, 2), st.slot(0, G_RING)
                        pe.wait_ge(f["g"][g], 16 * (st.lap(0, G_RING) + 1))
                        after(pe, f["xgT"], j - 1)
                        pe.transpose(bank[6 + r][:, 0:P], xg[g][:, 0:D], ident).then_inc(f["T"], 1)
                    if st.on(1, NT):
                        j, r = st.item(1), st.slot(1, 2)
                        pe.wait_ge(f["xgT"], j + 1)
                        pe.wait_ge(f["w1"], j + 1)
                        after(pe, f["hA"], 2 * (j - 1))
                        after(pe, f["hV"], 2 * (j - 1))
                        for k in range(FC):
                            mm = pe.matmul(bank[r + 2 * (k // 2)][:, k % 2 * P:(k % 2 + 1) * P],
                                           w1[r][:, k * P:(k + 1) * P], xgT[r][:, :], start=True, stop=True)
                            if k % 2:
                                mm.then_inc(f["H"], 1)
                    if st.on(2, NT):
                        j, r = st.item(2), st.slot(2, 2)
                        pe.wait_ge(f["hA"], 2 * (j + 1))
                        pe.wait_ge(f["hV"], 2 * (j + 1))
                        pe.wait_ge(f["w2"], j + 1)
                        after(pe, f["y"], j - 1)
                        for k in range(FC):
                            mm = pe.matmul(bank[4 + r][:, 0:D], hT[r][:, k, :], w2[r][:, k * D:(k + 1) * D],
                                           start=(k == 0), stop=(k == FC - 1))
                        mm.then_inc(f["Y"], 1)

            route_tensor(0)
            experts_tensor(0)

            pe.wait_ge(ffns[0]["y"], NT)
            pe.wait_ge(ld_wb, 48)
            pe.wait_ge(b_["bo"], 1)
            pe.matmul(bank[2][:, 0:D], WB[:, 8 * D:9 * D], WB[:, 7 * D:8 * D], start=True, stop=True)
            pe.matmul(bank[3][:, 0:D], bv_rep[:, :], WB[:, 7 * D:8 * D], start=True, stop=True).then_inc(b_["wvo"], 1)
            pe.wait_ge(b_["init"], 1)
            pe.wait_ge(b_["bo"], 2)
            keep_clock(KEEP_GATHER, bank[4][:, 0:P])
            for st in steps(pe, B, 4, 6, 2, ahead=1):
                def project(pair):
                    b, r = st.item(0), st.slot(0, 2)
                    after(pe, b_["pje"], 8 * b + 2 * (pair - 1))
                    for i in (2 * pair, 2 * pair + 1):
                        to = bank[2 + pair % 2][:, i % 2 * S:(i % 2 + 1) * S]
                        if i < 7:
                            mm = pe.matmul(to, WB[:, i * D:(i + 1) * D], xbT[r][:, :], start=True, stop=True)
                        else:
                            for c in range(C):
                                mm = pe.matmul(to[:, c * D:(c + 1) * D], xbT[r][:, c * P:(c + 1) * P], WVO[:, :],
                                               start=True, stop=True)
                    mm.then_inc(b_["pj"], 1)

                def index_scores(c):
                    b, r = st.item(0), st.slot(0, 2)
                    for h in range(IDX_HEADS):
                        lo = IDX_DIM * (h % 2)
                        if h < 2:
                            after(pe, b_["rel"], 2 * (C * b + c - 1) + h + 1)
                        mm = pe.matmul(bank[h % 2][:, h // 2 * S:(h // 2 + 1) * S],
                                       iq[r][lo:lo + IDX_DIM, h // 2, c * P:(c + 1) * P], ik[r][lo:lo + IDX_DIM, :],
                                       start=True, stop=True)
                        if h >= 2:
                            mm.then_inc(b_["idx"], 1)

                if st.on(0, B):
                    b, r = st.item(0), st.slot(0, 2)
                    pe.wait_ge(b_["xb"], b + 1)
                    after(pe, b_["iwe"], b)
                    after(pe, tails[1]["xfT"], b - 3)
                    for c in range(C):
                        mm = pe.transpose(bank[5][:, c * P:(c + 1) * P], xb[r][:, c, :], ident)
                    mm.then_inc(b_["T"], 1)
                if st.on(4, B):
                    after(pe, b_["sc"], min(st.item(3) + 1, B) if st.base >= B else st.item(3) + 1)
                    router(1, st.item(4), st.slot(4, 2), bank[7][:, S:S + C * E])
                if st.on(0, B):
                    pe.wait_ge(b_["xbT"], st.item(0) + 1)
                    project(0)
                    project(1)
                if st.on(2, B):
                    b, r = st.item(2), st.slot(2, 2)
                    after(pe, b_["prT"], b)
                    for c in range(C):
                        pe.wait_ge(b_["exp"], C * b + c + 1)
                        for k in range(C):
                            mm = pe.transpose(bank[4][:, c * S + k * P:c * S + (k + 1) * P], pr[r][:, c, k * P:(k + 1) * P], ident)
                    mm.then_inc(b_["PT"], 1)
                if st.on(1, B):
                    b, r = st.item(1), st.slot(1, 2)
                    pe.wait_ge(b_["qr"], b + 1)
                    after(pe, b_["ttr"], C * b)
                    for c in range(C):
                        pe.matmul(bank[6][:, c * S:(c + 1) * S], qr[r][:, 0, c * P:(c + 1) * P], qr[r][:, 1, :],
                                  start=True, stop=True).then_inc(b_["S"], 1)
                if st.on(0, B):
                    project(2)
                if st.on(2, B):
                    b, r = st.item(2), st.slot(2, 2)
                    pe.wait_ge(b_["prT"], b + 1)
                    after(pe, b_["sc"], b)
                    after(pe, tails[1]["lg"], b - 1)
                    for c in range(C):
                        for k in range(C):
                            mm = pe.matmul(bank[7][:, c * D:(c + 1) * D], prT[r][:, c, k * P:(k + 1) * P], vb[r][:, k, :],
                                           start=(k == 0), stop=(k == C - 1))
                        mm.then_inc(b_["PV"], 1)
                if st.on(0, B):
                    b, r = st.item(0), st.slot(0, 2)
                    project(3)
                if st.on(0, B):
                    pe.matmul(bank[5][:, S:S + C * IDX_HEADS], ones[0:1, :], rowc[:, 0:C * IDX_HEADS], start=True, stop=False)
                    for c in range(C):
                        mm = pe.matmul(bank[5][:, S + c * IDX_HEADS:S + (c + 1) * IDX_HEADS], xbT[r][:, c * P:(c + 1) * P],
                                       WB[:, 9 * D:9 * D + IDX_HEADS], start=False, stop=(c == C - 1))
                    mm.then_inc(b_["pj"], 1)
                if st.on(0, B):
                    index_scores(0)
                if st.on(3, B):
                    pe.wait_ge(b_["iwe"], st.item(0) + 1 if st.on(0, B) else B)
                    turn_xf(1, st.item(3), st.slot(3, 2), bank[5][:, 0:S])
                if st.on(0, B):
                    index_scores(1)
            route_tensor(1)
            experts_tensor(1)

        @block.scalar
        def _(act):
            def xf_out(n, b, r, where):
                t = tails[n]
                act.wait_ge(t["T"], b + 1)
                after(act, t["R"], b - 1)
                act.activation(xfT[r][:, :], where, ACT.Copy).then_inc(t["xfT"], 1)

            def logits_out(n, b, where):
                t = tails[n]
                act.wait_ge(t["R"], b + 1)
                act.activation(logits[:, tiles(b), :], where.rearrange("p (c e) -> p c e", c=C), ACT.Copy).then_inc(t["lg"], 1)

            act.preload_act_table(ACT.Exp)
            act.wait_ge(ld_c, 48)
            for st in steps(act, B, 6, 7, 4, ahead=1):
                b, r = st.item(0), st.slot(0, 2)
                if st.on(0, B):
                    k = st.slot(0, 4)
                    act.wait_ge(a_T, b + 1)
                    after(act, a_out, b - 3)
                    act.activation(xaT[k][:, :], bank[2][:, 0:S], ACT.Identity, scale=COL[:, 0:1],
                                   bias=COL[:, 1:2]).then_inc(a_xaT, 1)
                if st.on(1, B):
                    p, q = st.item(1), st.slot(1, 2)
                    act.wait_ge(a_ekT, p + 1)
                    after(act, a_ctx, p - 1)
                    act.activation(ek[q][:, :, :], bank[5][:, 0:S].rearrange("p (c d) -> p c d", c=C), ACT.Copy).then_inc(a_ek, 1)
                if st.on(6, B):
                    logits_out(0, st.item(6), bank[6][:, S:S + C * E])
                if st.on(1, B):
                    p, q = st.item(1), st.slot(1, 2)
                    act.wait_ge(a_coef, 4 if st.base > 5 else p // 4 + 1)
                    after(act, tails[0]["x"], p - 1)
                    for c in range(C):
                        at = bass.ds(p * C + c, 1)
                        ins = act.activation(xres[q][:, c, :], X[:, at, :].rearrange("p a d -> p (a d)"), ACT.Identity,
                                             scale=xs[:, 0, at], bias=xs[:, 1, at])
                    ins.then_inc(a_pt, 1)
                if st.on(2, B):
                    p, q = st.item(2), st.slot(2, 2)
                    act.wait_ge(a_H, p + 1)
                    after(act, a_out, p - 1)
                    act.activation(Hs[q][:, :], bank[7][:, 0:D], ACT.Copy).then_inc(a_Hs, 1)
                if st.on(0, B):
                    act.wait_ge(a_kneg, b + 1)
                    after(act, a_ekT, b - 1)
                    after(act, a_einv, b - 3)
                    act.activation(ekT[r][:, :], bank[0][:, 0:S], ACT.Exp, bias=kneg[r][:, :],
                                   accum_out=esum[k][:, :]).then_inc(a_exp, 1)
                    act.wait_ge(a_V, b + 1)
                    after(act, a_ctx, b - 1)
                    act.activation(va[r][:, :, :], bank[1][:, 0:S].rearrange("p (c d) -> p c d", c=C),
                                   ACT.Copy).then_inc(a_va, 1)
                if st.on(5, B):
                    xf_out(0, st.item(5), st.slot(5, 2), bank[6][:, 0:S])

            def route_scalar(n):
                act.wait_ge(rt["sub"], n + 1)
                act.activation(r_b[:, :, :], r_a[:, :, :], ACT.Exp).then_inc(rt["exp"], 1)
                act.wait_ge(rt["slots"], 5 * n + 1)
                act.activation(oneh_tile[:, :, 0, :], is_tile[:, :, :], ACT.Copy, scale=const("part1")).then_inc(rt["part"], 1)

            def experts_scalar(n):
                f = ffns[n]
                if n == 0:
                    act.wait_ge(ld_we, 48)
                act.preload_act_table(ACT.Exp)
                act.wait_ge(rt["te"], n + 1)
                for st in steps(act, NT, 2, 2 * TURN, TURN):
                    if st.base % TURN == 0 and st.on(0, NT):
                        experts = experts_of(mybir.EngineType.Activation, st)
                    if st.on(0, NT):
                        j, r = st.item(0), st.slot(0, 2)
                        after(act, f["H"], 2 * (j - 1))
                        act.activation(w1[r][:, :], WE[:, bass.ds(experts[st.base % TURN], 1), W1_AT:W1_AT + F
                                                       ].rearrange("p a w -> p (a w)"), ACT.Copy).then_inc(f["w1"], 1)
                        act.wait_ge(f["T"], j + 1)
                        act.activation(xgT[r][:, :], bank[6 + r][:, 0:P], ACT.Copy).then_inc(f["xgT"], 1)
                    if st.on(1, NT):
                        j, r = st.item(1), st.slot(1, 2)
                        act.wait_ge(f["w2"], j + 1)
                        act.wait_ge(f["H"], 2 * j + 1)
                        for k in range(FC // 2):
                            act.activation(hT[r][:, k, :], bank[r][:, k * P:(k + 1) * P], ACT.Relu,
                                           bias=w2[r][:, F + k:F + k + 1]).then_inc(f["hA"], 1)
                    if st.on(0, NT):
                        j, r, g = st.item(0), st.slot(0, 2), st.slot(0, G_RING)
                        act.wait_ge(f["neg"], j + 1)
                        after(act, f["y"], j + 1 - Y_RING)
                        act.activation(lexp[r][:, :], xg[g][:, 2 * D:ROW], ACT.Exp, bias=lneg[r][:, :],
                                       accum_out=lsum[st.slot(0, Y_RING)][:, :]).then_inc(f["exp"], 1)

            route_scalar(0)
            experts_scalar(0)

            act.wait_ge(b_["wvo"], 1)
            act.activation(WVO[:, :], bank[2][:, 0:D], ACT.Copy).then_inc(b_["init"], 1)
            act.preload_act_table(ACT.Exp)
            scale = float(D) ** -0.5

            def turned(b, r):
                act.wait_ge(b_["T"], b + 1)
                after(act, b_["idx"], 2 * C * (b - 1))
                act.activation(xbT[r][:, :], bank[5][:, 0:S], ACT.Copy).then_inc(b_["xbT"], 1)

            turned(0, 0)
            for st in steps(act, B, 4, 6, 2, ahead=1):
                b, r = st.item(0), st.slot(0, 2)

                def projected(pair):
                    act.wait_ge(b_["pj"], 5 * b + pair + 1)
                    for i in (2 * pair, 2 * pair + 1):
                        src = bank[2 + pair % 2][:, i % 2 * S:(i % 2 + 1) * S]
                        if i == 3:
                            after(act, b_["qr"], b - 1)
                        if i < 7:
                            dst = iq[r][:, i, :] if i < 2 else ik[r][:, :] if i == 2 else qk[r][:, (0, 2, 1, 3)[i - 3], :]
                            act.activation(dst, src, ACT.Identity, bias=COL[:, 2 + i:3 + i]).then_inc(b_["pje"], 1)
                        else:
                            after(act, b_["PV"], C * (b - 1))
                            act.activation(vb[r][:, :, :], src.rearrange("p (c d) -> p c d", c=C), ACT.Copy).then_inc(b_["pje"], 1)

                if st.on(0, B):
                    projected(0)
                if st.on(2, B):
                    p, q = st.item(2), st.slot(2, 2)
                    for c in range(C):
                        act.wait_ge(b_["lnb"], C * p + c + 1)
                        after(act, b_["pinv"], p - 1)
                        act.activation(pr[q][:, c, :], lg[q][:, c, :], ACT.Exp, bias=lnb[q][:, c:c + 1], scale=scale,
                                       accum_out=psm[q][:, c:c + 1]).then_inc(b_["exp"], 1)
                if st.on(4, B):
                    logits_out(1, st.item(4), bank[7][:, S:S + C * E])
                if st.on(0, B):
                    projected(1)
                if st.on(2, B):
                    act.wait_ge(b_["PT"], p + 1)
                    after(act, b_["PV"], C * (p - 1))
                    act.activation(prT[q][:, :, :], bank[4][:, :].rearrange("p (c k) -> p c k", c=C), ACT.Copy).then_inc(b_["prT"], 1)
                if st.on(0, B):
                    projected(2)
                    projected(3)
                    act.wait_ge(b_["pj"], 5 * (b + 1))
                    after(act, b_["wk"], C * (b - 1))
                    act.activation(iw[r][:, :, :],
                                   bank[5][:, S:S + C * IDX_HEADS].rearrange("p (c h) -> p c h", c=C),
                                   ACT.Copy).then_inc(b_["iwe"], 1)
                if st.on(2, B):
                    act.wait_ge(b_["pinv"], p + 1)
                    act.wait_ge(b_["PV"], C * (p + 1))
                    after(act, tails[1]["xf"], p - 1)
                    after(act, tails[1]["store"][q], 32 * st.lap(2, 2))
                    for c in range(C):
                        ins = act.activation(x3[q][:, c, :], bank[7][:, c * D:(c + 1) * D], ACT.Copy, scale=pinv[:, c:c + 1])
                    ins.then_inc(b_["sc"], 1)
                for c in range(C):
                    if st.on(0, B):
                        if c == 0:
                            after(act, b_["hs"], C * (b - 1))
                            act.wait_ge(b_["iwe"], b + 1)
                        for i in range(2):
                            act.wait_ge(b_["idx"], 2 * (C * b + c) + i + 1)
                            act.activation(rel[r][:, c, i::2, :],
                                           bank[i][:, :].rearrange("p (h k) -> p h k", h=2), ACT.Relu).then_inc(b_["rel"], 1)
                    if c == C - 1 and st.on(-1, B):
                        turned(st.item(-1), st.slot(-1, 2))
                    if st.on(0, B):
                        act.wait_ge(b_["rel"], 2 * (C * b + c + 1))
                        for h in range(2):
                            ins = act.activation(part[r][:, c, h, :], rel[r][:, c, h, :], ACT.Copy,
                                                 scale=iw[r][:, c, h:h + 1])
                        ins.then_inc(b_["prt"], 1)
                    if c == 0 and st.on(3, B):
                        xf_out(1, st.item(3), st.slot(3, 2), bank[5][:, 0:S])
            route_scalar(1)
            experts_scalar(1)

        @block.vector
        def _(dve):
            def stats(t, x_of, stat, mv, b, r, free, count):
                spread(t, x_of, stat)
                aggregate(t, stat, mv, b, r, free, count)

            def spread(t, x_of, stat):
                for c in range(C):
                    ins = dve.bn_stats(stat[:, c, :], x_of(c))
                ins.then_inc(t["st"], 1)

            def aggregate(t, stat, mv, b, r, free, count):
                alone(dve, t["st"], b + 1, passed["dve"])
                alone(dve, free, count, passed["dve"])
                for c in range(C):
                    ins = dve.bn_aggr(mv[r][:, c, :], stat[:, c, :])
                ins.then_inc(t["mv"], 1)

            def normalise(t, key, x_of, dst, mv, rs, b, r):
                dve.wait_ge(t["rs"], b + 1)
                dve.wait_ge(t["mv"], b + 1)
                for c in range(C):
                    ins = dve.tensor_scalar(dst[:, c, :], x_of(c), mv[r][:, c, 0:1], rs[r][:, c:c + 1],
                                            ALU.subtract, ALU.mult)
                ins.then_inc(t[key], 1)

            def one_tile(b, c):
                return X[:, bass.ds(b * C + c, 1), :].rearrange("p a d -> p (a d)")

            per = T // 4

            def coefficients(g):
                cs = slice(g * per, (g + 1) * per)
                dve.wait_ge(a_pow, g + 2)
                dve.tensor_scalar(xs[:, 0, cs], r1[:, 0, cs], 1.0, None, ALU.add)
                dve.scalar_tensor_tensor(xs[:, 1, cs], mv1[:, cs, 0], -1.0, r1[:, 0, cs], ALU.mult, ALU.mult).then_inc(a_coef, 1)

            def variances(g):
                cs = slice(g * per, (g + 1) * per)
                dve.wait_ge(ld_x[g], 16)
                for c in range(g * per, (g + 1) * per):
                    ins = dve.bn_stats(stat1[:, c, :], X[:, c, :])
                ins.then_inc(a_stat, 1)
                dve.wait_ge(a_stat, 2 * g + 1)
                for c in range(g * per, (g + 1) * per):
                    ins = dve.bn_aggr(mv1[:, c, :], stat1[:, c, :])
                ins.then_inc(a_stat, 1)
                dve.wait_ge(a_stat, 2 * g + 2)
                dve.tensor_scalar(v1[:, 0, cs], mv1[:, cs, 1], EPS, None, ALU.add)
                dve.tensor_scalar(v1[:, 1, cs], mv1[:, cs, 1], 1.0 + EPS, EPS * EPS, ALU.mult, ALU.add).then_inc(a_var, 1)

            def twice_normal(b, r):
                after(dve, a_T, b - 1)
                for c in range(C):
                    at = bass.ds(b * C + c, 1)
                    ins = dve.tensor_scalar(xa[r][:, c, :], one_tile(b, c), mv1[:, at, 0], r1[:, 1, at],
                                            ALU.subtract, ALU.mult)
                ins.then_inc(a_xa, 1)

            variances(0)
            dve.wait_ge(a_pow, 1)
            twice_normal(0, 0)
            dve.wait_ge(ld_c, 48)
            for st in steps(dve, B, 4, 7, 4, ahead=1):
                b, r = st.item(0), st.slot(0, 2)
                if st.base in GROUP_STEPS and st.on(-1, B):
                    variances(GROUP_STEPS[st.base])
                if st.base == 0:
                    coefficients(0)
                if st.base - 2 in GROUP_STEPS and st.on(-1, B):
                    coefficients(GROUP_STEPS[st.base - 2])
                if st.on(2, B):
                    p, q = st.item(2), st.slot(2, 2)
                    dve.wait_ge(a_exp, p + 1)
                    after(dve, a_Gs, p - 1)
                    dve.reciprocal(einv[q][:, :], esum[st.slot(2, 4)][:, :]).then_inc(a_einv, 1)
                if st.on(3, B):
                    n, m = st.item(3), st.slot(3, 2)
                    alone(dve, tails[0]["x"], n + 1, passed["dve"])
                    alone(dve, tails[0]["mv"], n, passed["dve"])
                    spread(tails[0], lambda c: one_tile(n, c), stat3)
                if st.on(2, B):
                    dve.wait_ge(a_G, p + 1)
                    dve.wait_ge(a_einv, p + 1)
                    after(dve, a_H, p - 1)
                    dve.tensor_scalar(Gs[q][:, :], bank[3][:, D:2 * D], einv[q][:, :], float(DIM_HEAD) ** -0.5,
                                      ALU.mult, ALU.mult).then_inc(a_Gs, 1)
                if st.on(3, B):
                    aggregate(tails[0], stat3, mv3, n, m, tails[0]["xf"], n - 1)
                if st.on(0, B):
                    dve.wait_ge(a_K, b + 1)
                    after(dve, a_exp, b - 1)
                    dve.tensor_reduce(kneg[r][:, :], bank[0][:, 0:S], AX.X, ALU.max, negate=True).then_inc(a_kneg, 1)
                if st.on(-1, B):
                    twice_normal(st.item(-1), st.slot(-1, 2))
                if st.on(4, B):
                    n, m = st.item(4), st.slot(4, 2)
                    after(dve, tails[0]["store"][m], 32 * st.lap(4, 2))
                    after(dve, tails[0]["T"], n - 1)
                    normalise(tails[0], "xf", lambda c: one_tile(n, c), xf[m], mv3, rs3, n, m)
                if st.on(1, B):
                    p, q = st.item(1), st.slot(1, 2)
                    dve.wait_ge(a_ctx, p + 1)
                    after(dve, a_G, p - 1)
                    dve.tensor_tensor(cm[q][:, :], bank[3][:, 0:D], const("blocks"), ALU.mult).then_inc(a_cm, 1)
                if st.on(2, B):
                    p, q = st.item(2), st.slot(2, 2)
                    dve.wait_ge(a_out, p + 1)
                    dve.wait_ge(a_xres, p + 1)
                    dve.tensor_tensor(X[:, tiles(p), :], bank[4][:, 0:S].rearrange("p (c d) -> p c d", c=C),
                                      xres[q][:, :, :], ALU.add).then_inc(tails[0]["x"], 1)

            def route_vector(n):
                count = 100 * n

                def link(ins):
                    nonlocal count
                    count += 1
                    ins.then_inc(rt["v"], 1)
                    dve.wait_ge(rt["v"], count)

                if n == 0:
                    dve.wait_ge(ld_wb, 48)
                    link(dve.tensor_copy(colbf[:, :], const("col")))
                dve.wait_ge(tails[n]["lg"], B)
                v = lambda k: r_m[:, k, :]
                over_e = lambda a: a.unsqueeze(2).to_broadcast([P, T, E])
                link(dve.tensor_reduce(v(0), logits[:, :, :], AX.X, ALU.max))
                dve.tensor_tensor(r_a[:, :, :], logits[:, :, :], over_e(v(0)), ALU.subtract).then_inc(rt["sub"], 1)
                dve.wait_ge(rt["exp"], n + 1)
                link(dve.tensor_reduce(v(1), r_b[:, :, :], AX.X, ALU.max))
                link(dve.tensor_tensor(r_a[:, :, :], r_b[:, :, :], over_e(v(1)), ALU.is_equal))
                link(dve.tensor_tensor(r_b[:, :, :], r_a[:, :, :], const("down").unsqueeze(1).to_broadcast([P, T, E]), ALU.mult))
                link(dve.tensor_reduce(v(2), r_b[:, :, :], AX.X, ALU.max))
                link(dve.tensor_tensor(oh[:, :, :].rearrange("p e t -> p t e"), r_b[:, :, :], over_e(v(2)), ALU.is_equal))
                link(dve.tensor_tensor_scan(incl[:, :, :].rearrange("p e t -> p (e t)"), const("keep"),
                                            oh[:, :, :].rearrange("p e t -> p (e t)"), 0.0, ALU.mult, ALU.add))
                dve.tensor_copy(rtot[:, :], incl[:, :, T - 1]).then_inc(rt["rtot"], 1)
                dve.wait_ge(rt["tot"], n + 1)
                over_t = lambda a: a.unsqueeze(2).to_broadcast([P, E, T])
                link(dve.tensor_copy(nt[:, 0, :], bank[0][:, 0:E]))
                link(dve.tensor_tensor(rr[:, :, :], over_t(bank[0][:, E:2 * E]),
                                       const("starts").unsqueeze(1).to_broadcast([P, E, T]), ALU.is_gt))
                link(dve.tensor_reduce(nt[:, 1, :], rr[:, :, :], AX.X, ALU.add))
                link(dve.tensor_tensor_scan(nt[:, 2, :], ones[:, 0:E], nt[:, 1, :], 0.0, ALU.mult, ALU.add))
                link(dve.tensor_tensor(nt[:, 1, :], nt[:, 2, :], nt[:, 1, :], ALU.subtract))
                link(dve.scalar_tensor_tensor(nt[:, 0, :], nt[:, 1, :], float(P), nt[:, 0, :], ALU.mult, ALU.add))
                link(dve.tensor_tensor(rr[:, :, :], incl[:, :, :], over_t(nt[:, 0, :]), ALU.add))
                link(dve.tensor_tensor(rr[:, :, :], rr[:, :, :], oh[:, :, :], ALU.mult))
                link(dve.tensor_reduce(v(3), rr[:, :, :].rearrange("p e t -> p t e"), AX.X, ALU.add))
                link(dve.tensor_scalar(v(4), v(3), 1.0 / P, -(P / 2 + 0.5) / P, ALU.mult, ALU.add))
                link(dve.tensor_scalar(v(4), v(4), MAGIC, MAGIC, ALU.add, ALU.subtract))
                link(dve.scalar_tensor_tensor(v(5), v(4), float(-P), v(3), ALU.mult, ALU.add))
                dve.tensor_tensor(is_tile[:, :, :], const("tile").unsqueeze(1).to_broadcast([P, T, NT]),
                                  v(4).unsqueeze(2).to_broadcast([P, T, NT]), ALU.is_equal).then_inc(rt["slots"], 1)
                for g in range(4):
                    cs = slice(g * per, (g + 1) * per)
                    dve.tensor_tensor(oneh_slot[:, cs, :], const("slot1").unsqueeze(1).to_broadcast([P, per, P]),
                                      r_m[:, 5, cs].unsqueeze(2).to_broadcast([P, per, P]), ALU.is_equal).then_inc(rt["slots"], 1)
                link(dve.tensor_tensor(tef[:, :, :], const("turns")[0:1, :].unsqueeze(2).to_broadcast([1, TE_LEN, E]),
                                       nt[0:1, 2, :].unsqueeze(1).to_broadcast([1, TE_LEN, E]), ALU.is_ge))
                link(dve.tensor_reduce(tes[:, :], tef[:, :, :], AX.X, ALU.add))
                dve.tensor_scalar(te[:, :], tes[:, :], float(E - 1), None, ALU.min).then_inc(rt["te"], 1)
                dve.wait_ge(rt["inv"], n + 1)
                link(dve.tensor_scalar(idxf[:, 0, :], bank[1][:, 0:NT], -1.0, None, ALU.add))
                link(dve.scalar_tensor_tensor(idxf[:, 1, :], bank[1][:, NT:2 * NT], float(P), idxf[:, 0, :], ALU.mult, ALU.add))
                dve.tensor_scalar(gidx[:, :], idxf[:, 1, :], 0.0, None, ALU.max).then_inc(rt["idx"], 1)
                link(dve.tensor_scalar(idxf[:, 2, :], idxf[:, 1, :], 0.0, float(2 * TOKENS), ALU.is_lt, ALU.mult))
                dve.tensor_tensor(sidx[:, :], idxf[:, 1, :], idxf[:, 2, :], ALU.add).then_inc(rt["idx"], 1)
                if n == 0:
                    dve.tensor_scalar(pidx[:, :], v(3), -1.0, None, ALU.add).then_inc(rt["idx"], 1)
                    dve.sem_inc(rt["v"], 100 - count)

            def experts_vector(n):
                f = ffns[n]
                if n == 0:
                    dve.wait_ge(ld_we, 48)
                dve.wait_ge(rt["te"], n + 1)
                for st in steps(dve, NT, 2, 2 * TURN, TURN):
                    if st.base % TURN == 0 and st.on(0, NT):
                        experts = experts_of(mybir.EngineType.DVE, st)
                    if st.on(1, NT):
                        j, r = st.item(1), st.slot(1, 2)
                        dve.wait_ge(f["w2"], j + 1)
                        dve.wait_ge(f["H"], 2 * (j + 1))
                        for k in range(FC // 2, FC):
                            dve.tensor_scalar(hT[r][:, k, :], bank[2 + r][:, k % 2 * P:(k % 2 + 1) * P], w2[r][:, F + k:F + k + 1], 0.0,
                                              ALU.add, ALU.max).then_inc(f["hV"], 1)
                    if st.on(2, NT):
                        j, r, g, o = st.item(2), st.slot(2, 2), st.slot(2, G_RING), st.slot(2, Y_RING)
                        dve.wait_ge(f["exp"], j + 1)
                        after(dve, f["y"], j)
                        dve.reciprocal(gate[:, :], lsum[o][:, :]).then_inc(f["v"], 1)
                        dve.wait_ge(f["Y"], j + 1)
                        dve.tensor_tensor(yb[:, :], bank[4 + r][:, 0:D], w2[r][:, F + FC:F + FC + D], ALU.add).then_inc(f["v"], 1)
                    if st.on(0, NT):
                        j, r, g = st.item(0), st.slot(0, 2), st.slot(0, G_RING)
                        dve.wait_ge(f["g"][g], 16 * (st.lap(0, G_RING) + 1))
                        after(dve, f["exp"], j - 1)
                        dve.tensor_reduce(lneg[r][:, :], xg[g][:, 2 * D:ROW], AX.X, ALU.max, negate=True).then_inc(f["neg"], 1)
                        after(dve, f["v"], 2 * (j - 1))
                        dve.tensor_copy(w2[r][:, :], WE[:, bass.ds(experts[st.base % TURN], 1), W2_AT:W_LEN
                                                        ].rearrange("p a w -> p (a w)")).then_inc(f["w2"], 1)
                    if st.on(2, NT):
                        j, g, o = st.item(2), st.slot(2, G_RING), st.slot(2, Y_RING)
                        dve.wait_ge(f["v"], 2 * (j + 1))
                        after(dve, f["s"][o], 16 * st.lap(2, Y_RING))
                        dve.scalar_tensor_tensor(yo[o][:, :], yb[:, :], gate[:, :], xg[g][:, D:2 * D],
                                                 ALU.mult, ALU.add).then_inc(f["y"], 1)

            route_vector(0)
            experts_vector(0)

            dve.wait_ge(ld_wb, 48)
            dve.tensor_scalar(bv_rep[:, :], ones, COL[:, 9:10], None, ALU.mult).then_inc(b_["bo"], 1)
            dve.wait_ge(b_["wvo"], 1)
            dve.tensor_tensor(bo_bc[:, :], bank[3][:, 0:D], bo_bc[:, :], ALU.add).then_inc(b_["bo"], 1)

            def stats_b(st, lag):
                b, r = st.item(lag), st.slot(lag, 2)
                alone(dve, b_["x"][r], 16 * C * (st.lap(lag, 2) + 1), passed["dve"])
                stats(b_, lambda c: xin[r][:, c, :], stat2, mv2, b, r, b_["xb"], b - 1)

            def normalise_b(b, r):
                after(dve, b_["T"], b - 1)
                normalise(b_, "xb", lambda c: xin[r][:, c, :], xb[r], mv2, rs2, b, r)

            stats_b(Step(0), 0)
            normalise_b(0, 0)
            scale = float(D) ** -0.5
            def inverse_sums(st):
                b, r = st.item(2), st.slot(2, 2)
                dve.wait_ge(b_["exp"], C * (b + 1))
                after(dve, b_["sc"], b)
                dve.reciprocal(pinv[:, :], psm[r][:, :]).then_inc(b_["pinv"], 1)

            def xf_b(st):
                b, r = st.item(3), st.slot(3, 2)
                after(dve, tails[1]["T"], b - 1)
                after(dve, tails[1]["store"][r], 32 * st.lap(3, 2))
                normalise(tails[1], "xf", lambda c: x3[r][:, c, :], xf[r], mv3, rs3, b, r)

            for st in steps(dve, B, 3, 6, 2, ahead=1):
                if st.on(-1, B) and not st.on(1, B):
                    stats_b(st, -1)
                if st.on(3, B):
                    p, q = st.item(3), st.slot(3, 2)
                    alone(dve, tails[1]["x"], p + 1, passed["dve"])
                    alone(dve, tails[1]["mv"], p, passed["dve"])
                    stats(tails[1], lambda c: x3[q][:, c, :], stat3, mv3, p, q, tails[1]["xf"], p - 1)
                if not st.on(1, B):
                    if st.on(2, B):
                        inverse_sums(st)
                    if st.on(3, B):
                        xf_b(st)
                if st.on(1, B):
                    b, r = st.item(1), st.slot(1, 2)
                    for c in range(C):
                        dve.wait_ge(b_["hs"], C * b + c + 1)
                        dve.scalar_tensor_tensor(wk[:, c, :], rel[r][:, c, 2, :], iw[r][:, c, 2:3], head_sum[r][:, c, :],
                                                 ALU.mult, ALU.add).then_inc(b_["s1"], 1)
                    for c in range(C):
                        dve.wait_ge(b_["s1"], C * b + c + 1)
                        dve.scalar_tensor_tensor(wk[:, c, :], rel[r][:, c, 3, :], iw[r][:, c, 3:4], wk[:, c, :],
                                                 ALU.mult, ALU.add).then_inc(b_["wk"], 1)
                    rounds = TOP_K // 8
                    for i in range(rounds):
                        for c in range(C):
                            if i == 0:
                                alone(dve, b_["wk"], C * b + c + 1, passed["dve"])
                            else:
                                alone(dve, b_["v"], 2 * C * (rounds * b + i - 1) + C + c + 1, passed["dve"])
                            dve.max(m8[:, c, :], wk[:, c, :]).then_inc(b_["v"], 1)
                        for c in range(C):
                            alone(dve, b_["v"], 2 * C * (rounds * b + i) + c + 1, passed["dve"])
                            dve.match_replace(wk[:, c, :], m8[:, c, :], wk[:, c, :], NEG).then_inc(b_["v"], 1)
                        if i == 0 and st.on(2, B):
                            inverse_sums(st)
                        if i == 2 and st.on(3, B):
                            xf_b(st)
                        if i == 2 and st.on(-1, B):
                            stats_b(st, -1)
                if st.on(-1, B):
                    normalise_b(st.item(-1), st.slot(-1, 2))
                if st.on(1, B):
                    for c in range(C):
                        dve.wait_ge(b_["v"], 2 * C * (rounds * (b + 1) - 1) + C + c + 1)
                        dve.tensor_scalar(pen[:, c, :], wk[:, c, :], -1.0e38, -1.0e30, ALU.is_gt, ALU.mult).then_inc(b_["fin"], 1)
                    for c in range(C):
                        alone(dve, b_["fin"], C * b + c + 1, passed["dve"])
                        alone(dve, b_["S"], C * (b + 1), passed["dve"])
                        alone(dve, b_["PT"], b - 1, passed["dve"])
                        dve.tensor_tensor_reduce(lg[r][:, c, :], bank[6][:, c * S:(c + 1) * S], pen[:, c, :], 1.0, -3.0e38,
                                                 ALU.add, ALU.max, lmax[:, c:c + 1]).then_inc(b_["ttr"], 1)
                    for c in range(C):
                        dve.wait_ge(b_["ttr"], C * b + c + 1)
                        dve.tensor_scalar(lnb[r][:, c:c + 1], lmax[:, c:c + 1], -scale, None, ALU.mult).then_inc(b_["lnb"], 1)
            route_vector(1)
            experts_vector(1)


def kernel(**inputs):
    import concourse.bacc as bacc
    from concourse.bass_utils import run_bass_kernel_spmd

    a = {k: np.asarray(v) for k, v in inputs.items()}

    def row(v):
        return np.ascontiguousarray(v).reshape(1, -1)

    w = a["L0_attn_a_w_qkv"]
    w_attn = np.concatenate([w[:, :D].T, w[:, D:2 * D], w[:, 2 * D:], a["L0_attn_a_w_out"]], axis=1)
    wt = a["L0_attn_b_w_qkv"].T
    other = np.r_[D // 2:D, 0:D // 2]
    wiq, wik = a["L0_attn_b_w_iq"].T, a["L0_attn_b_w_ik"].T
    wiw = np.zeros((D, D), np.float32)
    wiw[:, :IDX_HEADS] = a["L0_attn_b_w_iw"].T
    w_idx = np.concatenate([wiq, wik, wik, wt[:, :D], wt[:, :D][:, other], wt[:, D:2 * D], wt[:, D:2 * D][:, other],
                            a["L0_attn_b_w_o"].T, a["L0_attn_b_w_qkv"][2 * D:], wiw], axis=1)
    bq, bk, bv = np.split(a["L0_attn_b_b_qkv"], 3)
    biq, bik = a["L0_attn_b_b_iq"], a["L0_attn_b_b_ik"]
    cols = np.stack([a["L0_attn_a_gamma"].reshape(D), a["L0_attn_a_beta"].reshape(D), biq[:D], biq[D:],
                     np.concatenate([bik, bik]), bq, bq[other], bk, bk[other], bv], axis=1)
    w1 = a["L0_ffn_W1"].transpose(1, 0, 2)
    w2 = a["L0_ffn_W2"].reshape(E, FC, P, D).transpose(2, 0, 1, 3).reshape(P, E, F)
    arrays = {
        "x": a["L0_attn_a_x"].reshape(TOKENS, D),
        "w_attn": w_attn,
        "w_idx": w_idx,
        "w_experts": np.concatenate([w1, w2], axis=2),
        "b1_cols": a["L0_ffn_b1"].reshape(E, FC, P).transpose(2, 0, 1),
        "b2": a["L0_ffn_b2"],
        "w_router": a["L0_ffn_Wr"],
        "cols": cols,
        "b_out": a["L0_attn_a_b_out"],
        "b_o": a["L0_attn_b_b_o"],
        "b_iw": row(a["L0_attn_b_b_iw"]),
        "b_r": row(a["L0_ffn_br"]),
        "consts": constant_table(),
    }
    arrays = {k: np.ascontiguousarray(v) for k, v in arrays.items()}
    nc = bacc.Bacc("TRN2", target_bir_lowering=False, num_devices=1)
    aps = {k: nc.dram_tensor(k, v.shape, mybir.dt.from_np(v.dtype), kind="ExternalInput").ap() for k, v in arrays.items()}
    out = nc.dram_tensor("out", (TOKENS, D), F32, kind="ExternalOutput").ap()
    build(nc, **aps, out=out)
    r = run_bass_kernel_spmd(nc, [arrays], core_ids=[0])
    return r.results[0]["out"].reshape(B, S, D)
```
